# Optimizing a Trainium2 kernel written in Bass

```python
import numpy as np
import jax
import jax.numpy as jnp

def _softmax(x, axis=-1):
    return jax.nn.softmax(x, axis=axis)

def _gelu(x):
    return jax.nn.gelu(x, approximate=True)

def _silu(x):
    return jax.nn.silu(x)

def _sigmoid(x):
    return jax.nn.sigmoid(x)

def _layernorm(x, axis=-1, eps=1e-05):
    m = jnp.mean(x, axis=axis, keepdims=True)
    v = jnp.var(x, axis=axis, keepdims=True)
    return (x - m) / jnp.sqrt(v + eps)

def _scatter_add(tgt, idx, src, axis=0):
    return tgt.at[idx].add(src)

def _segment_sum(src, seg, n):
    return jax.ops.segment_sum(src, seg, n)
kernel_name = 'mk_gnn_ffn_d4_gnn_r8_33c211'

def setup_inputs(seed: int=0):
    np.random.seed(seed)
    _w = jnp.asarray

    def _rec_inputs():
        import jax
        import jax.numpy as jnp
        _gk = jax.random.key(seed)
        x = -0.001003 + 1 * jax.random.normal(jax.random.fold_in(_gk, 1), (256, 768), jnp.float32)
        _s = jax.random.randint(jax.random.fold_in(_gk, 2), (2048,), 0, 256, jnp.int32)
        _d = jax.random.randint(jax.random.fold_in(_gk, 3), (2048,), 0, 256, jnp.int32)
        _loop = jnp.arange(256, dtype=jnp.int32)
        src = jnp.concatenate([_s, _d, _loop])
        dst = jnp.concatenate([_d, _s, _loop])
        _o = jnp.argsort(dst, stable=True)
        src = src[_o]
        dst = dst[_o]
        edge_type_3 = jax.random.randint(jax.random.fold_in(_gk, 13), (4352,), 0, 3, jnp.int32)
        return (x, src, dst, edge_type_3)
    x, src, dst, edge_type_3 = _rec_inputs()

    def _L0_gnn_setup():
        import jax, jax.numpy as jnp
        import numpy as np
        NUM_RELATIONS = 3

        def _rgcn(x, W_rel, W_root, bias, src, dst, etype):
            n = x.shape[0]
            xr = jnp.einsum('ni,rio->rno', x, W_rel)
            msg = xr[etype, src]
            out = x @ W_root + bias
            for r in range(NUM_RELATIONS):
                m = etype == r
                s = jax.ops.segment_sum(jnp.where(m[:, None], msg, 0.0), dst, num_segments=n)
                c = jax.ops.segment_sum(m.astype(x.dtype), dst, num_segments=n)
                out = out + s / jnp.maximum(c, 1.0)[:, None]
            return out

        def _gate(h, q, Wg, bg, Wq, bq):
            B, L, F = q.shape
            N = h.shape[0] // B
            h3 = h.reshape(B, N, F)
            hg = jnp.einsum('bnf,gf->bng', h3, Wg[:, :F])
            qg = jnp.einsum('blf,gf->blg', q, Wg[:, F:]) + bg
            attn = jax.nn.sigmoid(hg[:, :, None, :] + qg[:, None, :, :])
            qi = jnp.einsum('bnlf,blf->bnf', attn, q)
            alpha = jax.nn.sigmoid(jnp.einsum('bnf,gf->bng', h3, Wq[:, :F]) + jnp.einsum('bnf,gf->bng', qi, Wq[:, F:]) + bq)
            hn = alpha * jnp.tanh(qi) + (1.0 - alpha) * h3
            return hn.reshape(B * N, F)
        key = jax.random.key(seed)
        ks = jax.random.split(key, 16)
        F = 768
        BN, E, B, L = (256, 8192, 8, 64)
        s = 0.02
        return {'x': jax.random.normal(ks[0], (BN, F), jnp.float32), 'edge_index': jax.random.randint(ks[1], (2, E), 0, BN), 'edge_type': jax.random.randint(ks[2], (E,), 0, NUM_RELATIONS), 'query_embs': jax.random.normal(ks[3], (B, L, F), jnp.float32), 'W_rel1': jax.random.normal(ks[4], (NUM_RELATIONS, F, F), jnp.float32) * s, 'W_root1': jax.random.normal(ks[5], (F, F), jnp.float32) * s, 'b1': jnp.zeros((F,), jnp.float32), 'W_rel2': jax.random.normal(ks[6], (NUM_RELATIONS, F, F), jnp.float32) * s, 'W_root2': jax.random.normal(ks[7], (F, F), jnp.float32) * s, 'b2': jnp.zeros((F,), jnp.float32), 'Wg': jax.random.normal(ks[8], (F, 2 * F), jnp.float32) * s, 'bg': jnp.zeros((F,), jnp.float32), 'Wq': jax.random.normal(ks[9], (F, 2 * F), jnp.float32) * s, 'bq': jnp.zeros((F,), jnp.float32)}
    _L0_gnn_all = _L0_gnn_setup()
    _L0_gnn_in = {k: v for k, v in _L0_gnn_all.items() if k in ('query_embs', 'W_rel1', 'W_root1', 'b1', 'W_rel2', 'W_root2', 'b2', 'Wg', 'bg', 'Wq', 'bq')}
    del _L0_gnn_all

    def _L0_ffn_setup():
        import jax, jax.numpy as jnp
        import numpy as np
        B, S, D = (4, 1024, 768)
        E = 8
        H = 768
        HS = 384
        TOPK_ROUTED = 2
        key = jax.random.key(seed)
        ks = jax.random.split(key, 10)
        w = lambda k, shape: jax.random.normal(k, shape, dtype=jnp.float32) * 0.02
        return {'x': jax.random.normal(ks[0], (B, S, D), dtype=jnp.float32), 'router_w': w(ks[1], (D, E)), 'w_gate': w(ks[2], (E, D, H)), 'w_up': w(ks[3], (E, D, H)), 'w_down': w(ks[4], (E, H, D)), 'ws_gate': w(ks[5], (D, HS)), 'ws_up': w(ks[6], (D, HS)), 'ws_down': w(ks[7], (HS, D)), 'sg_w': w(ks[8], (D, 1)), 'sg_b': jnp.zeros((1,), jnp.float32)}
    _L0_ffn_all = _L0_ffn_setup()
    _L0_ffn_in = {k: v for k, v in _L0_ffn_all.items() if k in ('router_w', 'w_gate', 'w_up', 'w_down', 'ws_gate', 'ws_up', 'ws_down', 'sg_w', 'sg_b')}
    del _L0_ffn_all

    def _L1_gnn_setup():
        import jax, jax.numpy as jnp
        import numpy as np
        N = 6250
        E = 31250
        H = 12
        D = 64
        NEG_SLOPE = 0.2
        key = jax.random.key(seed)
        k1, k2, k3, k4, k5, k6, k7 = jax.random.split(key, 7)
        h = jax.random.normal(k1, (N, H * D), dtype=jnp.float32)
        src = jnp.concatenate([jnp.arange(N, dtype=jnp.int32), jax.random.randint(k2, (E - N,), 0, N, dtype=jnp.int32)])
        dst = jnp.concatenate([jnp.arange(N, dtype=jnp.int32), jax.random.randint(k3, (E - N,), 0, N, dtype=jnp.int32)])
        xav = 1.414 / np.sqrt(D)
        W_fc = jax.random.normal(k4, (D, D), dtype=jnp.float32) * xav
        attn_l = jax.random.normal(k5, (H, D), dtype=jnp.float32) * 0.15
        attn_r = jax.random.normal(k6, (H, D), dtype=jnp.float32) * 0.15
        W_res = jax.random.normal(k7, (D, D), dtype=jnp.float32) * xav
        return {'h': h, 'W_fc': W_fc, 'attn_l': attn_l, 'attn_r': attn_r, 'W_res': W_res, 'src': src, 'dst': dst}
    _L1_gnn_all = _L1_gnn_setup()
    _L1_gnn_in = {k: v for k, v in _L1_gnn_all.items() if k in ('W_fc', 'attn_l', 'attn_r', 'W_res')}
    del _L1_gnn_all

    def _L1_ffn_setup():
        import jax, jax.numpy as jnp
        import numpy as np
        import math
        N_HEAD = 12
        N_EXP = 8
        TOP_K = 2
        EVAL_CAPACITY = 1.0
        MIN_CAPACITY = 4
        EPS = 1e-05

        def layer_norm(x, w):
            mu = jnp.mean(x, axis=-1, keepdims=True)
            var = jnp.var(x, axis=-1, keepdims=True)
            return (x - mu) / jnp.sqrt(var + EPS) * w

        def attention(x, c_attn_w, c_proj_w):
            B, T, C = x.shape
            H, D = (N_HEAD, C // N_HEAD)
            qkv = x @ c_attn_w.T
            q, k, v = jnp.split(qkv, 3, axis=-1)
            q = q.reshape(B, T, H, D).transpose(0, 2, 1, 3)
            k = k.reshape(B, T, H, D).transpose(0, 2, 1, 3)
            v = v.reshape(B, T, H, D).transpose(0, 2, 1, 3)
            scores = jnp.einsum('bhqd,bhkd->bhqk', q, k) * (1.0 / math.sqrt(D))
            causal = jnp.tril(jnp.ones((T, T), dtype=bool))
            scores = jnp.where(causal, scores, -jnp.inf)
            att = jax.nn.softmax(scores, axis=-1)
            y = jnp.einsum('bhqk,bhkd->bhqd', att, v)
            y = y.transpose(0, 2, 1, 3).reshape(B, T, C)
            return y @ c_proj_w.T

        def get_capacity(num_tokens):
            cap = int(math.floor(TOP_K * EVAL_CAPACITY * num_tokens / N_EXP))
            cap += cap % 2
            return max(cap, MIN_CAPACITY)

        def moe(x_flat, w_g, c_fc, c_proj_e):
            n_tok, C = x_flat.shape
            logits = x_flat @ w_g.T
            top_vals, top_idx = jax.lax.top_k(logits, TOP_K)
            rows = jnp.arange(n_tok)[:, None]
            masked = jnp.full_like(logits, -jnp.inf).at[rows, top_idx].set(top_vals)
            probs = jax.nn.softmax(masked, axis=-1)
            cap = get_capacity(n_tok)
            flat_e = top_idx.reshape(-1)
            onehot = jax.nn.one_hot(flat_e, N_EXP, dtype=jnp.int32)
            pos = jnp.cumsum(onehot, axis=0) - onehot
            slot = jnp.take_along_axis(pos, flat_e[:, None], axis=1)[:, 0]
            valid = slot < cap
            tok = jnp.repeat(jnp.arange(n_tok), TOP_K)
            slot_c = jnp.where(valid, slot, cap)
            sec = jnp.zeros((n_tok, N_EXP, cap + 1), dtype=x_flat.dtype)
            sec = sec.at[tok, flat_e, slot_c].set(1.0)[:, :, :cap]
            w_tok = probs[tok, flat_e]
            cb = jnp.zeros((n_tok, N_EXP, cap + 1), dtype=x_flat.dtype)
            cb = cb.at[tok, flat_e, slot_c].set(w_tok)[:, :, :cap]
            dispatched = jnp.einsum('tec,td->ecd', sec, x_flat)
            h = jax.nn.gelu(jnp.einsum('ecd,edh->ech', dispatched, c_fc), approximate=False)
            out = jnp.einsum('ech,ehd->ecd', h, c_proj_e)
            return jnp.einsum('tec,ecd->td', cb, out)
        key = jax.random.key(seed)
        ks = jax.random.split(key, 7)
        B, T, C = (2, 256, 768)
        std = 0.02
        return {'x': jax.random.normal(ks[0], (B, T, C), dtype=jnp.float32), 'ln1_w': jnp.ones((C,), dtype=jnp.float32), 'ln2_w': jnp.ones((C,), dtype=jnp.float32), 'c_attn_w': jax.random.normal(ks[1], (3 * C, C), dtype=jnp.float32) * std, 'c_proj_w': jax.random.normal(ks[2], (C, C), dtype=jnp.float32) * std, 'w_g': jax.random.normal(ks[3], (N_EXP, C), dtype=jnp.float32) * std, 'c_fc': jax.random.normal(ks[4], (N_EXP, C, 4 * C), dtype=jnp.float32) * std, 'c_proj_e': jax.random.normal(ks[5], (N_EXP, 4 * C, C), dtype=jnp.float32) * std}
    _L1_ffn_all = _L1_ffn_setup()
    _L1_ffn_in = {k: v for k, v in _L1_ffn_all.items() if k in ('ln1_w', 'ln2_w', 'c_attn_w', 'c_proj_w', 'w_g', 'c_fc', 'c_proj_e')}
    del _L1_ffn_all

    def _L2_gnn_setup():
        import jax, jax.numpy as jnp
        import numpy as np
        NEG_SLOPE = 0.2
        EPS = 1e-16
        N_NODES = 4096
        N_EDGES = 20000
        DIM = 768
        HEADS1 = 4
        OUT1 = DIM // HEADS1
        HEADS2 = 1
        OUT2 = DIM
        N_REL = 3

        def rgat_conv(x, W, q, k, b, src, dst, etype, heads, out_ch, n_nodes):
            xr = jnp.einsum('nd,rdf->rnf', x, W)
            oi = xr[etype, dst]
            oj = xr[etype, src]
            qi = oi @ q
            kj = oj @ k
            alpha = jax.nn.leaky_relu(qi + kj, NEG_SLOPE)
            m = jax.ops.segment_max(alpha, dst, num_segments=n_nodes)
            e = jnp.exp(alpha - m[dst])
            z = jax.ops.segment_sum(e, dst, num_segments=n_nodes)
            a = e / (z[dst] + EPS)
            msg = (a[:, :, None] * oj.reshape(-1, heads, out_ch)).reshape(-1, heads * out_ch)
            out = jax.ops.segment_sum(msg, dst, num_segments=n_nodes)
            return out + b
        key = jax.random.key(seed)
        ks = jax.random.split(key, 12)
        s = 0.02
        return {'x': jax.random.normal(ks[0], (N_NODES, DIM), dtype=jnp.float32), 'edge_index': jax.random.randint(ks[1], (2, N_EDGES), 0, N_NODES, dtype=jnp.int64), 'edge_type': jax.random.randint(ks[2], (N_EDGES,), 0, N_REL, dtype=jnp.int64), 'W1': jax.random.normal(ks[3], (N_REL, DIM, HEADS1 * OUT1), dtype=jnp.float32) * s, 'q1': jax.random.normal(ks[4], (HEADS1 * OUT1, HEADS1), dtype=jnp.float32) * s, 'k1': jax.random.normal(ks[5], (HEADS1 * OUT1, HEADS1), dtype=jnp.float32) * s, 'b1': jnp.zeros((HEADS1 * OUT1,), dtype=jnp.float32), 'W2': jax.random.normal(ks[6], (N_REL, DIM, HEADS2 * OUT2), dtype=jnp.float32) * s, 'q2': jax.random.normal(ks[7], (HEADS2 * OUT2, HEADS2), dtype=jnp.float32) * s, 'k2': jax.random.normal(ks[8], (HEADS2 * OUT2, HEADS2), dtype=jnp.float32) * s, 'b2': jnp.zeros((HEADS2 * OUT2,), dtype=jnp.float32)}
    _L2_gnn_all = _L2_gnn_setup()
    _L2_gnn_in = {k: v for k, v in _L2_gnn_all.items() if k in ('W1', 'q1', 'k1', 'b1', 'W2', 'q2', 'k2', 'b2')}
    del _L2_gnn_all

    def _L2_ffn_setup():
        import jax, jax.numpy as jnp
        import numpy as np
        CAPACITY_FACTOR = 1.25
        key = jax.random.key(seed)
        ks = jax.random.split(key, 5)
        B, S, D, F, E = (8, 256, 768, 384, 8)
        return {'x': jax.random.normal(ks[0], (B, S, D), jnp.float32), 'switch_w': jax.random.normal(ks[1], (D, E), jnp.float32) * 0.02, 'switch_b': jnp.zeros((E,), jnp.float32), 'w1': jax.random.normal(ks[2], (E, D, F), jnp.float32) * 0.02, 'b1': jnp.zeros((E, F), jnp.float32), 'w2': jax.random.normal(ks[3], (E, F, D), jnp.float32) * 0.02, 'b2': jnp.zeros((E, D), jnp.float32)}
    _L2_ffn_all = _L2_ffn_setup()
    _L2_ffn_in = {k: v for k, v in _L2_ffn_all.items() if k in ('switch_w', 'switch_b', 'w1', 'b1', 'w2', 'b2')}
    del _L2_ffn_all

    def _L3_gnn_setup():
        import jax, jax.numpy as jnp
        import numpy as np
        N_NODES = 1250
        key = jax.random.key(seed)
        k1, k2, k3 = jax.random.split(key, 3)
        x = jax.random.normal(k1, (N_NODES, 768), dtype=jnp.float32)
        edge_index = jax.random.randint(k2, (2, 12500), 0, N_NODES, dtype=jnp.int32)
        W = jax.random.normal(k3, (768, 768), dtype=jnp.float32) * (1.0 / np.sqrt(768))
        b = jnp.zeros((768,), dtype=jnp.float32)
        return {'x': x, 'edge_index': edge_index, 'W': W, 'b': b}
    _L3_gnn_all = _L3_gnn_setup()
    _L3_gnn_in = {k: v for k, v in _L3_gnn_all.items() if k in ('W', 'b')}
    del _L3_gnn_all

    def _L3_ffn_setup():
        import jax, jax.numpy as jnp
        import numpy as np
        B, S, H = (4, 1024, 768)
        NH, HD = (12, 64)
        E, K, F = (8, 2, 384)
        SF = 768
        EPS = 1e-06

        def rmsnorm(x, w):
            xf = x.astype(jnp.float32)
            var = jnp.mean(xf * xf, axis=-1, keepdims=True)
            return w * (xf * jax.lax.rsqrt(var + EPS)).astype(x.dtype)
        key = jax.random.key(seed)
        ks = jax.random.split(key, 16)
        sc = 0.02
        return {'hidden_states': jax.random.normal(ks[0], (B, S, H), jnp.float32), 'norm1_w': jnp.ones((H,), jnp.float32), 'Wq': jax.random.normal(ks[1], (H, H), jnp.float32) * sc, 'Wk': jax.random.normal(ks[2], (H, H), jnp.float32) * sc, 'Wv': jax.random.normal(ks[3], (H, H), jnp.float32) * sc, 'Wo': jax.random.normal(ks[4], (H, H), jnp.float32) * sc, 'norm2_w': jnp.ones((H,), jnp.float32), 'gate_w': jax.random.normal(ks[5], (E, H), jnp.float32) * sc, 'Weg': jax.random.normal(ks[6], (E, F, H), jnp.float32) * sc, 'Weu': jax.random.normal(ks[7], (E, F, H), jnp.float32) * sc, 'Wed': jax.random.normal(ks[8], (E, H, F), jnp.float32) * sc, 'Wsg': jax.random.normal(ks[9], (SF, H), jnp.float32) * sc, 'Wsu': jax.random.normal(ks[10], (SF, H), jnp.float32) * sc, 'Wsd': jax.random.normal(ks[11], (H, SF), jnp.float32) * sc}
    _L3_ffn_all = _L3_ffn_setup()
    _L3_ffn_in = {k: v for k, v in _L3_ffn_all.items() if k in ('norm1_w', 'Wq', 'Wk', 'Wv', 'Wo', 'norm2_w', 'gate_w', 'Weg', 'Weu', 'Wed', 'Wsg', 'Wsu', 'Wsd')}
    del _L3_ffn_all
    return {'x': x, 'src': src, 'dst': dst, 'edge_type_3': edge_type_3, 'L0_gnn_query_embs': _L0_gnn_in['query_embs'], 'L0_gnn_W_rel1': _L0_gnn_in['W_rel1'], 'L0_gnn_W_root1': _L0_gnn_in['W_root1'], 'L0_gnn_b1': _L0_gnn_in['b1'], 'L0_gnn_W_rel2': _L0_gnn_in['W_rel2'], 'L0_gnn_W_root2': _L0_gnn_in['W_root2'], 'L0_gnn_b2': _L0_gnn_in['b2'], 'L0_gnn_Wg': _L0_gnn_in['Wg'], 'L0_gnn_bg': _L0_gnn_in['bg'], 'L0_gnn_Wq': _L0_gnn_in['Wq'], 'L0_gnn_bq': _L0_gnn_in['bq'], 'L0_ffn_router_w': _L0_ffn_in['router_w'], 'L0_ffn_w_gate': _L0_ffn_in['w_gate'], 'L0_ffn_w_up': _L0_ffn_in['w_up'], 'L0_ffn_w_down': _L0_ffn_in['w_down'], 'L0_ffn_ws_gate': _L0_ffn_in['ws_gate'], 'L0_ffn_ws_up': _L0_ffn_in['ws_up'], 'L0_ffn_ws_down': _L0_ffn_in['ws_down'], 'L0_ffn_sg_w': _L0_ffn_in['sg_w'], 'L0_ffn_sg_b': _L0_ffn_in['sg_b'], 'L1_gnn_W_fc': _L1_gnn_in['W_fc'], 'L1_gnn_attn_l': _L1_gnn_in['attn_l'], 'L1_gnn_attn_r': _L1_gnn_in['attn_r'], 'L1_gnn_W_res': _L1_gnn_in['W_res'], 'L1_ffn_ln1_w': _L1_ffn_in['ln1_w'], 'L1_ffn_ln2_w': _L1_ffn_in['ln2_w'], 'L1_ffn_c_attn_w': _L1_ffn_in['c_attn_w'], 'L1_ffn_c_proj_w': _L1_ffn_in['c_proj_w'], 'L1_ffn_w_g': _L1_ffn_in['w_g'], 'L1_ffn_c_fc': _L1_ffn_in['c_fc'], 'L1_ffn_c_proj_e': _L1_ffn_in['c_proj_e'], 'L2_gnn_W1': _L2_gnn_in['W1'], 'L2_gnn_q1': _L2_gnn_in['q1'], 'L2_gnn_k1': _L2_gnn_in['k1'], 'L2_gnn_b1': _L2_gnn_in['b1'], 'L2_gnn_W2': _L2_gnn_in['W2'], 'L2_gnn_q2': _L2_gnn_in['q2'], 'L2_gnn_k2': _L2_gnn_in['k2'], 'L2_gnn_b2': _L2_gnn_in['b2'], 'L2_ffn_switch_w': _L2_ffn_in['switch_w'], 'L2_ffn_switch_b': _L2_ffn_in['switch_b'], 'L2_ffn_w1': _L2_ffn_in['w1'], 'L2_ffn_b1': _L2_ffn_in['b1'], 'L2_ffn_w2': _L2_ffn_in['w2'], 'L2_ffn_b2': _L2_ffn_in['b2'], 'L3_gnn_W': _L3_gnn_in['W'], 'L3_gnn_b': _L3_gnn_in['b'], 'L3_ffn_norm1_w': _L3_ffn_in['norm1_w'], 'L3_ffn_Wq': _L3_ffn_in['Wq'], 'L3_ffn_Wk': _L3_ffn_in['Wk'], 'L3_ffn_Wv': _L3_ffn_in['Wv'], 'L3_ffn_Wo': _L3_ffn_in['Wo'], 'L3_ffn_norm2_w': _L3_ffn_in['norm2_w'], 'L3_ffn_gate_w': _L3_ffn_in['gate_w'], 'L3_ffn_Weg': _L3_ffn_in['Weg'], 'L3_ffn_Weu': _L3_ffn_in['Weu'], 'L3_ffn_Wed': _L3_ffn_in['Wed'], 'L3_ffn_Wsg': _L3_ffn_in['Wsg'], 'L3_ffn_Wsu': _L3_ffn_in['Wsu'], 'L3_ffn_Wsd': _L3_ffn_in['Wsd']}

def reference(x, src, dst, edge_type_3, L0_gnn_query_embs, L0_gnn_W_rel1, L0_gnn_W_root1, L0_gnn_b1, L0_gnn_W_rel2, L0_gnn_W_root2, L0_gnn_b2, L0_gnn_Wg, L0_gnn_bg, L0_gnn_Wq, L0_gnn_bq, L0_ffn_router_w, L0_ffn_w_gate, L0_ffn_w_up, L0_ffn_w_down, L0_ffn_ws_gate, L0_ffn_ws_up, L0_ffn_ws_down, L0_ffn_sg_w, L0_ffn_sg_b, L1_gnn_W_fc, L1_gnn_attn_l, L1_gnn_attn_r, L1_gnn_W_res, L1_ffn_ln1_w, L1_ffn_ln2_w, L1_ffn_c_attn_w, L1_ffn_c_proj_w, L1_ffn_w_g, L1_ffn_c_fc, L1_ffn_c_proj_e, L2_gnn_W1, L2_gnn_q1, L2_gnn_k1, L2_gnn_b1, L2_gnn_W2, L2_gnn_q2, L2_gnn_k2, L2_gnn_b2, L2_ffn_switch_w, L2_ffn_switch_b, L2_ffn_w1, L2_ffn_b1, L2_ffn_w2, L2_ffn_b2, L3_gnn_W, L3_gnn_b, L3_ffn_norm1_w, L3_ffn_Wq, L3_ffn_Wk, L3_ffn_Wv, L3_ffn_Wo, L3_ffn_norm2_w, L3_ffn_gate_w, L3_ffn_Weg, L3_ffn_Weu, L3_ffn_Wed, L3_ffn_Wsg, L3_ffn_Wsu, L3_ffn_Wsd):
    import jax
    import jax.numpy as jnp

    def _L0_gnn_ref(x, edge_index, edge_type, query_embs, W_rel1, W_root1, b1, W_rel2, W_root2, b2, Wg, bg, Wq, bq):
        import jax, jax.numpy as jnp
        import numpy as np
        NUM_RELATIONS = 3

        def _rgcn(x, W_rel, W_root, bias, src, dst, etype):
            n = x.shape[0]
            xr = jnp.einsum('ni,rio->rno', x, W_rel)
            msg = xr[etype, src]
            out = x @ W_root + bias
            for r in range(NUM_RELATIONS):
                m = etype == r
                s = jax.ops.segment_sum(jnp.where(m[:, None], msg, 0.0), dst, num_segments=n)
                c = jax.ops.segment_sum(m.astype(x.dtype), dst, num_segments=n)
                out = out + s / jnp.maximum(c, 1.0)[:, None]
            return out

        def _gate(h, q, Wg, bg, Wq, bq):
            B, L, F = q.shape
            N = h.shape[0] // B
            h3 = h.reshape(B, N, F)
            hg = jnp.einsum('bnf,gf->bng', h3, Wg[:, :F])
            qg = jnp.einsum('blf,gf->blg', q, Wg[:, F:]) + bg
            attn = jax.nn.sigmoid(hg[:, :, None, :] + qg[:, None, :, :])
            qi = jnp.einsum('bnlf,blf->bnf', attn, q)
            alpha = jax.nn.sigmoid(jnp.einsum('bnf,gf->bng', h3, Wq[:, :F]) + jnp.einsum('bnf,gf->bng', qi, Wq[:, F:]) + bq)
            hn = alpha * jnp.tanh(qi) + (1.0 - alpha) * h3
            return hn.reshape(B * N, F)
        src, dst = (edge_index[0], edge_index[1])
        h = jax.nn.relu(_rgcn(x, W_rel1, W_root1, b1, src, dst, edge_type))
        h = _gate(h, query_embs, Wg, bg, Wq, bq)
        h = jax.nn.relu(_rgcn(h, W_rel2, W_root2, b2, src, dst, edge_type))
        h = _gate(h, query_embs, Wg, bg, Wq, bq)
        return h

    def _L0_ffn_ref(x, router_w, w_gate, w_up, w_down, ws_gate, ws_up, ws_down, sg_w, sg_b):
        import jax, jax.numpy as jnp
        import numpy as np
        B, S, D = (4, 1024, 768)
        E = 8
        H = 768
        HS = 384
        TOPK_ROUTED = 2
        probs = jax.nn.softmax(x @ router_w, axis=-1)
        gates, idx = jax.lax.top_k(probs, TOPK_ROUTED)
        gates = gates / jnp.sum(gates, axis=-1, keepdims=True)
        n_exp = router_w.shape[1]
        dense_g = jnp.sum(jax.nn.one_hot(idx, n_exp, dtype=x.dtype) * gates[..., None], axis=-2)
        g = jax.nn.silu(jnp.einsum('bsd,edh->bseh', x, w_gate))
        u = jnp.einsum('bsd,edh->bseh', x, w_up)
        expert_out = jnp.einsum('bseh,ehd->bsed', g * u, w_down)
        routed = jnp.einsum('bse,bsed->bsd', dense_g, expert_out)
        shared = jax.nn.silu(x @ ws_gate) * (x @ ws_up) @ ws_down
        alpha = jax.nn.sigmoid(x @ sg_w + sg_b)
        return alpha * shared + (1.0 - alpha) * routed

    def _L1_gnn_ref(h, W_fc, attn_l, attn_r, W_res, src, dst):
        import jax, jax.numpy as jnp
        import numpy as np
        N = 6250
        E = 31250
        H = 12
        D = 64
        NEG_SLOPE = 0.2
        n = h.shape[0]
        hh = h.reshape(n, H, D)
        ft = jnp.einsum('nhd,ed->nhe', hh, W_fc)
        a1 = jnp.einsum('nhd,hd->nh', ft, attn_l)
        a2 = jnp.einsum('nhd,hd->nh', ft, attn_r)
        e = jax.nn.leaky_relu(a1[src] + a2[dst], negative_slope=NEG_SLOPE)
        m = jax.ops.segment_max(e, dst, num_segments=n)
        ee = jnp.exp(e - m[dst])
        denom = jax.ops.segment_sum(ee, dst, num_segments=n)
        alpha = ee / denom[dst]
        agg = jax.ops.segment_sum(alpha[:, :, None] * ft[src], dst, num_segments=n)
        res = jnp.einsum('nhd,ed->nhe', hh, W_res)
        return jax.nn.relu((res + agg).reshape(n, H * D))

    def _L1_ffn_ref(x, ln1_w, ln2_w, c_attn_w, c_proj_w, w_g, c_fc, c_proj_e):
        import jax, jax.numpy as jnp
        import numpy as np
        import math
        N_HEAD = 12
        N_EXP = 8
        TOP_K = 2
        EVAL_CAPACITY = 1.0
        MIN_CAPACITY = 4
        EPS = 1e-05

        def layer_norm(x, w):
            mu = jnp.mean(x, axis=-1, keepdims=True)
            var = jnp.var(x, axis=-1, keepdims=True)
            return (x - mu) / jnp.sqrt(var + EPS) * w

        def attention(x, c_attn_w, c_proj_w):
            B, T, C = x.shape
            H, D = (N_HEAD, C // N_HEAD)
            qkv = x @ c_attn_w.T
            q, k, v = jnp.split(qkv, 3, axis=-1)
            q = q.reshape(B, T, H, D).transpose(0, 2, 1, 3)
            k = k.reshape(B, T, H, D).transpose(0, 2, 1, 3)
            v = v.reshape(B, T, H, D).transpose(0, 2, 1, 3)
            scores = jnp.einsum('bhqd,bhkd->bhqk', q, k) * (1.0 / math.sqrt(D))
            causal = jnp.tril(jnp.ones((T, T), dtype=bool))
            scores = jnp.where(causal, scores, -jnp.inf)
            att = jax.nn.softmax(scores, axis=-1)
            y = jnp.einsum('bhqk,bhkd->bhqd', att, v)
            y = y.transpose(0, 2, 1, 3).reshape(B, T, C)
            return y @ c_proj_w.T

        def get_capacity(num_tokens):
            cap = int(math.floor(TOP_K * EVAL_CAPACITY * num_tokens / N_EXP))
            cap += cap % 2
            return max(cap, MIN_CAPACITY)

        def moe(x_flat, w_g, c_fc, c_proj_e):
            n_tok, C = x_flat.shape
            logits = x_flat @ w_g.T
            top_vals, top_idx = jax.lax.top_k(logits, TOP_K)
            rows = jnp.arange(n_tok)[:, None]
            masked = jnp.full_like(logits, -jnp.inf).at[rows, top_idx].set(top_vals)
            probs = jax.nn.softmax(masked, axis=-1)
            cap = get_capacity(n_tok)
            flat_e = top_idx.reshape(-1)
            onehot = jax.nn.one_hot(flat_e, N_EXP, dtype=jnp.int32)
            pos = jnp.cumsum(onehot, axis=0) - onehot
            slot = jnp.take_along_axis(pos, flat_e[:, None], axis=1)[:, 0]
            valid = slot < cap
            tok = jnp.repeat(jnp.arange(n_tok), TOP_K)
            slot_c = jnp.where(valid, slot, cap)
            sec = jnp.zeros((n_tok, N_EXP, cap + 1), dtype=x_flat.dtype)
            sec = sec.at[tok, flat_e, slot_c].set(1.0)[:, :, :cap]
            w_tok = probs[tok, flat_e]
            cb = jnp.zeros((n_tok, N_EXP, cap + 1), dtype=x_flat.dtype)
            cb = cb.at[tok, flat_e, slot_c].set(w_tok)[:, :, :cap]
            dispatched = jnp.einsum('tec,td->ecd', sec, x_flat)
            h = jax.nn.gelu(jnp.einsum('ecd,edh->ech', dispatched, c_fc), approximate=False)
            out = jnp.einsum('ech,ehd->ecd', h, c_proj_e)
            return jnp.einsum('tec,ecd->td', cb, out)
        x = x + attention(layer_norm(x, ln1_w), c_attn_w, c_proj_w)
        B, T, C = x.shape
        x_ln = layer_norm(x, ln2_w)
        moe_out = moe(x_ln.reshape(B * T, C), w_g, c_fc, c_proj_e)
        return x + moe_out.reshape(B, T, C)

    def _L2_gnn_ref(x, edge_index, edge_type, W1, q1, k1, b1, W2, q2, k2, b2):
        import jax, jax.numpy as jnp
        import numpy as np
        NEG_SLOPE = 0.2
        EPS = 1e-16
        N_NODES = 4096
        N_EDGES = 20000
        DIM = 768
        HEADS1 = 4
        OUT1 = DIM // HEADS1
        HEADS2 = 1
        OUT2 = DIM
        N_REL = 3

        def rgat_conv(x, W, q, k, b, src, dst, etype, heads, out_ch, n_nodes):
            xr = jnp.einsum('nd,rdf->rnf', x, W)
            oi = xr[etype, dst]
            oj = xr[etype, src]
            qi = oi @ q
            kj = oj @ k
            alpha = jax.nn.leaky_relu(qi + kj, NEG_SLOPE)
            m = jax.ops.segment_max(alpha, dst, num_segments=n_nodes)
            e = jnp.exp(alpha - m[dst])
            z = jax.ops.segment_sum(e, dst, num_segments=n_nodes)
            a = e / (z[dst] + EPS)
            msg = (a[:, :, None] * oj.reshape(-1, heads, out_ch)).reshape(-1, heads * out_ch)
            out = jax.ops.segment_sum(msg, dst, num_segments=n_nodes)
            return out + b
        src, dst = (edge_index[0], edge_index[1])
        n = x.shape[0]
        h = rgat_conv(x, W1, q1, k1, b1, src, dst, edge_type, HEADS1, OUT1, n)
        h = jax.nn.elu(h)
        out = rgat_conv(h, W2, q2, k2, b2, src, dst, edge_type, HEADS2, OUT2, n)
        return out

    def _L2_ffn_ref(x, switch_w, switch_b, w1, b1, w2, b2):
        import jax, jax.numpy as jnp
        import numpy as np
        CAPACITY_FACTOR = 1.25
        B, S, D = x.shape
        E = w1.shape[0]
        xf = x.reshape(-1, D)
        N = xf.shape[0]
        capacity = int(CAPACITY_FACTOR * N / E)
        probs = jax.nn.softmax(xf @ switch_w + switch_b, axis=-1)
        prob_max = jnp.max(probs, axis=-1)
        routes = jnp.argmax(probs, axis=-1)
        sort_idx = jnp.lexsort((-prob_max, routes))
        counts = jnp.bincount(routes, length=E)
        starts = jnp.concatenate([jnp.zeros((1,), counts.dtype), jnp.cumsum(counts)[:-1]])
        rank_sorted = jnp.arange(N) - starts[routes[sort_idx]]
        rank = jnp.zeros((N,), jnp.int32).at[sort_idx].set(rank_sorted.astype(jnp.int32))
        keep = rank < capacity
        dest_e = jnp.where(keep, routes, E)
        dest_c = jnp.where(keep, rank, 0)
        buf = jnp.zeros((E + 1, capacity, D), xf.dtype).at[dest_e, dest_c].set(xf)
        h = jax.nn.gelu(jnp.einsum('ecd,edf->ecf', buf[:E], w1) + b1[:, None, :], approximate=False)
        o = jnp.einsum('ecf,efd->ecd', h, w2) + b2[:, None, :]
        y_exp = o[routes, dest_c]
        y = jnp.where(keep[:, None], y_exp, xf)
        out = y * prob_max[:, None]
        return out.reshape(B, S, D)

    def _L3_gnn_ref(x, edge_index, W, b):
        import jax, jax.numpy as jnp
        import numpy as np
        N_NODES = 1250
        n = x.shape[0]
        loops = jnp.arange(n, dtype=edge_index.dtype)
        row = jnp.concatenate([edge_index[0], loops])
        col = jnp.concatenate([edge_index[1], loops])
        ones = jnp.ones(row.shape[0], dtype=x.dtype)
        deg = jax.ops.segment_sum(ones, col, num_segments=n)
        dinv = jnp.where(deg > 0, jax.lax.rsqrt(deg), 0.0)
        norm = dinv[row] * dinv[col]
        h = x @ W
        msg = h[row] * norm[:, None]
        out = jax.ops.segment_sum(msg, col, num_segments=n) + b
        return out

    def _L3_ffn_ref(hidden_states, norm1_w, Wq, Wk, Wv, Wo, norm2_w, gate_w, Weg, Weu, Wed, Wsg, Wsu, Wsd):
        import jax, jax.numpy as jnp
        import numpy as np
        B, S, H = (4, 1024, 768)
        NH, HD = (12, 64)
        E, K, F = (8, 2, 384)
        SF = 768
        EPS = 1e-06

        def rmsnorm(x, w):
            xf = x.astype(jnp.float32)
            var = jnp.mean(xf * xf, axis=-1, keepdims=True)
            return w * (xf * jax.lax.rsqrt(var + EPS)).astype(x.dtype)
        b, s, h = hidden_states.shape
        res = hidden_states
        x = rmsnorm(hidden_states, norm1_w)

        def heads(t):
            return t.reshape(b, s, NH, HD).transpose(0, 2, 1, 3)
        q, k, v = (heads(x @ Wq.T), heads(x @ Wk.T), heads(x @ Wv.T))
        scores = jnp.einsum('bhqd,bhkd->bhqk', q, k) / np.float32(np.sqrt(HD))
        attn = jax.nn.softmax(scores, axis=-1)
        ctx = jnp.einsum('bhqk,bhkd->bhqd', attn, v)
        ctx = ctx.transpose(0, 2, 1, 3).reshape(b, s, h)
        x = res + ctx @ Wo.T
        res2 = x
        xn = rmsnorm(x, norm2_w)
        t = xn.reshape(-1, h)
        gate_scores = jax.nn.softmax(t @ gate_w.T, axis=-1)
        topk_w, topk_idx = jax.lax.top_k(gate_scores, K)
        topk_w = topk_w / (topk_w.sum(-1, keepdims=True) + 1e-20)
        combine = (jax.nn.one_hot(topk_idx, E, dtype=t.dtype) * topk_w[..., None]).sum(1)
        g = jnp.einsum('td,efd->tef', t, Weg)
        u = jnp.einsum('td,efd->tef', t, Weu)
        act = jax.nn.silu(g) * u
        y_routed = jnp.einsum('tef,edf,te->td', act, Wed, combine)
        y_shared = jax.nn.silu(t @ Wsg.T) * (t @ Wsu.T) @ Wsd.T
        y = (y_routed + y_shared).reshape(b, s, h)
        return res2 + y
    edge_index = jnp.stack([src, dst])
    x = x + _L0_gnn_ref(_layernorm(x, axis=-1), edge_index, edge_type_3, L0_gnn_query_embs, L0_gnn_W_rel1, L0_gnn_W_root1, L0_gnn_b1, L0_gnn_W_rel2, L0_gnn_W_root2, L0_gnn_b2, L0_gnn_Wg, L0_gnn_bg, L0_gnn_Wq, L0_gnn_bq)
    x = x + _L0_ffn_ref(_layernorm(x, axis=-1)[None], L0_ffn_router_w, L0_ffn_w_gate, L0_ffn_w_up, L0_ffn_w_down, L0_ffn_ws_gate, L0_ffn_ws_up, L0_ffn_ws_down, L0_ffn_sg_w, L0_ffn_sg_b)[0]
    x = x + _L1_gnn_ref(_layernorm(x, axis=-1), L1_gnn_W_fc, L1_gnn_attn_l, L1_gnn_attn_r, L1_gnn_W_res, src, dst)
    x = x + _L1_ffn_ref(_layernorm(x, axis=-1)[None], L1_ffn_ln1_w, L1_ffn_ln2_w, L1_ffn_c_attn_w, L1_ffn_c_proj_w, L1_ffn_w_g, L1_ffn_c_fc, L1_ffn_c_proj_e)[0]
    x = x + _L2_gnn_ref(_layernorm(x, axis=-1), edge_index, edge_type_3, L2_gnn_W1, L2_gnn_q1, L2_gnn_k1, L2_gnn_b1, L2_gnn_W2, L2_gnn_q2, L2_gnn_k2, L2_gnn_b2)
    x = x + _L2_ffn_ref(_layernorm(x, axis=-1)[None], L2_ffn_switch_w, L2_ffn_switch_b, L2_ffn_w1, L2_ffn_b1, L2_ffn_w2, L2_ffn_b2)[0]
    x = x + _L3_gnn_ref(_layernorm(x, axis=-1), edge_index, L3_gnn_W, L3_gnn_b)
    x = x + _L3_ffn_ref(_layernorm(x, axis=-1)[None], L3_ffn_norm1_w, L3_ffn_Wq, L3_ffn_Wk, L3_ffn_Wv, L3_ffn_Wo, L3_ffn_norm2_w, L3_ffn_gate_w, L3_ffn_Weg, L3_ffn_Weu, L3_ffn_Wed, L3_ffn_Wsg, L3_ffn_Wsu, L3_ffn_Wsd)[0]
    return x

_drawn_inputs = setup_inputs


def setup_inputs(seed=0):
    import zlib

    import numpy as np

    out = dict(_drawn_inputs(seed))
    spreads = {'L0_gnn_b1': (0.0, 0.324),
     'L0_gnn_b2': (0.0, 0.1),
     'L0_gnn_bg': (0.0, 0.282),
     'L0_gnn_bq': (0.0, 0.39),
     'L1_ffn_ln1_w': (1.0, 0.6),
     'L1_ffn_ln2_w': (1.0, 0.2),
     'L2_gnn_b1': (0.0, 0.576),
     'L2_gnn_b2': (0.0, 0.1),
     'L2_ffn_switch_b': (0.0, 0.668),
     'L2_ffn_b1': (0.0, 0.8),
     'L2_ffn_b2': (0.0, 0.796),
     'L3_gnn_b': (0.0, 0.1),
     'L3_ffn_norm1_w': (1.0, 0.6),
     'L3_ffn_norm2_w': (1.0, 0.6)}
    factors = {'L0_ffn_sg_w': 3.723,
     'L2_gnn_W1': 4.466,
     'L2_gnn_q1': 8.0,
     'L2_gnn_k1': 8.0,
     'L2_gnn_W2': 2.959,
     'L2_gnn_q2': 8.0,
     'L2_gnn_k2': 8.0,
     'L2_ffn_w1': 4.723,
     'L2_ffn_w2': 4.404,
     'L3_ffn_Wq': 8.0,
     'L3_ffn_Wk': 8.0,
     'L3_ffn_gate_w': 4.471,
     'L3_ffn_Weg': 3.991,
     'L3_ffn_Weu': 3.858,
     'L3_ffn_Wed': 3.837,
     'L3_ffn_Wsg': 3.059,
     'L3_ffn_Wsu': 2.894,
     'L3_ffn_Wsd': 2.908}
    for name, (base, spread) in spreads.items():
        noise = np.random.default_rng([zlib.crc32(name.encode()), seed]).standard_normal(out[name].shape)
        drawn = base * np.exp(spread * noise) if base else spread * noise
        out[name] = jnp.asarray(drawn.astype(out[name].dtype))
    for name, factor in factors.items():
        out[name] = (out[name] * factor).astype(out[name].dtype)
    return out
```

```python
import math
from contextlib import ExitStack

import numpy as np
import concourse.bass as bass
from concourse import mybir

F32 = mybir.dt.float32
BF16 = mybir.dt.bfloat16
I32 = mybir.dt.int32
ALU = mybir.AluOpType
ACT = mybir.ActivationFunctionType
AX = mybir.AxisListType

P = 128
T = 256
TC = T // P
D = 768
DC = D // P
HALF = D // 2
NREL = 3
NEDGE = 4352
EC = NEDGE // P
HEADS, HD = 12, 64
RH = 4
QB, QL, QN = 8, 64, T // 8
NEXP = 8
SLOT = 64
CAP1 = 64
CAP2 = int(1.25 * T / NEXP)
WCOLS = DC * D
NSLOT = 5
NEG = -1.0e30


class Tok:
    __slots__ = ("sem", "eng", "n", "marked", "value")

    def __init__(self, eng=None, n=0, sem=None, value=0):
        self.eng, self.n, self.sem, self.value, self.marked = eng, n, sem, value, False


class Prog:

    ENGINES = ("pe", "act", "dve", "pool", "sp")

    def __init__(self):
        self.q = {e: [] for e in self.ENGINES}
        self.last = {e: None for e in self.ENGINES}
        self.pending = {e: [] for e in self.ENGINES}

    def op(self, eng, fn, *waits, link=False):
        w = [t for t in waits if t is not None] + self.pending[eng]
        self.pending[eng] = []
        if link and self.last[eng] is not None:
            w.append(self.last[eng])
        tok = Tok(eng, len(self.q[eng]))
        for t in w:
            t.marked = True
        self.q[eng].append((fn, w, tok, None))
        self.last[eng] = tok
        return tok

    def dma(self, fn, sem, value, *waits, eng="sp"):
        w = [t for t in waits if t is not None]
        for t in w:
            t.marked = True
        self.q[eng].append((fn, w, None, sem))
        return Tok(sem=sem, value=value)

    def phase(self):
        for e in ("pe", "act", "dve", "pool"):
            self.pending[e] += [self.last[o] for o in ("pe", "act", "dve", "pool")
                                if self.last[o] is not None and (o != e or e != "pe")]

    def here(self):
        return [self.last[o] for o in ("pe", "act", "dve", "pool") if self.last[o] is not None]

    def number(self, sems):
        for e in self.ENGINES:
            n = 0
            for _, _, tok, _ in self.q[e]:
                if tok is not None:
                    n += tok.marked
                    tok.sem, tok.value = sems[e], n

    def emit(self, eng, e):
        seen = {}
        for fn, waits, tok, sem in self.q[eng]:
            for t in waits:
                if seen.get(t.sem.name, 0) < t.value:
                    e.wait_ge(t.sem, t.value)
                    seen[t.sem.name] = t.value
            ins = fn(e)
            if sem is not None:
                ins.then_inc(sem, 16)
            elif tok.marked:
                ins.then_inc(tok.sem, 1)


class Slot:
    def __init__(self, ap, sem):
        self.ap, self.sem, self.count, self.free = ap, sem, 0, ()


def build(nc, dram, out_dram, stages):
    pr = Prog()
    ctx = ExitStack()
    with ctx:
        def sb(name, shape, dt=F32, where=ctx):
            return where.enter_context(nc.sbuf_tensor(name, shape, dt))

        def sem(name):
            return ctx.enter_context(nc.semaphore(name))

        PS = ctx.enter_context(nc.psum_tensor("banks", [P, 8, 512], F32))
        ring = sb("weight_ring", [P, NSLOT, WCOLS])
        x_tok = sb("x_tok", [P, TC, D])
        xn_tok = sb("xn_tok", [P, TC, D])
        xT = sb("xT", [P, DC, T])
        A_ds = sb("A_ds", [P, TC, NREL, T])
        ident = sb("ident", [P, P])
        selrow = sb("selrow", [HEADS, HEADS, P])
        ones = sb("ones", [P, P])
        desc = sb("desc", [P, NEXP])
        iota_slot = sb("iota_slot", [P, SLOT])
        before = sb("before", [P, TC, T])
        stat = sb("stat", [P, 64])

        eng_sem = {e: sem("done_" + e) for e in Prog.ENGINES}
        slots = [Slot(ring[:, i, :], sem(f"slot{i}_loaded")) for i in range(NSLOT)]
        turn = [0]
        io_sems = {}

        def load_small(dst, src, name, *waits):
            if name not in io_sems:
                io_sems[name] = [sem("ld_" + name), 0]
            s = io_sems[name]
            s[1] += 16
            return pr.dma(lambda e: e.dma_start(dst, src), s[0], s[1], *waits)

        def load(*parts):
            s = slots[turn[0] % NSLOT]
            turn[0] += 1
            at, waits, aps = 0, s.free, []
            for src in parts:
                n = src.shape[-1]
                dst = s.ap[:, at:at + n]
                s.count += 16
                tok = pr.dma(lambda e, d=dst, r=src: e.dma_start(d, r), s.sem, s.count, *waits)
                aps.append(dst)
                at += n
            return s, tok, aps

        def release(s, *toks):
            s.free = toks

        def w3(ap, k, n):
            return ap[:, 0:k * n].rearrange("p (k n) -> p k n", k=k)

        def mm(out, lhsT, rhs, start, stop, *waits):
            return pr.op("pe", lambda e: e.matmul(out, lhsT, rhs, start=start, stop=stop), *waits)

        def tr(out, src, *waits, n=P):
            return pr.op("pe", lambda e: e.transpose(out, src, ident[0:n, 0:n]), *waits)

        def vtt(out, a, b, op, *waits, link=True, eng="dve"):
            return pr.op(eng, lambda e: e.tensor_tensor(out, a, b, op), *waits, link=link)

        def vts(out, a, s1, s2, op0, op1=None, *waits, link=True, eng="dve"):
            if op1 is None:
                return pr.op(eng, lambda e: e.tensor_scalar(out, a, s1, None, op0), *waits, link=link)
            return pr.op(eng, lambda e: e.tensor_scalar(out, a, s1, s2, op0, op1), *waits, link=link)

        def stt(out, a, s, b, op0, op1, *waits, link=True):
            return pr.op("dve", lambda e: e.scalar_tensor_tensor(out=out, in0=a, scalar=s, in1=b, op0=op0,
                                                                 op1=op1), *waits, link=link)

        def vred(out, a, op, *waits, link=True):
            return pr.op("dve", lambda e: e.tensor_reduce(out, a, AX.X, op), *waits, link=link)

        def vcopy(out, a, *waits, link=True, eng="dve"):
            return pr.op(eng, lambda e: e.tensor_copy(out, a), *waits, link=link)

        def vrec(out, a, *waits):
            return pr.op("dve", lambda e: e.reciprocal(out, a), *waits, link=True)

        def act(out, a, f, *waits, bias=None, scale=1.0, accum=None, link=False):
            kw = {"scale": scale}
            if bias is not None:
                kw["bias"] = bias
            if accum is not None:
                kw["accum_out"] = accum
            return pr.op("act", lambda e: e.activation(out, a, f, **kw), *waits, link=link)

        def acopy(out, a, *waits):
            return pr.op("act", lambda e: e.copy(out, a), *waits)

        def bc(ap, shape):
            return ap.broadcast_to(shape)

        const_loads = [load_small(dst, src, "const") for dst, src in (
            (ident[:], dram["c_ident"]), (selrow[:], dram["c_selrow"]), (desc[:], dram["c_desc"]),
            (iota_slot[:], dram["c_iota_slot"]), (before[:], dram["c_before"]),
            (x_tok[:], dram["x"]))]
        pr.op("dve", lambda e: e.memset(stat[:, 62:64], -0.5), const_loads[-1])
        pr.op("dve", lambda e: e.memset(ones[:], 1.0), const_loads[-1])
        pr.pending["pe"] = [const_loads[-1]]
        pr.pending["act"] = [const_loads[-1]]
        pr.pending["pool"] = [const_loads[-1]]

        acc_tok = PS[:, 0:4, 0:HALF]
        acc_T = PS[:, 0:DC, 0:T]

        def as_tok(buf):
            return buf.rearrange("p c (h n) -> p (c h) n", h=2)

        def tok_to_T(dst, src):
            pr.phase()
            for g in range(DC // 2):
                for f in range(2):
                    for c in range(TC):
                        t = tr(PS[:, 5 + g, f * T + c * P:f * T + c * P + P],
                               src[:, c, (2 * g + f) * P:(2 * g + f + 1) * P])
                d = dst[:, 2 * g:2 * g + 2, :].rearrange("p a t -> p (a t)")
                (acopy if g == 1 else vcopy)(d, PS[:, 5 + g, :], t)
            pr.phase()

        def T_to_tok(dst, src):
            pr.phase()
            for i in range(4):
                c, g = i // 2, i % 2
                for f in range(3):
                    t = tr(PS[:, 4 + i, f * P:(f + 1) * P], src[:, 3 * g + f, c * P:(c + 1) * P])
                (acopy if i % 2 else vcopy)(dst[:, c, g * HALF:(g + 1) * HALF], PS[:, 4 + i, 0:HALF], t)
            pr.phase()

        def project_T(units, movers, bias_rows=None):
            for u, ((s, tok, (w,)), mv) in enumerate(zip(units, movers)):
                w = w3(w, DC, D)
                for o in range(DC):
                    for k in range(DC):
                        t = mm(PS[:, o, 0:T], w[:, k, o * P:(o + 1) * P], mv[:, k, :],
                               u == 0 and k == 0, u == len(units) - 1 and k == DC - 1, tok)
                release(s, t)
            return t

        def project_tok(units, stats, chunks=TC):
            for u, ((s, tok, (w,)), st) in enumerate(zip(units, stats)):
                w = w3(w, DC, D)
                for k in range(DC):
                    for c in range(chunks):
                        for h in range(2):
                            t = mm(PS[:, 2 * c + h, 0:HALF], st[:, k, c * P:(c + 1) * P],
                                   w[:, k, h * HALF:(h + 1) * HALF],
                                   u == 0 and k == 0, u == len(units) - 1 and k == DC - 1, tok)
                release(s, t)
            return t

        def norm(dst, src, eps, center=True, weight=None):
            pr.phase()
            half_stats = stat[:, 0:24].rearrange("p (c h s) -> p c h s", c=TC, h=2)
            moments = stat[:, 24:28].rearrange("p (c s) -> p c s", c=TC)
            mean, var, rstd = moments[:, :, 0], moments[:, :, 1], stat[:, 28:30]
            for c in range(TC):
                for h in range(2):
                    pr.op("dve", lambda e, c=c, h=h: e.bn_stats(half_stats[:, c, h, :],
                                                                src[:, c, h * HALF:(h + 1) * HALF]))
            for c in range(TC):
                pr.op("dve", lambda e, c=c: e.bn_aggr(moments[:, c, :], half_stats[:, c, :, :]
                                                      .rearrange("p h s -> p (h s)")), link=True)
            if not center:
                vtt(rstd, mean, mean, ALU.mult)
                vtt(var, var, rstd, ALU.add)
            t = vts(rstd, var, eps, None, ALU.add)
            t = pr.op("pool", lambda e: e.tensor_tensor(rstd, rstd, stat[:, 62:64], ALU.pow), t)
            for c in range(TC):
                if center:
                    t = vts(dst[:, c, :], src[:, c, :], mean[:, c:c + 1], rstd[:, c:c + 1], ALU.subtract,
                            ALU.mult, t, link=False)
                    if weight is not None:
                        vtt(dst[:, c, :], dst[:, c, :], weight, ALU.mult, t)
                else:
                    stt(dst[:, c, :], src[:, c, :], rstd[:, c:c + 1], weight, ALU.mult, ALU.mult, t)
            pr.phase()

        def rows_to_all(dst, src_tok, n, tmp):
            pr.phase()
            for c in range(TC):
                t = tr(PS[0:n, 4, c * P:(c + 1) * P], src_tok[:, c, 0:n])
            vcopy(tmp[0:n, :], PS[0:n, 4, 0:T], t)
            pr.phase()
            spread_rows(dst, tmp, n)

        def spread_rows(dst, rows, n):
            done = {}
            for r in range(n):
                b = 6 + r % 2
                t = mm(PS[:, b, 0:T], selrow[0:n, r, :], rows[0:n, :], True, True, done.get(r - 2))
                done[r] = (acopy if r % 2 else vcopy)(dst[:, r, :], PS[:, b, 0:T], t)
            pr.phase()

        def first_max(oh, s, v, tmp):
            sh = [P, TC, NEXP]
            dsc = bc(desc[:].unsqueeze(1), sh)
            vred(v, s, ALU.max)
            vtt(tmp, s, bc(v.unsqueeze(2), sh), ALU.is_equal)
            vtt(tmp, tmp, dsc, ALU.mult)
            vred(stat[:, 60:62], tmp, ALU.max)
            vtt(oh, tmp, bc(stat[:, 60:62].unsqueeze(2), sh), ALU.is_equal)

        def top2(oh1, oh2, s, v1, v2, tmp, s2):
            first_max(oh1, s, v1, tmp)
            stt(s2, oh1, -3.0e38, s, ALU.mult, ALU.add)
            first_max(oh2, s2, v2, tmp)

        def softmax8(p, logits_ps):
            sh = [P, TC, NEXP]
            m, z = stat[:, 40:42], stat[:, 42:44]
            vred(m, logits_ps, ALU.max)
            vtt(p, logits_ps, bc(m.unsqueeze(2), sh), ALU.subtract)
            pr.phase()
            act(p, p, ACT.Exp)
            pr.phase()
            vred(z, p, ALU.add)
            vrec(z, z)
            vtt(p, p, bc(z.unsqueeze(2), sh), ALU.mult)

        def small_logits(bank, src_T, w, n):
            for c in range(TC):
                for k in range(DC):
                    mm(PS[:, bank, c * 16:c * 16 + n], src_T[:, k, c * P:(c + 1) * P], w[:, k, :],
                       k == 0, k == DC - 1)
            return PS[:, bank, 0:32].rearrange("p (c n) -> p c n", c=TC)[:, :, 0:n]

        def glu_experts(xT_, gates, experts, hT, tmp):
            pr.phase()
            n_exp = len(experts)
            bank_free = {}
            ht_free = [None, None]
            step = 0
            for e, (load_up, load_down, hc_n, row) in enumerate(experts):
                gate_unit, up_unit = load_up()
                (gs, gt, gw), (us, ut, uw) = gate_unit, up_unit
                n = hc_n * P
                gw, uw = w3(gw, DC, n), w3(uw, DC, n)
                h = hT[e % 2]
                ready = []
                for o in range(hc_n):
                    b = 4 + step % 4
                    for k in range(DC):
                        mm(PS[:, b, 0:T], gw[:, k, o * P:(o + 1) * P], xT_[:, k, :], k == 0, k == DC - 1,
                           gt, bank_free.get(step - 4))
                    for k in range(DC):
                        t = mm(PS[:, b, T:2 * T], uw[:, k, o * P:(o + 1) * P], xT_[:, k, :], k == 0,
                               k == DC - 1, ut)
                    s_buf = tmp[:, step % 4, :]
                    a = act(s_buf, PS[:, b, 0:T], ACT.Silu, t, bank_free.get(step - 4))
                    v = vtt(h[:, o, :], PS[:, b, T:2 * T], s_buf, ALU.mult, a, ht_free[e % 2], link=False)
                    bank_free[step] = v
                    if row is not None:
                        v = vtt(h[:, o, :], h[:, o, :], gates[:, row, :], ALU.mult, v)
                    ready.append(v)
                    step += 1
                release(gs, t)
                release(us, t)
                ds, dt, (dw,) = load_down()
                dw = w3(dw, hc_n, D)
                for o in range(hc_n):
                    for c in range(TC):
                        for hf in range(2):
                            t = mm(PS[:, 2 * c + hf, 0:HALF], h[:, o, c * P:(c + 1) * P],
                                   dw[:, o, hf * HALF:(hf + 1) * HALF], e == 0 and o == 0,
                                   e == n_exp - 1 and o == hc_n - 1, dt, ready[o])
                release(ds, t)
                ht_free[e % 2] = t
            pr.phase()

        def edge_attention(nh, rels, counts, a_src, a_dst, values, width, E, ET, maskb, rcp, eps):
            S = rels * T
            pr.phase()
            vts(maskb, counts, 0.0, NEG, ALU.is_equal, ALU.mult)
            m = stat[:, 16:16 + TC * nh].rearrange("p (c h) -> p c h", c=TC)
            spread = {}
            step = 0
            for h in range(nh):
                for r in range(rels):
                    b = 6 + step % 2
                    t = mm(PS[:, b, 0:T], selrow[0:nh, h, :], a_src[0:nh, r * T:(r + 1) * T], True, True,
                           spread.get(step - 2))
                    for c in range(TC):
                        spread[step] = act(E[:, c, h * S + r * T:h * S + (r + 1) * T], PS[:, b, 0:T],
                                           ACT.Identity, t, bias=a_dst(c, h, r))
                    step += 1
            pr.phase()
            exped = {}
            for c in range(TC):
                Ec = E[:, c, 0:nh * S]
                E3 = Ec.rearrange("p (h s) -> p h s", h=nh)
                sh = [P, nh, S]
                stt(Ec, Ec, 0.2, Ec, ALU.mult, ALU.max)
                vtt(E3, E3, bc(maskb[:, c, :].unsqueeze(1), sh), ALU.add)
                vred(m[:, c, :], E3, ALU.max)
                t = vts(m[:, c, :], m[:, c, :], -1.0, None, ALU.mult)
                exped[c] = []
                for h in range(nh):
                    exped[c].append(act(E3[:, h, :], E3[:, h, :], ACT.Exp, t, bias=m[:, c, h:h + 1]))
            for c in range(TC):
                for h in range(nh):
                    Eh = E[:, c, h * S:(h + 1) * S]
                    pr.op("dve", lambda e, c=c, h=h, Eh=Eh: e.scalar_tensor_tensor(
                        out=Eh, in0=Eh, scalar=1.0, in1=counts[:, c, :], op0=ALU.mult, op1=ALU.mult,
                        accum_out=rcp[:, c, h:h + 1]), exped[c][h])
            pr.pending["dve"].append(pr.last["dve"])
            if eps:
                vts(rcp, rcp, eps, None, ALU.add)
            else:
                vts(rcp, rcp, 1e-30, None, ALU.max)
            vrec(rcp, rcp)
            pr.phase()
            n_src = S // P
            per_bank = min(n_src, 2)
            banks, et_free = {}, {}
            step = 0
            for h in range(nh):
                et = ET[:, h % 2, 0:n_src, :]
                copied = []
                for g in range(n_src // per_bank):
                    b = 4 + step % 4
                    for j in range(per_bank):
                        for c in range(TC):
                            jj = g * per_bank + j
                            t = tr(PS[:, b, j * T + c * P:j * T + c * P + P],
                                   E[:, c, h * S + jj * P:h * S + (jj + 1) * P], banks.get(step - 4))
                    cp = (acopy if step % 2 else vcopy)(
                        et[:, g * per_bank:(g + 1) * per_bank, :].rearrange("p a t -> p (a t)"),
                        PS[:, b, :], t, et_free.get(h - 2))
                    banks[step] = cp
                    copied.append(cp)
                    step += 1
                for c in range(TC):
                    for n0 in range(0, width, HALF):
                        n1 = min(width, n0 + HALF)
                        col = h * width + n0
                        o = PS[:, 2 * c + col // HALF, col % HALF:col % HALF + n1 - n0]
                        for j in range(n_src):
                            t = mm(o, et[:, j, c * P:(c + 1) * P], values(j)[:, col:col + n1 - n0],
                                   j == 0, j == n_src - 1, *copied)
                et_free[h] = t
            pr.phase()

        def attention(qT, kT, v, yT, Pm, PT, causal):
            scale = 1.0 / math.sqrt(HD)
            mx = stat[:, 8:8 + HEADS * TC].rearrange("p (h c) -> p h c", h=HEADS)
            sm = stat[:, 32:32 + HEADS * TC].rearrange("p (h c) -> p h c", h=HEADS)
            pr.phase()
            free = {}
            for h in range(HEADS):
                f, p0 = h // 2, HD * (h % 2)
                b = h % 4
                for c in range(TC):
                    t = mm(PS[:, b, c * T:(c + 1) * T], qT[p0:p0 + HD, f, c * P:(c + 1) * P],
                           kT[p0:p0 + HD, f, :], True, True, free.get(h - 4))
                s3 = PS[:, b, :].rearrange("p (c t) -> p c t", c=TC)
                if causal is not None:
                    stt(Pm[:, h, :, :], s3, scale, causal, ALU.mult, ALU.add, t)
                    src, sc = Pm[:, h, :, :], 1.0
                else:
                    src, sc = s3, scale
                vred(mx[:, h, :], src, ALU.max, t)
                t = vts(mx[:, h, :], mx[:, h, :], -sc, None, ALU.mult)
                for c in range(TC):
                    free[h] = act(Pm[:, h, c, :], src[:, c, :], ACT.Exp, t, bias=mx[:, h, c:c + 1], scale=sc,
                                  accum=sm[:, h, c:c + 1])
            pr.phase()
            vrec(sm, sm)
            free, yfree, pt_free = {}, {}, {}
            for h in range(HEADS):
                f, p0 = h // 2, HD * (h % 2)
                n = vtt(Pm[:, h, :, :], Pm[:, h, :, :], bc(sm[:, h, :].unsqueeze(2), [P, TC, T]), ALU.mult)
                b = h % 4
                for k in range(TC):
                    for c in range(TC):
                        t = tr(PS[:, b, k * T + c * P:k * T + c * P + P], Pm[:, h, c, k * P:(k + 1) * P], n,
                               free.get(h - 4))
                pt = PT[:, h % 2, :]
                cp = acopy(pt, PS[:, b, :], t, pt_free.get(h - 2))
                free[h] = cp
                for k in range(TC):
                    t = mm(PS[p0:p0 + HD, 4 + f % 4, 0:T], v[:, k, h * HD:(h + 1) * HD],
                           pt[:, k * T:(k + 1) * T], k == 0, k == TC - 1, cp, yfree.get(f - 4))
                pt_free[h] = t
                if h % 2:
                    yfree[f] = vcopy(yT[:, f, :], PS[:, 4 + f % 4, 0:T], t)
            pr.phase()

        def dispatched_experts(rows_tok, S, probs, run_experts, xdT, cbT, o2):
            pr.phase()
            NS = NEXP * SLOT
            for f in range(DC):
                b = f % 4
                for c in range(TC):
                    t = mm(PS[:, b, :], rows_tok[:, c, f * P:(f + 1) * P], S[:, c, :], c == 0, c == TC - 1,
                           fr[f - 4] if f >= 4 else None)
                cp = (acopy if f % 2 else vcopy)(xdT[:, f, :], PS[:, b, :], t)
                if f == 0:
                    fr = {}
                fr[f] = cp
            pr.phase()
            for c in range(TC):
                for e in range(NEXP):
                    sl = S[:, c, e * SLOT:(e + 1) * SLOT]
                    vts(sl, sl, probs[:, c, e:e + 1], None, ALU.mult, link=False)
            pr.phase()
            for j in range(NS // P):
                for c in range(TC):
                    t = tr(PS[:, 4 + j, c * P:(c + 1) * P], S[:, c, j * P:(j + 1) * P])
                (acopy if j % 2 else vcopy)(cbT[:, j, :], PS[:, 4 + j, 0:T], t)
            pr.phase()
            run_experts(lambda e: xdT[:, :, e * SLOT:(e + 1) * SLOT], o2)
            pr.phase()
            for j in range(NS // P):
                for c in range(TC):
                    for h in range(2):
                        mm(PS[:, 2 * c + h, 0:HALF], cbT[:, j, c * P:(c + 1) * P],
                           o2[:, j, h * HALF:(h + 1) * HALF], j == 0, j == NS // P - 1)
            pr.phase()

        def stage_graph():
            with ExitStack() as st:
                idx = sb("edge_idx", [P, 3, EC], I32, st)
                idf = sb("edge_idx_f", [P, 3, EC], F32, st)
                rs = sb("edge_rel_src", [P, EC], F32, st)
                iota = sb("iota_rel_src", [P, NREL * T], F32, st)
                ohd = sb("onehot_dst", [P, 3, T], BF16, st)
                ohs = sb("onehot_rel_src", [P, 3, NREL * T], BF16, st)
                load_small(iota[:], dram["c_iota"], "edges", *pr.here())
                for i, n in enumerate(("src", "dst", "edge_type_3")):
                    t = load_small(idx[:, i, :], dram[n], "edges")
                vcopy(idf[:], idx[:], t)
                stt(rs[:], idf[:, 2, :], float(T), idf[:, 0, :], ALU.mult, ALU.add)
                done = {}
                for k in range(EC):
                    b = k % 3
                    v1 = vts(ohs[:, b, :], iota[:], rs[:, k:k + 1], None, ALU.is_equal, None,
                             done.get(k - 3), link=(k == 0))
                    v2 = vts(ohd[:, b, :], iota[:, 0:T], idf[:, 1, k:k + 1], None, ALU.is_equal, None,
                             link=False)
                    for c in range(TC):
                        for h in range(2):
                            t = mm(PS[:, 2 * c + h, 0:HALF], ohd[:, b, c * P:(c + 1) * P],
                                   ohs[:, b, h * HALF:(h + 1) * HALF], k == 0, k == EC - 1, v1, v2)
                    done[k] = t
                vcopy(A_ds[:].rearrange("p c r s -> p (c r s)").rearrange("p (b n) -> p b n", n=HALF),
                      acc_tok, t)
                pr.phase()

        def residual_add():
            pr.phase()
            vtt(as_tok(x_tok[:]), acc_tok, as_tok(x_tok[:]), ALU.add)
            pr.phase()

        def stage_L0_gnn():
            with ExitStack() as st:
                A_sd = sb("A_sd", [P, NREL, TC, T], F32, st)
                hT = xT
                qiT = sb("gate_qiT", [P, DC, T], F32, st)
                G = sb("gate_rows", [96, 3, QB, D], BF16, st)
                selg = sb("gate_sel", [96, QN * QL], BF16, st)
                qT = sb("gate_qT", [P, DC, QB * QL], F32, st)
                brow = sb("gate_bg_row", [1, D], F32, st)
                bcol = sb("gate_bias_cols", [P, 3, DC], F32, st)
                work = sb("gate_work", [P, 2, QN * QL], F32, st)
                aggT = work[:, 0, 0:DC * T].rearrange("p (k t) -> p k t", k=DC)
                hg = work[:, 0, 0:TC * D].rearrange("p (c n) -> p c n", c=TC)
                parts = work[:, 1, 0:TC * D].bitcast(BF16)
                part = [parts[:, 0:TC * D].rearrange("p (c n) -> p c n", c=TC),
                        parts[:, TC * D:2 * TC * D].rearrange("p (c n) -> p c n", c=TC),
                        qiT[:].rearrange("p k t -> p (k t)").bitcast(BF16)[:, 0:TC * D]
                        .rearrange("p (c n) -> p c n", c=TC)]
                t = load_small(qT[:], dram["L0_gnn_query_T"], "gate", *pr.here())
                for i, n in enumerate(("L0_gnn_b1", "L0_gnn_b2", "L0_gnn_bq")):
                    t = load_small(bcol[:, i, :], dram[n], "gate")
                t = load_small(brow[:], dram["L0_gnn_bg"], "gate")
                selq = load_small(hg_all := work[0:96, 0, :], dram["c_selg"], "selg")
                vcopy(selg[:], hg_all, selq)
                pr.phase()
                pr.pending["pe"].append(t)
                pr.pending["act"].append(t)
                pr.phase()
                turned = []
                for r in range(NREL):
                    for k in range(TC):
                        for c in range(TC):
                            t = tr(PS[:, r, k * T + c * P:k * T + c * P + P], A_ds[:, c, r, k * P:(k + 1) * P])
                    turned.append(vcopy(A_sd[:, r, :, :].rearrange("p k t -> p (k t)"), PS[:, r, :], t))
                for r in range(NREL):
                    for k in range(TC):
                        t = mm(PS[:, 3 + r, 0:T], ones[:], A_sd[:, r, k, :], k == 0, k == TC - 1, turned[r])
                    cnt = work[:, 0, r * T:(r + 1) * T]
                    vts(cnt, PS[:, 3 + r, 0:T], 1.0, None, ALU.max, None, t)
                    vrec(cnt, cnt)
                    vtt(A_sd[:, r, :, :], PS[:, r, :].rearrange("p (k t) -> p k t", k=TC),
                        bc(cnt.unsqueeze(1), [P, TC, T]), ALU.mult)
                pr.phase()

                def split_rows(dst_part, n_src_tok):
                    vcopy(dst_part[0], n_src_tok)
                    vtt(n_src_tok, n_src_tok, dst_part[0], ALU.subtract)
                    vcopy(dst_part[1], n_src_tok)
                    vtt(n_src_tok, n_src_tok, dst_part[1], ALU.subtract)
                    return vcopy(dst_part[2], n_src_tok)

                moved = None
                wgq_slot, wgq_tok, (wgq,) = load(dram["L0_gnn_Wg"][1])
                wq3 = w3(wgq, DC, D)
                for half in range(2):
                    pr.phase()
                    for c in range(TC):
                        for h in range(2):
                            o = PS[:, 2 * c + h, 0:HALF]
                            mm(o, ones[0:1, :], brow[0:1, h * HALF:(h + 1) * HALF], True, False)
                            for k in range(DC):
                                r0 = half * T + c * P
                                t = mm(o, qT[:, k, r0:r0 + P], wq3[:, k, h * HALF:(h + 1) * HALF], False,
                                       k == DC - 1, wgq_tok)
                    vcopy(as_tok(hg), acc_tok, t, moved)
                    v = split_rows(part, hg)
                    for i in range(3):
                        for z in range(2):
                            dst = G[QN:QN + QL, i, 4 * half:4 * half + 4, :].rearrange(
                                "p (c z) n -> p z c n", z=2)[:, z, :, :]
                            moved = load_small(dst, part[i][QL * z:QL * (z + 1), :, :], "grow", v)
                release(wgq_slot, t)

                def gate():
                    nonlocal moved
                    pr.phase()
                    t = project_tok([load(dram["L0_gnn_Wg"][0])], [hT])
                    vcopy(as_tok(hg), acc_tok, t, moved)
                    v = split_rows(part, hg)
                    for i in range(3):
                        for z in range(4):
                            dst = G[0:QN, i, :, :].rearrange("p (c z) n -> p z c n", z=4)[:, z, :, :]
                            moved = load_small(dst, part[i][QN * z:QN * (z + 1), :, :], "grow", v)
                    pr.phase()
                    nodes = xn_tok[:].rearrange("p c n -> p (c n)").rearrange("p (k t) -> p k t", k=DC)
                    wqh_slot, wqh_tok, (wqh,) = load(dram["L0_gnn_Wq"][0])
                    wqh = w3(wqh, DC, D)
                    slot_free, work_free, side_free = {}, {}, {}
                    step = 0
                    for b in range(QB):
                        for f in range(DC):
                            it = b * DC + f
                            w = work[:, it % 2, :]
                            for q in range(2):
                                pb = 2 * (step % 3)
                                for i in range(3):
                                    for k in range(2):
                                        col = (2 * q + k) * 512
                                        t = mm(PS[:, pb + k, :], G[0:96, i, b, f * P:(f + 1) * P],
                                               selg[:, col:col + 512], i == 0, i == 2, moved,
                                               slot_free.get(step - 3))
                                a = act(PS[:, pb:pb + 2, :], PS[:, pb:pb + 2, :], ACT.Sigmoid, t)
                                n16 = QN // 2
                                s4 = PS[:, pb:pb + 2, :].rearrange("p a (n l) -> p (a n) l", l=QL)
                                q4 = bc(qT[:, f, b * QL:(b + 1) * QL].unsqueeze(1), [P, n16, QL])
                                w4 = w[:, q * 1024:(q + 1) * 1024].rearrange("p (n l) -> p n l", l=QL)
                                slot_free[step] = vtt(w4, s4, q4, ALU.mult, a, work_free.get(it - 2),
                                                      link=False)
                                step += 1
                            w3_ = w.rearrange("p (n l) -> p n l", l=QL)
                            folded = vtt(w3_[:, :, 0:QL // 2], w3_[:, :, 0:QL // 2], w3_[:, :, QL // 2:QL],
                                         ALU.add, slot_free[step - 1], eng="pool", link=False)
                            waiting.append((it, b, f, w3_, folded))
                            if it > 0:
                                finish_sum(waiting.pop(0), work_free)
                            if it % 7 == 3 and it // 7 < DC:
                                o = it // 7
                                for k in range(DC):
                                    t = mm(PS[:, 6 + o % 2, 0:T], wqh[:, k, o * P:(o + 1) * P], hT[:, k, :],
                                           k == 0, k == DC - 1, wqh_tok, side_free.get(o - 2))
                                side_free[o] = acopy(nodes[:, o, :], PS[:, 6 + o % 2, 0:T], t)
                    release(wqh_slot, t)
                    finish_sum(waiting.pop(0), work_free)
                    pr.phase()
                    t = project_T([load(dram["L0_gnn_Wq"][1])], [qiT])
                    alpha = work[:, 0, 0:DC * T].rearrange("p (k t) -> p k t", k=DC)
                    th = work[:, 1, 0:DC * T].rearrange("p (k t) -> p k t", k=DC)
                    a = act(th, qiT[:], ACT.Tanh)
                    vtt(th, th, hT[:], ALU.subtract, a)
                    v = vtt(nodes, acc_T, nodes, ALU.add, t)
                    for o in range(DC):
                        a = act(alpha[:, o, :], nodes[:, o, :], ACT.Sigmoid, v, bias=bcol[:, 2, o:o + 1])
                    vtt(th, th, alpha, ALU.mult, a)
                    vtt(hT[:], hT[:], th, ALU.add)
                    pr.phase()

                waiting = []

                def finish_sum(item, work_free):
                    it, b, f, w3_, folded = item
                    work_free[it] = vred(qiT[:, f, b * QN:(b + 1) * QN], w3_[:, :, 0:QL // 2], ALU.add,
                                         folded, link=False)

                def rgcn(h_tok, h_T, layer, root, b):
                    pr.phase()
                    units, movers = [load(dram[root])], [h_T]
                    s, tok, (w,) = units[0]
                    w = w3(w, DC, D)
                    for o in range(DC):
                        for k in range(DC):
                            t = mm(PS[:, o, 0:T], w[:, k, o * P:(o + 1) * P], h_T[:, k, :], k == 0, False, tok)
                    release(s, t)
                    agg_free, bank_free = None, {}
                    step = 0
                    for r in range(NREL):
                        s, tok, (w,) = load(dram[layer][r])
                        w = w3(w, DC, D)
                        for f in range(DC):
                            bk = 6 + step % 2
                            for k in range(TC):
                                t = mm(PS[:, bk, 0:T], h_tok[:, k, f * P:(f + 1) * P], A_sd[:, r, k, :], k == 0,
                                       k == TC - 1, bank_free.get(step - 2))
                            bank_free[step] = cp = vcopy(aggT[:, f, :], PS[:, bk, 0:T], t, agg_free, link=False)
                            step += 1
                        for o in range(DC):
                            for k in range(DC):
                                t = mm(PS[:, o, 0:T], w[:, k, o * P:(o + 1) * P], aggT[:, k, :], False,
                                       r == NREL - 1 and k == DC - 1, tok, cp)
                        release(s, t)
                        agg_free = t
                    for o in range(DC):
                        act(hT[:, o, :], PS[:, o, 0:T], ACT.Relu, t, bias=bcol[:, b, o:o + 1])
                    pr.phase()

                pr.phase()
                pr.pending["act"].append(moved)
                pr.pending["dve"].append(moved)
                norm(xn_tok, x_tok, 1e-5)
                tok_to_T(xT, xn_tok)
                rgcn(xn_tok, xT, "L0_gnn_W_rel1", "L0_gnn_W_root1", 0)
                gate()
                T_to_tok(xn_tok, hT)
                rgcn(xn_tok, xT, "L0_gnn_W_rel2", "L0_gnn_W_root2", 1)
                gate()
                T_to_tok(xn_tok, hT)
                vtt(x_tok[:], x_tok[:], xn_tok[:], ALU.add)
                pr.phase()

        def stage_L0_ffn():
            with ExitStack() as st:
                rw = sb("router_w", [P, DC, NEXP + 1], F32, st)
                sgb = sb("sg_b", [P, 1], F32, st)
                gt = sb("gates_tok", [P, TC, 16], F32, st)
                sc = [sb(f"route{i}", [P, TC, NEXP], F32, st) for i in range(5)]
                gates = sb("gates_all", [P, NEXP + 1, T], F32, st)
                grow = sb("gates_row", [16, T], F32, st)
                hT = [sb(f"hidden{i}", [P, DC, T], F32, st) for i in range(2)]
                tmp = sb("silu", [P, 4, T], F32, st)
                load_small(rw[:], dram["L0_ffn_router_sg_w"], "l0f", *pr.here())
                t = load_small(sgb[:], dram["L0_ffn_sg_b"], "l0f")
                norm(xn_tok, x_tok, 1e-5)
                tok_to_T(xT, xn_tok)
                pr.pending["pe"].append(t)
                pr.pending["act"].append(t)
                lg = small_logits(4, xT, rw, NEXP + 1)
                pr.phase()
                alpha = gt[:, :, NEXP:NEXP + 1]
                for c in range(TC):
                    act(gt[:, c, NEXP:NEXP + 1], PS[:, 4, c * 16 + NEXP:c * 16 + NEXP + 1], ACT.Sigmoid,
                        bias=sgb[:, 0:1])
                pr.phase()
                probs, oh1, oh2, tm, s2 = (s[:] for s in sc)
                softmax8(probs, lg[:, :, 0:NEXP])
                v1, v2, z = stat[:, 44:46], stat[:, 46:48], stat[:, 48:50]
                top2(oh1, oh2, probs, v1, v2, tm, s2)
                vtt(z, v1, v2, ALU.add)
                vrec(z, z)
                vts(s2[:, :, 0:1], alpha, -1.0, 1.0, ALU.mult, ALU.add)
                vtt(z.unsqueeze(2), z.unsqueeze(2), s2[:, :, 0:1], ALU.mult)
                vtt(oh1, oh1, oh2, ALU.add)
                vtt(oh1, oh1, probs, ALU.mult)
                vtt(gt[:, :, 0:NEXP], oh1, bc(z.unsqueeze(2), [P, TC, NEXP]), ALU.mult)
                rows_to_all(gates, gt, NEXP + 1, grow)

                def experts():
                    def up(e):
                        a, b = load(dram["L0_ffn_w_gate"][e]), load(dram["L0_ffn_w_up"][e])
                        return (a[0], a[1], a[2][0]), (b[0], b[1], b[2][0])

                    def shared_up():
                        s, t_, (g, u) = load(dram["L0_ffn_ws_gate"], dram["L0_ffn_ws_up"])
                        return (s, t_, g), (s, t_, u)
                    r = [(lambda e=e: up(e), lambda e=e: load(dram["L0_ffn_w_down"][e]), DC, e)
                         for e in range(NEXP)]
                    return r + [(shared_up, lambda: load(dram["L0_ffn_ws_down"]), DC // 2, NEXP)]
                glu_experts(xT, gates, experts(), hT, tmp)
                residual_add()

        def stage_L1_gnn():
            with ExitStack() as st:
                bd = sb("gat_blockdiag", [P, 2 * P], F32, st)
                ab = sb("gat_attn", [P, 2, D], F32, st)
                ft = sb("gat_ft", [P, TC, D], F32, st)
                res = sb("gat_res", [P, TC, D], F32, st)
                a12 = sb("gat_a", [P, TC, 2, HEADS], F32, st)
                arow = sb("gat_arow", [HEADS, T], F32, st)
                cnt = sb("gat_counts", [P, TC, T], F32, st)
                maskb = sb("gat_mask", [P, TC, T], F32, st)
                rcp = sb("gat_rcp", [P, TC, HEADS], F32, st)
                E = sb("gat_E", [P, TC, HEADS * T], F32, st)
                ET = sb("gat_ET", [P, 2, TC, T], F32, st)
                z = pr.op("dve", lambda e: e.memset(bd[:], 0.0), link=True)
                for i, n in enumerate(("L1_gnn_W_fc", "L1_gnn_W_res")):
                    for k in range(2):
                        load_small(bd[HD * k:HD * (k + 1), P * i + HD * k:P * i + HD * (k + 1)], dram[n],
                                   "gat", z)
                for i, n in enumerate(("L1_gnn_attn_l", "L1_gnn_attn_r")):
                    t = load_small(ab[:, i, :], dram[n].partition_broadcast(P), "gat", z)
                norm(xn_tok, x_tok, 1e-5)
                tok_to_T(xT, xn_tok)
                pr.pending["pe"].append(t)
                pr.pending["dve"].append(t)
                for c in range(TC):
                    for f in range(DC):
                        t = mm(PS[:, 3 * c + f // 2, (f % 2) * T:(f % 2 + 1) * T],
                               xT[:, f, c * P:(c + 1) * P], bd[:], True, True)
                pr.phase()
                for c in range(TC):
                    o4 = PS[:, 3 * c:3 * c + 3, :].rearrange("p b (f w) -> p (b f) w", f=2)
                    cp = acopy if c else vcopy
                    cp(ft[:, c, :].rearrange("p (f n) -> p f n", f=DC), o4[:, :, 0:P])
                    cp(res[:, c, :].rearrange("p (f n) -> p f n", f=DC), o4[:, :, P:2 * P])
                pr.phase()
                for c in range(TC):
                    for i in range(2):
                        pv = E[:, c, 0:D]
                        vtt(pv, ft[:, c, :], ab[:, i, :], ALU.mult)
                        vred(a12[:, c, i, :], pv.rearrange("p (h e) -> p h e", h=HEADS), ALU.add)
                vtt(cnt[:], A_ds[:, :, 0, :], A_ds[:, :, 1, :], ALU.add)
                vtt(cnt[:], cnt[:], A_ds[:, :, 2, :], ALU.add)
                pr.phase()
                for c in range(TC):
                    t = tr(PS[0:HEADS, 6, c * P:(c + 1) * P], a12[:, c, 0, :])
                vcopy(arow[:], PS[0:HEADS, 6, 0:T], t)
                edge_attention(HEADS, 1, cnt[:], arow[:], lambda c, h, r: a12[:, c, 1, h:h + 1],
                               lambda j: ft[:, j, :], HD, E[:], ET[:], maskb[:], rcp[:], 0.0)
                for c in range(TC):
                    for g in range(2):
                        o3 = PS[:, 2 * c + g, 0:HALF].rearrange("p (h e) -> p h e", e=HD)
                        f3 = ft[:, c, g * HALF:(g + 1) * HALF].rearrange("p (h e) -> p h e", e=HD)
                        vtt(f3, o3, bc(rcp[:, c, 6 * g:6 * g + 6].unsqueeze(2), [P, 6, HD]), ALU.mult)
                vtt(ft[:], ft[:], res[:], ALU.add)
                stt(x_tok[:], ft[:], 0.0, x_tok[:], ALU.max, ALU.add)
                pr.phase()

        def store_slots(S, mask, slot):
            for c in range(TC):
                for e in range(NEXP):
                    vts(S[:, c, e * SLOT:(e + 1) * SLOT], iota_slot[:], slot[:, c, e:e + 1],
                        mask[:, c, e:e + 1], ALU.is_equal, ALU.mult, link=(c == 0 and e == 0))

        def stage_L1_ffn():
            with ExitStack() as st0:
                wln = sb("ln_w", [P, 2, D], F32, st0)
                y_tok = sb("y_tok", [P, TC, D], F32, st0)
                load_small(wln[:, 0, :], dram["L1_ffn_ln1_w"].partition_broadcast(P), "l1f", *pr.here())
                t = load_small(wln[:, 1, :], dram["L1_ffn_ln2_w"].partition_broadcast(P), "l1f")
                with ExitStack() as st:
                    causal = sb("causal", [P, TC, T], F32, st)
                    qT = sb("att_qT", [P, DC, T], F32, st)
                    kT = sb("att_kT", [P, DC, T], F32, st)
                    v = sb("att_v", [P, TC, D], F32, st)
                    Pm = sb("att_P", [P, HEADS, TC, T], F32, st)
                    PT = sb("att_PT", [P, 2, 2 * T], F32, st)
                    t = load_small(causal[:], dram["c_causal"], "l1f", *pr.here())
                    norm(y_tok, x_tok, 1e-5)
                    pr.pending["dve"].append(t)
                    norm(xn_tok, y_tok, 1e-5, weight=wln[:, 0, :])
                    tok_to_T(xT, xn_tok)
                    qkv(qT, kT, v, [dram["L1_ffn_c_attn_w"][i] for i in range(3)])
                    attention(qT, kT, v, xT, Pm, PT, causal[:])
                    project_tok([load(dram["L1_ffn_c_proj_w"])], [xT])
                    pr.phase()
                    vtt(as_tok(y_tok[:]), acc_tok, as_tok(y_tok[:]), ALU.add)
                    pr.phase()
                with ExitStack() as st:
                    wg = sb("moe_wg", [P, DC, NEXP], F32, st)
                    sc = [sb(f"moe_r{i}", [P, TC, NEXP], F32, st) for i in range(6)]
                    S = sb("moe_S", [P, TC, NEXP * SLOT], F32, st)
                    xdT = sb("moe_xdT", [P, DC, NEXP * SLOT], F32, st)
                    cbT = sb("moe_cbT", [P, NEXP * SLOT // P, T], F32, st)
                    o2 = sb("moe_out", [P, NEXP * SLOT // P, D], F32, st)
                    hT = sb("moe_h", [P, 8, DC * SLOT], F32, st)
                    t = load_small(wg[:], dram["L1_ffn_w_g"], "l1f", *pr.here())
                    norm(xn_tok, y_tok, 1e-5, weight=wln[:, 1, :])
                    tok_to_T(xT, xn_tok)
                    pr.pending["pe"].append(t)
                    lg = small_logits(4, xT, wg, NEXP)
                    pr.phase()
                    logits, oh1, oh2, tm, s2, probs = (s[:] for s in sc)
                    vcopy(logits, lg)
                    v1, v2, z = stat[:, 44:46], stat[:, 46:48], stat[:, 48:50]
                    top2(oh1, oh2, logits, v1, v2, tm, s2)
                    vtt(oh1, oh1, oh2, ALU.add)
                    vtt(probs, logits, bc(v1.unsqueeze(2), [P, TC, NEXP]), ALU.subtract)
                    pr.phase()
                    act(probs, probs, ACT.Exp)
                    pr.phase()
                    vtt(probs, probs, oh1, ALU.mult)
                    vred(z, probs, ALU.add)
                    vrec(z, z)
                    vtt(probs, probs, bc(z.unsqueeze(2), [P, TC, NEXP]), ALU.mult)
                    for c in range(TC):
                        for k in range(TC):
                            mm(PS[:, 5, c * 16:c * 16 + NEXP], before[:, k, c * P:(c + 1) * P], oh1[:, k, :],
                               k == 0, k == TC - 1, pr.last["dve"])
                    pr.phase()
                    vcopy(s2, PS[:, 5, 0:32].rearrange("p (c n) -> p c n", c=TC)[:, :, 0:NEXP])
                    store_slots(S, oh1, s2)

                    hid = 4
                    buffers = 2 * hid
                    gelu, used, drained = {}, {}, {}

                    def up_unit(e, u, xd):
                        s, tok, (w,) = load(dram["L1_ffn_c_fc"][e, u])
                        w = w3(w, DC, D)
                        n = hid * e + u
                        b = 4 + n % 4
                        for o in range(DC):
                            for k in range(DC):
                                t = mm(PS[:, b, o * SLOT:(o + 1) * SLOT], w[:, k, o * P:(o + 1) * P],
                                       xd[:, k, :], k == 0, k == DC - 1, tok, gelu.get(n - 4))
                        release(s, t)
                        gelu[n] = act(hT[:, n % buffers, :], PS[:, b, 0:DC * SLOT], ACT.Gelu, t,
                                      used.get(n - buffers))

                    def down_unit(e, u, o2_):
                        s, tok, (w,) = load(dram["L1_ffn_c_proj_e"][e, u])
                        w = w3(w, DC, D)
                        n = hid * e + u
                        p0, pair = SLOT * (e % 2), 2 * ((e // 2) % 2)
                        for k in range(DC):
                            for h in range(2):
                                t = mm(PS[p0:p0 + SLOT, pair + h, 0:HALF],
                                       hT[:, n % buffers, k * SLOT:(k + 1) * SLOT],
                                       w[:, k, h * HALF:(h + 1) * HALF], u == 0 and k == 0,
                                       u == hid - 1 and k == DC - 1, tok, gelu[n], drained.get(e // 2 - 2))
                        release(s, t)
                        used[n] = t
                        if e % 2 and u == hid - 1:
                            drained[e // 2] = vcopy(o2_[:, e // 2, :].rearrange("p (h n) -> p h n", h=2),
                                                    PS[:, pair:pair + 2, 0:HALF], t)

                    def run_experts(xd, o2_):
                        for e in range(NEXP + 1):
                            for u in range(hid):
                                if e < NEXP:
                                    up_unit(e, u, xd(e))
                                if e > 0:
                                    down_unit(e - 1, u, o2_)

                    dispatched_experts(xn_tok, S, probs, run_experts, xdT, cbT, o2)
                    vtt(as_tok(x_tok[:]), acc_tok, as_tok(x_tok[:]), ALU.add)
                    vtt(x_tok[:], x_tok[:], y_tok[:], ALU.add)
                    pr.phase()

        def qkv(qT, kT, v, units):
            for dst, u in ((qT, units[0]), (kT, units[1])):
                pr.phase()
                project_T([load(u)], [xT])
                pr.phase()
                vcopy(dst[:, 0:3, :], acc_T[:, 0:3, :])
                acopy(dst[:, 3:6, :], acc_T[:, 3:6, :])
            pr.phase()
            project_tok([load(units[2])], [xT])
            pr.phase()
            vcopy(as_tok(v[:])[:, 0:2, :], acc_tok[:, 0:2, :])
            acopy(as_tok(v[:])[:, 2:4, :], acc_tok[:, 2:4, :])
            pr.phase()

        def stage_L2_gnn():
            with ExitStack() as st:
                xr = sb("rgat_xr", [P, NREL, TC, D], F32, st)
                qk = sb("rgat_qk", [P, DC, 2 * RH], F32, st)
                qk2 = sb("rgat_qk2", [P, DC, 2], F32, st)
                bias = sb("rgat_bias", [P, 2, D], F32, st)
                kj = sb("rgat_kj", [RH, NREL * T], F32, st)
                qi = sb("rgat_qi", [P, NREL, TC, RH], F32, st)
                rcp = sb("rgat_rcp", [P, TC, RH], F32, st)
                maskb = sb("rgat_mask", [P, TC, NREL * T], F32, st)
                E = sb("rgat_E", [P, TC, RH * NREL * T], F32, st)
                ET = sb("rgat_ET", [P, 2, NREL * TC, T], F32, st)
                w = pr.here()
                load_small(qk[:], dram["L2_gnn_qk1"], "rgat", *w)
                load_small(qk2[:], dram["L2_gnn_qk2"], "rgat")
                load_small(bias[:, 0, :], dram["L2_gnn_b1"].partition_broadcast(P), "rgat")
                t = load_small(bias[:, 1, :], dram["L2_gnn_b2"].partition_broadcast(P), "rgat")
                norm(xn_tok, x_tok, 1e-5)
                pr.pending["pe"].append(t)
                pr.pending["dve"].append(t)

                def layer(weights, qkw, nh, brow, finish):
                    tok_to_T(xT, xn_tok)
                    xrT = E[:, 0, 0:DC * T].rearrange("p (k t) -> p k t", k=DC)
                    for r in range(NREL):
                        project_tok([load(dram[weights][r])], [xT])
                        pr.phase()
                        vcopy(as_tok(xr[:, r, :, :])[:, 0:2, :], acc_tok[:, 0:2, :])
                        acopy(as_tok(xr[:, r, :, :])[:, 2:4, :], acc_tok[:, 2:4, :])
                        tok_to_T(xrT, xr[:, r, :, :])
                        for k in range(DC):
                            t = mm(PS[0:nh, 4, 0:T], qkw[:, k, nh:2 * nh], xrT[:, k, :], k == 0, k == DC - 1)
                        vcopy(kj[0:nh, r * T:(r + 1) * T], PS[0:nh, 4, 0:T], t)
                        for c in range(TC):
                            for k in range(DC):
                                t = mm(PS[:, 5, c * 16:c * 16 + nh], xrT[:, k, c * P:(c + 1) * P],
                                       qkw[:, k, 0:nh], k == 0, k == DC - 1)
                        vcopy(qi[:, r, :, 0:nh],
                              PS[:, 5, 0:32].rearrange("p (c n) -> p c n", c=TC)[:, :, 0:nh], t)
                        pr.phase()
                    edge_attention(nh, NREL, A_ds[:].rearrange("p c r s -> p c (r s)"), kj[:],
                                   lambda c, h, r: qi[:, r, c, h:h + 1],
                                   lambda j: xr[:, j // TC, j % TC, :], D // nh, E[:], ET[:], maskb[:],
                                   rcp[:, :, 0:nh], 1e-16)
                    for c in range(TC):
                        for g in range(2):
                            w_ = min(HALF, D // nh)
                            hn = HALF // w_
                            o3 = PS[:, 2 * c + g, 0:HALF].rearrange("p (h e) -> p h e", e=w_)
                            d3 = xn_tok[:, c, g * HALF:(g + 1) * HALF].rearrange("p (h e) -> p h e", e=w_)
                            rc = rcp[:, c, hn * g:hn * (g + 1)] if nh > 1 else rcp[:, c, 0:1]
                            vtt(d3, o3, bc(rc.unsqueeze(2), [P, hn, w_]), ALU.mult)
                    vtt(xn_tok[:], xn_tok[:], bc(brow.unsqueeze(1), [P, TC, D]), ALU.add)
                    finish()

                def elu():
                    ev = E[:, 0, 0:TC * D].rearrange("p (c n) -> p c n", c=TC)
                    t = vts(ev, xn_tok[:], 0.0, None, ALU.min)
                    t = act(ev, ev, ACT.Exp, t)
                    vts(ev, ev, -1.0, None, ALU.add, None, t)
                    stt(xn_tok[:], xn_tok[:], 0.0, ev, ALU.max, ALU.add)
                    pr.phase()

                def add_residual():
                    vtt(x_tok[:], x_tok[:], xn_tok[:], ALU.add)
                    pr.phase()

                layer("L2_gnn_W1", qk, RH, bias[:, 0, :], elu)
                layer("L2_gnn_W2", qk2, 1, bias[:, 1, :], add_residual)

        def stage_L2_ffn():
            with ExitStack() as st:
                sw = sb("sw_w", [P, DC, NEXP], F32, st)
                swb = sb("sw_b", [P, NEXP], F32, st)
                sc = [sb(f"sw_r{i}", [P, TC, NEXP], F32, st) for i in range(4)]
                pr2 = sb("sw_pair", [P, TC, 2], F32, st)
                prow = sb("sw_prow", [2, T], F32, st)
                pall = sb("sw_pall", [P, 2, T], F32, st)
                cmpb = sb("sw_cmp", [P, 3, T], F32, st)
                S = sb("sw_S", [P, TC, NEXP * SLOT], F32, st)
                xdT = sb("sw_xdT", [P, DC, NEXP * SLOT], F32, st)
                cbT = sb("sw_cbT", [P, NEXP * SLOT // P, T], F32, st)
                o2 = sb("sw_out", [P, NEXP * SLOT // P, D], F32, st)
                hT = sb("sw_h", [P, 2, 3 * SLOT], F32, st)
                b1 = sb("sw_b1", [1, NEXP * HALF], F32, st)
                b2 = sb("sw_b2", [1, NEXP * D], F32, st)
                earlier = sb("earlier", [P, TC, T], F32, st)
                w = pr.here()
                load_small(sw[:], dram["L2_ffn_switch_w"], "sw", *w)
                load_small(swb[:], dram["L2_ffn_switch_b"].partition_broadcast(P), "sw")
                load_small(earlier[:], dram["c_earlier"], "sw")
                load_small(b1[:], dram["L2_ffn_b1"], "sw")
                t = load_small(b2[:], dram["L2_ffn_b2"], "sw")
                norm(xn_tok, x_tok, 1e-5)
                tok_to_T(xT, xn_tok)
                pr.pending["pe"].append(t)
                pr.pending["dve"].append(t)
                lg = small_logits(4, xT, sw, NEXP)
                pr.phase()
                probs, oh, tm, slot = (s[:] for s in sc)
                vtt(slot, lg, bc(swb[:].unsqueeze(1), [P, TC, NEXP]), ALU.add)
                softmax8(probs, slot)
                pmax = stat[:, 44:46]
                first_max(oh, probs, pmax, tm)
                vcopy(pr2[:, :, 0], pmax)
                vtt(tm, oh, bc(desc[:].unsqueeze(1), [P, TC, NEXP]), ALU.mult)
                vred(pr2[:, :, 1], tm, ALU.max)
                rows_to_all(pall, pr2, 2, prow)
                rank, keep = stat[:, 46:48], stat[:, 48:50]
                for c in range(TC):
                    p1, r1 = pr2[:, c, 0:1], pr2[:, c, 1:2]
                    vts(cmpb[:, 0, :], pall[:, 0, :], p1, None, ALU.is_gt)
                    vts(cmpb[:, 1, :], pall[:, 0, :], p1, None, ALU.is_equal)
                    vtt(cmpb[:, 1, :], cmpb[:, 1, :], earlier[:, c, :], ALU.mult)
                    vtt(cmpb[:, 0, :], cmpb[:, 0, :], cmpb[:, 1, :], ALU.add)
                    vts(cmpb[:, 1, :], pall[:, 1, :], r1, None, ALU.is_equal)
                    vtt(cmpb[:, 0, :], cmpb[:, 0, :], cmpb[:, 1, :], ALU.mult)
                    vred(rank[:, c:c + 1], cmpb[:, 0, :], ALU.add)
                vts(keep, rank, float(CAP2), None, ALU.is_lt)
                vtt(oh, oh, bc(keep.unsqueeze(2), [P, TC, NEXP]), ALU.mult)
                vcopy(slot, bc(rank.unsqueeze(2), [P, TC, NEXP]))
                store_slots(S, oh, slot)

                free = {}

                def expert(e, xd, o2_):
                    s, tok, (wa, wb) = load(dram["L2_ffn_w1"][e], dram["L2_ffn_w2"][e])
                    wa, wb = w3(wa, DC, HALF), w3(wb, 3, D)
                    b = 4 + e % 4
                    for o in range(3):
                        d = PS[:, b, o * SLOT:(o + 1) * SLOT]
                        mm(d, b1[0:1, e * HALF + o * P:e * HALF + (o + 1) * P], ones[0:1, 0:SLOT], True, False,
                           free.get(("ps", e - 4)))
                        for k in range(DC):
                            t = mm(d, wa[:, k, o * P:(o + 1) * P], xd[:, k, :], False, k == DC - 1, tok)
                    a = act(hT[:, e % 2, :], PS[:, b, 0:3 * SLOT], ACT.Gelu, t, free.get(("h", e - 2)))
                    free["ps", e] = a
                    p0, pair = SLOT * (e % 2), 2 * ((e // 2) % 2)
                    for h in range(2):
                        d = PS[p0:p0 + SLOT, pair + h, 0:HALF]
                        mm(d, ones[0:1, 0:SLOT], b2[0:1, e * D + h * HALF:e * D + (h + 1) * HALF], True, False,
                           free.get(("o", e // 2 - 2)))
                        for k in range(3):
                            t = mm(d, hT[:, e % 2, k * SLOT:(k + 1) * SLOT], wb[:, k, h * HALF:(h + 1) * HALF],
                                   False, k == 2, a)
                    release(s, t)
                    free["h", e] = t
                    if e % 2:
                        free["o", e // 2] = vcopy(o2_[:, e // 2, :].rearrange("p (h n) -> p h n", h=2),
                                                  PS[:, pair:pair + 2, 0:HALF], t)

                def run_experts(xd, o2_):
                    for e in range(NEXP):
                        expert(e, xd(e), o2_)

                dispatched_experts(xn_tok, S, probs, run_experts, xdT, cbT, o2)
                vtt(as_tok(x_tok[:]), acc_tok, as_tok(x_tok[:]), ALU.add)
                drop = stat[:, 50:52]
                vts(drop, keep, -1.0, 1.0, ALU.mult, ALU.add)
                vtt(drop, drop, pmax, ALU.mult)
                for c in range(TC):
                    stt(x_tok[:, c, :], xn_tok[:, c, :], drop[:, c:c + 1], x_tok[:, c, :], ALU.mult, ALU.add)
                pr.phase()

        def stage_L3_gnn():
            with ExitStack() as st:
                A3 = sb("gcn_A_ds", [P, TC, T], F32, st)
                A3s = sb("gcn_A_sd", [P, TC, T], F32, st)
                eye = sb("gcn_eye", [P, TC, T], F32, st)
                b = sb("gcn_b", [P, D], F32, st)
                xs = sb("gcn_xs", [P, TC, D], F32, st)
                aggT = sb("gcn_aggT", [P, DC, T], F32, st)
                w = pr.here()
                load_small(eye[:], dram["c_eye"], "gcn", *w)
                t = load_small(b[:], dram["L3_gnn_b"].partition_broadcast(P), "gcn")
                deg, dinv = stat[:, 30:32], stat[:, 32:34]
                norm(xn_tok, x_tok, 1e-5)
                pr.pending["dve"].append(t)
                vtt(A3[:], A_ds[:, :, 0, :], A_ds[:, :, 1, :], ALU.add)
                vtt(A3[:], A3[:], A_ds[:, :, 2, :], ALU.add)
                vtt(A3[:], A3[:], eye[:], ALU.add)
                vred(deg, A3[:], ALU.add)
                pr.phase()
                t = pr.op("pool", lambda e: e.tensor_tensor(dinv, deg, stat[:, 62:64], ALU.pow))
                pr.pending["dve"].append(t)
                for c in range(TC):
                    vts(xs[:, c, :], xn_tok[:, c, :], dinv[:, c:c + 1], None, ALU.mult)
                for k in range(TC):
                    for c in range(TC):
                        t = tr(PS[:, 6, k * T + c * P:k * T + c * P + P], A3[:, c, k * P:(k + 1) * P])
                vcopy(A3s[:].rearrange("p k t -> p (k t)"), PS[:, 6, :], t)
                pr.phase()
                for f in range(DC):
                    for k in range(TC):
                        mm(PS[:, f, 0:T], xs[:, k, f * P:(f + 1) * P], A3s[:, k, :], k == 0, k == TC - 1)
                pr.phase()
                vcopy(aggT[:, 0:3, :], acc_T[:, 0:3, :])
                acopy(aggT[:, 3:6, :], acc_T[:, 3:6, :])
                pr.phase()
                project_tok([load(dram["L3_gnn_W"])], [aggT])
                pr.phase()
                for c in range(TC):
                    for h in range(2):
                        x2 = x_tok[:, c, h * HALF:(h + 1) * HALF]
                        stt(x2, PS[:, 2 * c + h, 0:HALF], dinv[:, c:c + 1], x2, ALU.mult, ALU.add)
                    vtt(x_tok[:, c, :], x_tok[:, c, :], b[:], ALU.add)
                pr.phase()

        def stage_L3_ffn():
            with ExitStack() as st0:
                nw = sb("rms_w", [P, 2, D], F32, st0)
                y_tok = sb("y3_tok", [P, TC, D], F32, st0)
                w = pr.here()
                load_small(nw[:, 0, :], dram["L3_ffn_norm1_w"].partition_broadcast(P), "l3f", *w)
                t = load_small(nw[:, 1, :], dram["L3_ffn_norm2_w"].partition_broadcast(P), "l3f")
                with ExitStack() as st:
                    qT = sb("at3_qT", [P, DC, T], F32, st)
                    kT = sb("at3_kT", [P, DC, T], F32, st)
                    v = sb("at3_v", [P, TC, D], F32, st)
                    Pm = sb("at3_P", [P, HEADS, TC, T], F32, st)
                    PT = sb("at3_PT", [P, 2, 2 * T], F32, st)
                    norm(y_tok, x_tok, 1e-5)
                    pr.pending["dve"].append(t)
                    norm(xn_tok, y_tok, 1e-6, center=False, weight=nw[:, 0, :])
                    tok_to_T(xT, xn_tok)
                    qkv(qT, kT, v, [dram["L3_ffn_Wq"], dram["L3_ffn_Wk"], dram["L3_ffn_Wv"]])
                    attention(qT, kT, v, xT, Pm, PT, None)
                    project_tok([load(dram["L3_ffn_Wo"])], [xT])
                    pr.phase()
                    vtt(as_tok(y_tok[:]), acc_tok, as_tok(y_tok[:]), ALU.add)
                    pr.phase()
                with ExitStack() as st:
                    gw = sb("g3_w", [P, DC, NEXP], F32, st)
                    gt = sb("g3_tok", [P, TC, 16], F32, st)
                    sc = [sb(f"g3_r{i}", [P, TC, NEXP], F32, st) for i in range(5)]
                    gates = sb("g3_all", [P, NEXP, T], F32, st)
                    grow = sb("g3_row", [16, T], F32, st)
                    hT = [sb(f"h3_{i}", [P, DC, T], F32, st) for i in range(2)]
                    tmp = sb("silu3", [P, 4, T], F32, st)
                    t = load_small(gw[:], dram["L3_ffn_gate_w"], "l3f", *pr.here())
                    norm(xn_tok, y_tok, 1e-6, center=False, weight=nw[:, 1, :])
                    tok_to_T(xT, xn_tok)
                    pr.pending["pe"].append(t)
                    lg = small_logits(4, xT, gw, NEXP)
                    pr.phase()
                    probs, oh1, oh2, tm, s2 = (s[:] for s in sc)
                    softmax8(probs, lg)
                    v1, v2, z = stat[:, 44:46], stat[:, 46:48], stat[:, 48:50]
                    top2(oh1, oh2, probs, v1, v2, tm, s2)
                    vtt(z, v1, v2, ALU.add)
                    vts(z, z, 1e-20, None, ALU.add)
                    vrec(z, z)
                    vtt(oh1, oh1, oh2, ALU.add)
                    vtt(oh1, oh1, probs, ALU.mult)
                    vtt(gt[:, :, 0:NEXP], oh1, bc(z.unsqueeze(2), [P, TC, NEXP]), ALU.mult)
                    rows_to_all(gates, gt, NEXP, grow)
                    vtt(x_tok[:], x_tok[:], y_tok[:], ALU.add)

                    def up(e):
                        s, t_, (g, u) = load(dram["L3_ffn_Weg"][e], dram["L3_ffn_Weu"][e])
                        return (s, t_, g), (s, t_, u)

                    def shared_up():
                        a, b = load(dram["L3_ffn_Wsg"]), load(dram["L3_ffn_Wsu"])
                        return (a[0], a[1], a[2][0]), (b[0], b[1], b[2][0])
                    experts = [(lambda e=e: up(e), lambda e=e: load(dram["L3_ffn_Wed"][e]), DC // 2, e)
                               for e in range(NEXP)]
                    experts.append((shared_up, lambda: load(dram["L3_ffn_Wsd"]), DC, None))
                    glu_experts(xT, gates, experts, hT, tmp)
                    residual_add()

        table = {"graph": stage_graph, "L0_gnn": stage_L0_gnn, "L0_ffn": stage_L0_ffn, "L1_gnn": stage_L1_gnn,
                 "L1_ffn": stage_L1_ffn, "L2_gnn": stage_L2_gnn, "L2_ffn": stage_L2_ffn,
                 "L3_gnn": stage_L3_gnn, "L3_ffn": stage_L3_ffn}
        for s in stages:
            table[s]()

        stored = sem("stored")
        pr.dma(lambda e: e.dma_start(out_dram, x_tok[:]), stored, 16, *pr.here())
        pr.number(eng_sem)

        block = ctx.enter_context(nc.Block())

        @block.sync
        def _(e):
            pr.emit("sp", e)
            e.wait_ge(stored, 16)

        @block.tensor
        def _(e):
            pr.emit("pe", e)

        @block.scalar
        def _(e):
            pr.emit("act", e)

        @block.vector
        def _(e):
            pr.emit("dve", e)

        @block.gpsimd
        def _(e):
            pr.emit("pool", e)


STAGES = ["graph", "L0_gnn", "L0_ffn", "L1_gnn", "L1_ffn", "L2_gnn", "L2_ffn", "L3_gnn", "L3_ffn"]


def _constants():
    t = np.arange(T)
    part = t.reshape(TC, P).T
    sel = np.zeros((96, QN, QL), np.float32)
    for n in range(QN):
        sel[n, n, :] = 1.0
        sel[QN + np.arange(QL), n, np.arange(QL)] = 1.0
    selrow = np.zeros((HEADS, HEADS, P), np.float32)
    selrow[np.arange(HEADS), np.arange(HEADS), :] = 1.0
    return {
        "c_ident": np.eye(P, dtype=np.float32),
        "c_selrow": selrow,
        "c_desc": np.tile(np.arange(NEXP, 0, -1, dtype=np.float32), (P, 1)),
        "c_iota_slot": np.tile(np.arange(SLOT, dtype=np.float32), (P, 1)),
        "c_iota": np.tile(np.arange(NREL * T, dtype=np.float32), (P, 1)),
        "c_before": (part[:, :, None] < t).astype(np.float32),
        "c_earlier": (t < part[:, :, None]).astype(np.float32),
        "c_eye": (part[:, :, None] == t).astype(np.float32),
        "c_causal": np.where(t <= part[:, :, None], 0.0, NEG).astype(np.float32),
        "c_selg": sel.reshape(96, QN * QL),
    }


def _rows(w):
    w = np.asarray(w)
    *lead, k, n = w.shape
    w = w.reshape(*lead, k // P, P, n)
    w = np.moveaxis(w, -3, -2)
    return np.ascontiguousarray(w).reshape(*lead, P, k // P * n)


def _flip(w):
    return np.swapaxes(np.asarray(w), -1, -2)


def _cols(v):
    return np.ascontiguousarray(np.asarray(v).reshape(-1, P).T)


def _layout(i):
    a = {}
    a["x"] = np.ascontiguousarray(np.asarray(i["x"]).reshape(TC, P, D).transpose(1, 0, 2))
    for n in ("src", "dst", "edge_type_3"):
        a[n] = np.ascontiguousarray(np.asarray(i[n]).reshape(EC, P).T)
    q = np.asarray(i["L0_gnn_query_embs"]).reshape(QB * QL, D).T
    a["L0_gnn_query_T"] = _rows(q).reshape(P, DC, QB * QL)
    for n in ("L0_gnn_W_rel1", "L0_gnn_W_root1", "L0_gnn_W_rel2", "L0_gnn_W_root2", "L0_ffn_w_gate",
              "L0_ffn_w_up", "L0_ffn_w_down", "L0_ffn_ws_gate", "L0_ffn_ws_up", "L0_ffn_ws_down",
              "L2_gnn_W1", "L2_gnn_W2", "L2_ffn_w1", "L2_ffn_w2", "L3_gnn_W"):
        a[n] = _rows(i[n])
    for n in ("L0_gnn_Wg", "L0_gnn_Wq"):
        a[n] = _rows(_flip(i[n]).reshape(2, D, D))
    for n in ("L0_gnn_b1", "L0_gnn_b2", "L0_gnn_bq"):
        a[n] = _cols(i[n])
    a["L0_gnn_bg"] = np.asarray(i["L0_gnn_bg"]).reshape(1, D)
    a["L2_ffn_switch_w"] = _rows(i["L2_ffn_switch_w"]).reshape(P, DC, NEXP)
    for n, (u, v) in (("L0_ffn_router_sg_w", ("L0_ffn_router_w", "L0_ffn_sg_w")),
                      ("L2_gnn_qk1", ("L2_gnn_q1", "L2_gnn_k1")), ("L2_gnn_qk2", ("L2_gnn_q2", "L2_gnn_k2"))):
        side = np.concatenate([np.asarray(i[u]), np.asarray(i[v])], axis=1)
        a[n] = _rows(side).reshape(P, DC, side.shape[1])
    a["L0_ffn_sg_b"] = np.ascontiguousarray(np.broadcast_to(np.asarray(i["L0_ffn_sg_b"]).reshape(1, 1), (P, 1)))
    for n in ("L1_gnn_W_fc", "L1_gnn_W_res"):
        a[n] = np.ascontiguousarray(_flip(i[n]))
    for n in ("L1_gnn_attn_l", "L1_gnn_attn_r", "L1_ffn_ln1_w", "L1_ffn_ln2_w", "L2_gnn_b1", "L2_gnn_b2",
              "L2_ffn_switch_b", "L3_gnn_b", "L3_ffn_norm1_w", "L3_ffn_norm2_w"):
        a[n] = np.asarray(i[n]).reshape(-1)
    a["L1_ffn_c_attn_w"] = _rows(np.ascontiguousarray(
        _flip(i["L1_ffn_c_attn_w"]).reshape(D, 3, D).transpose(1, 0, 2)))
    a["L1_ffn_c_fc"] = _rows(np.ascontiguousarray(
        np.asarray(i["L1_ffn_c_fc"]).reshape(NEXP, D, 4, D).transpose(0, 2, 1, 3)))
    a["L1_ffn_c_proj_e"] = _rows(np.asarray(i["L1_ffn_c_proj_e"]).reshape(NEXP, 4, D, D))
    for n in ("L1_ffn_w_g", "L3_ffn_gate_w"):
        a[n] = _rows(_flip(i[n])).reshape(P, DC, NEXP)
    for n in ("L1_ffn_c_proj_w", "L3_ffn_Wq", "L3_ffn_Wk", "L3_ffn_Wv", "L3_ffn_Wo", "L3_ffn_Weg", "L3_ffn_Weu",
              "L3_ffn_Wed", "L3_ffn_Wsg", "L3_ffn_Wsu", "L3_ffn_Wsd"):
        a[n] = _rows(_flip(i[n]))
    for n in ("L2_ffn_b1", "L2_ffn_b2"):
        a[n] = np.asarray(i[n]).reshape(1, -1)
    return a


def kernel(**inputs):
    import concourse.bacc as bacc
    from concourse.bass_utils import run_bass_kernel_spmd

    nc = bacc.Bacc("TRN2", target_bir_lowering=False, num_devices=1)
    arrays = {f"in_{k}_dram": v for k, v in {**_layout(inputs), **_constants()}.items()}
    dram = {k[3:-5]: nc.dram_tensor(k, v.shape, mybir.dt.from_np(v.dtype), kind="ExternalInput").ap()
            for k, v in arrays.items()}
    out = nc.dram_tensor("out_dram", (P, TC, D), F32, kind="ExternalOutput").ap()
    build(nc, dram, out, STAGES)
    r = run_bass_kernel_spmd(nc, [arrays], core_ids=[0])
    got = r.results[0]["out_dram"]
    return np.ascontiguousarray(got.transpose(1, 0, 2)).reshape(T, D)
```

```python
import math
from contextlib import ExitStack

import numpy as np
import concourse.bass as bass
from concourse import mybir

F32 = mybir.dt.float32
BF16 = mybir.dt.bfloat16
I32 = mybir.dt.int32
ALU = mybir.AluOpType
ACT = mybir.ActivationFunctionType
AX = mybir.AxisListType

P = 128
T = 256
TC = T // P
D = 768
DC = D // P
HALF = D // 2
NREL = 3
NEDGE = 4352
EC = NEDGE // P
HEADS, HD = 12, 64
RH = 4
QB, QL, QN = 8, 64, T // 8
NEXP = 8
SLOT = 64
WIDE = 128
CAP1 = 64
CAP2 = int(1.25 * T / NEXP)
WCOLS = DC * D
NSLOT = 5
NEG = -1.0e30


class Tok:
    __slots__ = ("sem", "eng", "n", "marked", "value")

    def __init__(self, eng=None, n=0, sem=None, value=0):
        self.eng, self.n, self.sem, self.value, self.marked = eng, n, sem, value, False


class Prog:

    ENGINES = ("pe", "act", "dve", "pool", "sp")

    def __init__(self):
        self.q = {e: [] for e in self.ENGINES}
        self.last = {e: None for e in self.ENGINES}
        self.pending = {e: [] for e in self.ENGINES}

    def op(self, eng, fn, *waits, link=False):
        w = [t for t in waits if t is not None] + self.pending[eng]
        self.pending[eng] = []
        if link and self.last[eng] is not None:
            w.append(self.last[eng])
        tok = Tok(eng, len(self.q[eng]))
        for t in w:
            t.marked = True
        self.q[eng].append((fn, w, tok, None))
        self.last[eng] = tok
        return tok

    def dma(self, fn, sem, value, *waits, eng="sp"):
        w = [t for t in waits if t is not None]
        for t in w:
            t.marked = True
        self.q[eng].append((fn, w, None, sem))
        return Tok(sem=sem, value=value)

    def phase(self):
        for e in ("pe", "act", "dve", "pool"):
            self.pending[e] += [self.last[o] for o in ("pe", "act", "dve", "pool")
                                if self.last[o] is not None and (o != e or e != "pe")]

    def join(self):
        for e in self.ENGINES:
            for t in self.here():
                t.marked = True
            self.q[e].append((None, self.here(), None, None))

    def branch(self, flag, sub, *waits):
        for t in waits:
            t.marked = True
        for eng in self.ENGINES:
            def run(e, eng=eng):
                taken = e.value_load(flag, min_val=0, max_val=1)
                with e.If(taken > 0):
                    sub.emit(eng, e)
            self.q[eng].append((run, list(waits), None, None))

    def here(self):
        return [self.last[o] for o in ("pe", "act", "dve", "pool") if self.last[o] is not None]

    def number(self, sems):
        for e in self.ENGINES:
            n = 0
            for _, _, tok, _ in self.q[e]:
                if tok is not None:
                    n += tok.marked
                    tok.sem, tok.value = sems[e], n

    def emit(self, eng, e):
        seen = {}
        for fn, waits, tok, sem in self.q[eng]:
            for t in waits:
                if seen.get(t.sem.name, 0) < t.value:
                    e.wait_ge(t.sem, t.value)
                    seen[t.sem.name] = t.value
            ins = fn(e) if fn is not None else None
            if sem is not None:
                ins.then_inc(sem, 16)
            elif tok is not None and tok.marked:
                ins.then_inc(tok.sem, 1)


class Slot:
    def __init__(self, ap, sem):
        self.ap, self.sem, self.count, self.free = ap, sem, 0, ()


def build(nc, dram, out_dram, stages):
    pr = Prog()
    subs = []
    ctx = ExitStack()
    with ctx:
        def sb(name, shape, dt=F32, where=ctx):
            return where.enter_context(nc.sbuf_tensor(name, shape, dt))

        def sem(name):
            return ctx.enter_context(nc.semaphore(name))

        PS = ctx.enter_context(nc.psum_tensor("banks", [P, 8, 512], F32))
        ring = sb("weight_ring", [P, NSLOT, WCOLS])
        x_tok = sb("x_tok", [P, TC, D])
        xn_tok = sb("xn_tok", [P, TC, D])
        xT = sb("xT", [P, DC, T])
        A_ds = sb("A_ds", [P, TC, NREL, T])
        ident = sb("ident", [P, P])
        selrow = sb("selrow", [HEADS, HEADS, P])
        ones = sb("ones", [P, P])
        desc = sb("desc", [P, NEXP])
        iota_slot = sb("iota_slot", [P, WIDE])
        before = sb("before", [P, TC, T])
        stat = sb("stat", [P, 64])

        eng_sem = {e: sem("done_" + e) for e in Prog.ENGINES}
        slots = [Slot(ring[:, i, :], sem(f"slot{i}_loaded")) for i in range(NSLOT)]
        turn = [0]
        io_sems = {}

        def load_small(dst, src, name, *waits, eng="sp"):
            if name not in io_sems:
                io_sems[name] = [sem("ld_" + name), 0]
            s = io_sems[name]
            s[1] += 16
            return pr.dma(lambda e: e.dma_start(dst, src), s[0], s[1], *waits, eng=eng)

        def load(*parts):
            s = slots[turn[0] % NSLOT]
            turn[0] += 1
            at, waits, aps = 0, s.free, []
            for src in parts:
                n = src.shape[-1]
                dst = s.ap[:, at:at + n]
                s.count += 16
                tok = pr.dma(lambda e, d=dst, r=src: e.dma_start(d, r), s.sem, s.count, *waits)
                aps.append(dst)
                at += n
            return s, tok, aps

        def release(s, *toks):
            s.free = toks

        def w3(ap, k, n):
            return ap[:, 0:k * n].rearrange("p (k n) -> p k n", k=k)

        def mm(out, lhsT, rhs, start, stop, *waits):
            return pr.op("pe", lambda e: e.matmul(out, lhsT, rhs, start=start, stop=stop), *waits)

        def tr(out, src, *waits, n=P):
            return pr.op("pe", lambda e: e.transpose(out, src, ident[0:n, 0:n]), *waits)

        def vtt(out, a, b, op, *waits, link=True, eng="dve"):
            return pr.op(eng, lambda e: e.tensor_tensor(out, a, b, op), *waits, link=link)

        def vts(out, a, s1, s2, op0, op1=None, *waits, link=True, eng="dve"):
            if op1 is None:
                return pr.op(eng, lambda e: e.tensor_scalar(out, a, s1, None, op0), *waits, link=link)
            return pr.op(eng, lambda e: e.tensor_scalar(out, a, s1, s2, op0, op1), *waits, link=link)

        def stt(out, a, s, b, op0, op1, *waits, link=True):
            return pr.op("dve", lambda e: e.scalar_tensor_tensor(out=out, in0=a, scalar=s, in1=b, op0=op0,
                                                                 op1=op1), *waits, link=link)

        def vred(out, a, op, *waits, link=True):
            return pr.op("dve", lambda e: e.tensor_reduce(out, a, AX.X, op), *waits, link=link)

        def vcopy(out, a, *waits, link=True, eng="dve"):
            return pr.op(eng, lambda e: e.tensor_copy(out, a), *waits, link=link)

        def vrec(out, a, *waits):
            return pr.op("dve", lambda e: e.reciprocal(out, a), *waits, link=True)

        def act(out, a, f, *waits, bias=None, scale=1.0, accum=None, link=False):
            kw = {"scale": scale}
            if bias is not None:
                kw["bias"] = bias
            if accum is not None:
                kw["accum_out"] = accum
            return pr.op("act", lambda e: e.activation(out, a, f, **kw), *waits, link=link)

        def acopy(out, a, *waits):
            return pr.op("act", lambda e: e.copy(out, a), *waits)

        def bc(ap, shape):
            return ap.broadcast_to(shape)

        const_loads = [load_small(dst, src, "const") for dst, src in (
            (ident[:], dram["c_ident"]), (selrow[:], dram["c_selrow"]), (desc[:], dram["c_desc"]),
            (iota_slot[:], dram["c_iota_slot"]), (before[:], dram["c_before"]),
            (x_tok[:], dram["x"]))]
        pr.op("dve", lambda e: e.memset(stat[:, 62:64], -0.5), const_loads[-1])
        pr.op("dve", lambda e: e.memset(ones[:], 1.0), const_loads[-1])
        pr.pending["pe"] = [const_loads[-1]]
        pr.pending["act"] = [const_loads[-1]]
        pr.pending["pool"] = [const_loads[-1]]

        acc_tok = PS[:, 0:4, 0:HALF]
        acc_T = PS[:, 0:DC, 0:T]

        def as_tok(buf):
            return buf.rearrange("p c (h n) -> p (c h) n", h=2)

        def tok_to_T(dst, src):
            pr.phase()
            for g in range(DC // 2):
                for f in range(2):
                    for c in range(TC):
                        t = tr(PS[:, 5 + g, f * T + c * P:f * T + c * P + P],
                               src[:, c, (2 * g + f) * P:(2 * g + f + 1) * P])
                d = dst[:, 2 * g:2 * g + 2, :].rearrange("p a t -> p (a t)")
                (acopy if g == 1 else vcopy)(d, PS[:, 5 + g, :], t)
            pr.phase()

        def T_to_tok(dst, src):
            pr.phase()
            for i in range(4):
                c, g = i // 2, i % 2
                for f in range(3):
                    t = tr(PS[:, 4 + i, f * P:(f + 1) * P], src[:, 3 * g + f, c * P:(c + 1) * P])
                (acopy if i % 2 else vcopy)(dst[:, c, g * HALF:(g + 1) * HALF], PS[:, 4 + i, 0:HALF], t)
            pr.phase()

        def project_T(units, movers, bias_rows=None):
            for u, ((s, tok, (w,)), mv) in enumerate(zip(units, movers)):
                w = w3(w, DC, D)
                for o in range(DC):
                    for k in range(DC):
                        t = mm(PS[:, o, 0:T], w[:, k, o * P:(o + 1) * P], mv[:, k, :],
                               u == 0 and k == 0, u == len(units) - 1 and k == DC - 1, tok)
                release(s, t)
            return t

        def project_tok(units, stats, chunks=TC):
            for u, ((s, tok, (w,)), st) in enumerate(zip(units, stats)):
                w = w3(w, DC, D)
                for k in range(DC):
                    for c in range(chunks):
                        for h in range(2):
                            t = mm(PS[:, 2 * c + h, 0:HALF], st[:, k, c * P:(c + 1) * P],
                                   w[:, k, h * HALF:(h + 1) * HALF],
                                   u == 0 and k == 0, u == len(units) - 1 and k == DC - 1, tok)
                release(s, t)
            return t

        def norm(dst, src, eps, center=True, weight=None):
            pr.phase()
            half_stats = stat[:, 0:24].rearrange("p (c h s) -> p c h s", c=TC, h=2)
            moments = stat[:, 24:28].rearrange("p (c s) -> p c s", c=TC)
            mean, var, rstd = moments[:, :, 0], moments[:, :, 1], stat[:, 28:30]
            for c in range(TC):
                for h in range(2):
                    pr.op("dve", lambda e, c=c, h=h: e.bn_stats(half_stats[:, c, h, :],
                                                                src[:, c, h * HALF:(h + 1) * HALF]))
            for c in range(TC):
                pr.op("dve", lambda e, c=c: e.bn_aggr(moments[:, c, :], half_stats[:, c, :, :]
                                                      .rearrange("p h s -> p (h s)")), link=True)
            if not center:
                vtt(rstd, mean, mean, ALU.mult)
                vtt(var, var, rstd, ALU.add)
            t = vts(rstd, var, eps, None, ALU.add)
            t = pr.op("pool", lambda e: e.tensor_tensor(rstd, rstd, stat[:, 62:64], ALU.pow), t)
            for c in range(TC):
                if center:
                    t = vts(dst[:, c, :], src[:, c, :], mean[:, c:c + 1], rstd[:, c:c + 1], ALU.subtract,
                            ALU.mult, t, link=False)
                    if weight is not None:
                        vtt(dst[:, c, :], dst[:, c, :], weight, ALU.mult, t)
                else:
                    stt(dst[:, c, :], src[:, c, :], rstd[:, c:c + 1], weight, ALU.mult, ALU.mult, t)
            pr.phase()

        def rows_to_all(dst, src_tok, n, tmp):
            pr.phase()
            for c in range(TC):
                t = tr(PS[0:n, 4, c * P:(c + 1) * P], src_tok[:, c, 0:n])
            vcopy(tmp[0:n, :], PS[0:n, 4, 0:T], t)
            pr.phase()
            spread_rows(dst, tmp, n)

        def spread_rows(dst, rows, n):
            done = {}
            for r in range(n):
                b = 6 + r % 2
                t = mm(PS[:, b, 0:T], selrow[0:n, r, :], rows[0:n, :], True, True, done.get(r - 2))
                done[r] = (acopy if r % 2 else vcopy)(dst[:, r, :], PS[:, b, 0:T], t)
            pr.phase()

        def first_max(oh, s, v, tmp):
            sh = [P, TC, NEXP]
            dsc = bc(desc[:].unsqueeze(1), sh)
            vred(v, s, ALU.max)
            vtt(tmp, s, bc(v.unsqueeze(2), sh), ALU.is_equal)
            vtt(tmp, tmp, dsc, ALU.mult)
            vred(stat[:, 60:62], tmp, ALU.max)
            vtt(oh, tmp, bc(stat[:, 60:62].unsqueeze(2), sh), ALU.is_equal)

        def top2(oh1, oh2, s, v1, v2, tmp, s2):
            first_max(oh1, s, v1, tmp)
            stt(s2, oh1, -3.0e38, s, ALU.mult, ALU.add)
            first_max(oh2, s2, v2, tmp)

        def softmax8(p, logits_ps):
            sh = [P, TC, NEXP]
            m, z = stat[:, 40:42], stat[:, 42:44]
            vred(m, logits_ps, ALU.max)
            vtt(p, logits_ps, bc(m.unsqueeze(2), sh), ALU.subtract)
            pr.phase()
            act(p, p, ACT.Exp)
            pr.phase()
            vred(z, p, ALU.add)
            vrec(z, z)
            vtt(p, p, bc(z.unsqueeze(2), sh), ALU.mult)

        def small_logits(bank, src_T, w, n):
            for c in range(TC):
                for k in range(DC):
                    mm(PS[:, bank, c * 16:c * 16 + n], src_T[:, k, c * P:(c + 1) * P], w[:, k, :],
                       k == 0, k == DC - 1)
            return PS[:, bank, 0:32].rearrange("p (c n) -> p c n", c=TC)[:, :, 0:n]

        def glu_experts(xT_, gates, experts, hT, tmp, opens=True):
            pr.phase()
            n_exp = len(experts)
            bank_free = {}
            ht_free = [None, None]
            step = 0
            for e, (load_up, load_down, hc_n, row) in enumerate(experts):
                gate_unit, up_unit = load_up()
                (gs, gt, gw), (us, ut, uw) = gate_unit, up_unit
                n = hc_n * P
                gw, uw = w3(gw, DC, n), w3(uw, DC, n)
                h = hT[e % len(hT)]
                ready = []
                for o in range(hc_n):
                    b = 4 + step % 4
                    for k in range(DC):
                        mm(PS[:, b, 0:T], gw[:, k, o * P:(o + 1) * P], xT_[:, k, :], k == 0, k == DC - 1,
                           gt, bank_free.get(step - 4))
                    for k in range(DC):
                        t = mm(PS[:, b, T:2 * T], uw[:, k, o * P:(o + 1) * P], xT_[:, k, :], k == 0,
                               k == DC - 1, ut)
                    s_buf = tmp[:, step % 4, :]
                    a = act(s_buf, PS[:, b, 0:T], ACT.Silu, t, bank_free.get(step - 4))
                    v = vtt(h[:, o, :], PS[:, b, T:2 * T], s_buf, ALU.mult, a, ht_free[e % 2], link=False)
                    bank_free[step] = v
                    if row is not None:
                        v = vtt(h[:, o, :], h[:, o, :], gates[:, row, :], ALU.mult, v)
                    ready.append(v)
                    step += 1
                release(gs, t)
                release(us, t)
                ds, dt, (dw,) = load_down()
                dw = w3(dw, hc_n, D)
                for o in range(hc_n):
                    for c in range(TC):
                        for hf in range(2):
                            t = mm(PS[:, 2 * c + hf, 0:HALF], h[:, o, c * P:(c + 1) * P],
                                   dw[:, o, hf * HALF:(hf + 1) * HALF], opens and e == 0 and o == 0,
                                   e == n_exp - 1 and o == hc_n - 1, dt, ready[o])
                release(ds, t)
                ht_free[e % 2] = t
            pr.phase()

        def slots_of(slot, mask):
            pr.phase()
            for c in range(TC):
                for k in range(TC):
                    t = mm(PS[:, 5, c * 16:c * 16 + NEXP], before[:, k, c * P:(c + 1) * P], mask[:, k, :],
                           k == 0, k == TC - 1)
            vcopy(slot, PS[:, 5, 0:32].rearrange("p (c n) -> p c n", c=TC)[:, :, 0:NEXP], t)

        def routed_buffers(st, stage):
            return {"xd": sb(f"{stage}_xd", [P, 2, DC, WIDE], F32, st),
                    "S": sb(f"{stage}_S", [P, 2, 2, TC, WIDE], F32, st),
                    "cbT": sb(f"{stage}_cbT", [P, 2, T], F32, st),
                    "out": sb(f"{stage}_out", [P, 2, D], F32, st),
                    "h": sb(f"{stage}_h", [P, 2, DC, WIDE], F32, st),
                    "silu": sb(f"{stage}_silu", [P, 2, WIDE], F32, st),
                    "flag": sb(f"{stage}_flag", [1, 1], I32, st),
                    "over": sb(f"{stage}_over", [P, TC, NEXP], F32, st),
                    "over_all": sb(f"{stage}_over_all", [P, NEXP, T], F32, st),
                    "over_row": sb(f"{stage}_over_row", [16, T], F32, st),
                    "over_h": sb(f"{stage}_over_h", [P, 2, T], F32, st),
                    "piece": sb(f"{stage}_piece", [P, 3, D], F32, st)}

        def routed_experts(rows_tok, mask, gate, slot, load_up, load_down, hc_n, B):
            pr.phase()
            xd, S, cbT, out, h, silu = (B[k] for k in ("xd", "S", "cbT", "out", "h", "silu"))
            built, sent, turned, turned_sb, gu_free, drained = {}, {}, {}, {}, {}, {}
            step = [0]

            def select(e):
                b = e % 2
                for c in range(TC):
                    vts(S[:, b, 0, c, :], iota_slot[:], slot[:, c, e:e + 1], mask[:, c, e:e + 1],
                        ALU.is_equal, ALU.mult, turned.get(e - 2), link=(e == 0 and c == 0))
                for c in range(TC):
                    built[e] = vts(S[:, b, 1, c, :], S[:, b, 0, c, :], gate[:, c, e:e + 1], None, ALU.mult,
                                   link=(c == 0))

            def dispatch(e):
                b = e % 2
                for f in range(DC):
                    for c in range(TC):
                        t = mm(PS[:, 6 + f // 3, (f % 3) * WIDE:(f % 3 + 1) * WIDE],
                               rows_tok[:, c, f * P:(f + 1) * P], S[:, b, 0, c, :], c == 0, c == TC - 1,
                               built[e], *drained.get(e - 2, ()))
                sent[e] = [vcopy(xd[:, b, 0:3, :].rearrange("p k t -> p (k t)"), PS[:, 6, 0:HALF], t, link=False),
                           acopy(xd[:, b, 3:6, :].rearrange("p k t -> p (k t)"), PS[:, 7, 0:HALF], t)]

            def turn(e):
                b, bank = e % 2, 4 + step[0] % 2
                for c in range(TC):
                    t = tr(PS[:, bank, c * P:(c + 1) * P], S[:, b, 1, c, :], gu_free.get(step[0] - 2))
                turned[e] = t
                turned_sb[e] = gu_free[step[0]] = acopy(cbT[:, b, :], PS[:, bank, 0:T], t)
                step[0] += 1

            def combine(e):
                b = e % 2
                for c in range(TC):
                    for hf in range(2):
                        mm(PS[:, 2 * c + hf, 0:HALF], cbT[:, b, c * P:(c + 1) * P],
                           out[:, b, hf * HALF:(hf + 1) * HALF], e == 0, False, turned_sb[e], *drained[e])

            select(0)
            dispatch(0)
            turn(0)
            for e in range(NEXP):
                b = e % 2
                if e + 1 < NEXP:
                    select(e + 1)
                (gs, gt_, gw), (us, ut, uw) = load_up(e)
                gw, uw = w3(gw, DC, hc_n * P), w3(uw, DC, hc_n * P)
                ready = []
                for o in range(hc_n):
                    n = step[0]
                    bank = 4 + n % 2
                    for w, tok, col in ((gw, gt_, 0), (uw, ut, WIDE)):
                        for k in range(DC):
                            t = mm(PS[:, bank, col:col + WIDE], w[:, k, o * P:(o + 1) * P], xd[:, b, k, :], k == 0,
                                   k == DC - 1, tok, gu_free.get(n - 2), *sent[e])
                    a = act(silu[:, n % 2, :], PS[:, bank, 0:WIDE], ACT.Silu, t)
                    gu_free[n] = vtt(h[:, b, o, :], PS[:, bank, WIDE:2 * WIDE], silu[:, n % 2, :], ALU.mult, a,
                                     link=False)
                    ready.append(gu_free[n])
                    step[0] += 1
                    if o == 0 and e > 0:
                        combine(e - 1)
                release(gs, t)
                release(us, t)
                if e + 1 < NEXP:
                    dispatch(e + 1)
                    turn(e + 1)
                ds, dt, (dw,) = load_down(e)
                dw = w3(dw, hc_n, D)
                for o in range(hc_n):
                    for hf in range(2):
                        t = mm(PS[:, 6 + hf, 0:HALF], h[:, b, o, :], dw[:, o, hf * HALF:(hf + 1) * HALF], o == 0,
                               o == hc_n - 1, dt, ready[o], *sent.get(e + 1, ()))
                release(ds, t)
                drained[e] = [vcopy(out[:, b, 0:HALF], PS[:, 6, 0:HALF], t, link=False),
                              acopy(out[:, b, HALF:D], PS[:, 7, 0:HALF], t)]
            combine(NEXP - 1)
            pr.phase()

        def overflow_branch(xT_, mask, gate, slot, gate_src, up_src, down_src, hc_n, B, name):
            nonlocal pr
            pr.phase()
            flag, over = B["flag"], B["over"]
            vts(over[:], slot[:], float(WIDE), None, ALU.is_ge)
            vtt(over[:], over[:], mask, ALU.mult)
            worst = stat[:, 52:53]
            vred(worst, over[:].rearrange("p c e -> p (c e)"), ALU.max)
            v = vtt(over[:], over[:], gate, ALU.mult)
            t = tr(PS[0:1, 4, 0:P], worst, v)
            vred(stat[0:1, 53:54], PS[0:1, 4, 0:P], ALU.max, t)
            known = vcopy(flag[:], stat[0:1, 53:54])
            pr.phase()

            main, pr = pr, Prog()
            for e in ("pe", "act", "dve", "pool"):
                pr.pending[e] = main.here()
            over_all, h2, piece = B["over_all"], B["over_h"], B["piece"]
            rows_to_all(over_all, over, NEXP, B["over_row"])
            free = main.here()
            for e in range(NEXP):
                for o in range(hc_n):
                    w = [piece[:, i, :].rearrange("p (k n) -> p k n", k=DC) for i in range(2)]
                    for i, src in enumerate((gate_src, up_src)):
                        load_small(w[i], src[e].rearrange("p (k n) -> p k n", k=DC)[:, :, o * P:(o + 1) * P],
                                   name, *free)
                    t = load_small(piece[:, 2, :], down_src[e][:, o * D:(o + 1) * D], name, *free)
                    pr.pending["pe"].append(t)
                    for i in range(2):
                        for k in range(DC):
                            t = mm(PS[:, 4, i * T:(i + 1) * T], w[i][:, k, :], xT_[:, k, :], k == 0, k == DC - 1,
                                   pr.last["dve"])
                    a = act(h2[:, 0, :], PS[:, 4, 0:T], ACT.Silu, t)
                    v = vtt(h2[:, 1, :], PS[:, 4, T:2 * T], h2[:, 0, :], ALU.mult, a)
                    v = vtt(h2[:, 1, :], h2[:, 1, :], over_all[:, e, :], ALU.mult)
                    for c in range(TC):
                        for hf in range(2):
                            t = mm(PS[:, 2 * c + hf, 0:HALF], h2[:, 1, c * P:(c + 1) * P],
                                   piece[:, 2, hf * HALF:(hf + 1) * HALF], e == 0 and o == 0,
                                   e == NEXP - 1 and o == hc_n - 1, v)
                    free = [t]
            residual_add()
            pr.join()
            sub, pr = pr, main
            subs.append(sub)
            pr.branch(flag[0:1, 0:1], sub, known)

        def edge_attention(nh, rels, counts, a_src, a_dst, values, width, E, ET, maskb, rcp, eps):
            S = rels * T
            pr.phase()
            vts(maskb, counts, 0.0, NEG, ALU.is_equal, ALU.mult)
            m = stat[:, 16:16 + TC * nh].rearrange("p (c h) -> p c h", c=TC)
            spread = {}
            step = 0
            for h in range(nh):
                for r in range(rels):
                    b = 4 + step % 4
                    t = mm(PS[:, b, 0:T], selrow[0:nh, h, :], a_src[0:nh, r * T:(r + 1) * T], True, True,
                           spread.get(step - 4))
                    for c in range(TC):
                        o = E[:, c, h * S + r * T:h * S + (r + 1) * T]
                        if step % 2:
                            spread[step] = vts(o, PS[:, b, 0:T], a_dst(c, h, r), None, ALU.add, None, t,
                                               link=False)
                        else:
                            spread[step] = act(o, PS[:, b, 0:T], ACT.Identity, t, bias=a_dst(c, h, r))
                    step += 1
            pr.phase()
            exped = {}
            for c in range(TC):
                Ec = E[:, c, 0:nh * S]
                E3 = Ec.rearrange("p (h s) -> p h s", h=nh)
                sh = [P, nh, S]
                stt(Ec, Ec, 0.2, Ec, ALU.mult, ALU.max)
                vtt(E3, E3, bc(maskb[:, c, :].unsqueeze(1), sh), ALU.add)
                vred(m[:, c, :], E3, ALU.max)
                t = vts(m[:, c, :], m[:, c, :], -1.0, None, ALU.mult)
                exped[c] = []
                for h in range(nh):
                    exped[c].append(act(E3[:, h, :], E3[:, h, :], ACT.Exp, t, bias=m[:, c, h:h + 1]))
            for c in range(TC):
                for h in range(nh):
                    Eh = E[:, c, h * S:(h + 1) * S]
                    pr.op("dve", lambda e, c=c, h=h, Eh=Eh: e.scalar_tensor_tensor(
                        out=Eh, in0=Eh, scalar=1.0, in1=counts[:, c, :], op0=ALU.mult, op1=ALU.mult,
                        accum_out=rcp[:, c, h:h + 1]), exped[c][h])
            pr.pending["dve"].append(pr.last["dve"])
            if eps:
                vts(rcp, rcp, eps, None, ALU.add)
            else:
                vts(rcp, rcp, 1e-30, None, ALU.max)
            vrec(rcp, rcp)
            pr.phase()
            n_src = S // P
            per_bank = min(n_src, 2)
            banks, et_free, copied = {}, {}, {}
            step = [0]

            def turn(h):
                et = ET[:, h % 2, 0:n_src, :]
                copied[h] = []
                for g in range(n_src // per_bank):
                    n = step[0]
                    b = 4 + n % 4
                    for j in range(per_bank):
                        for c in range(TC):
                            jj = g * per_bank + j
                            t = tr(PS[:, b, j * T + c * P:j * T + c * P + P],
                                   E[:, c, h * S + jj * P:h * S + (jj + 1) * P], banks.get(n - 4))
                    banks[n] = (acopy if n % 2 else vcopy)(
                        et[:, g * per_bank:(g + 1) * per_bank, :].rearrange("p a t -> p (a t)"),
                        PS[:, b, :], t, et_free.get(h - 2))
                    copied[h].append(banks[n])
                    step[0] += 1

            def weigh(h):
                et = ET[:, h % 2, 0:n_src, :]
                for c in range(TC):
                    for n0 in range(0, width, HALF):
                        n1 = min(width, n0 + HALF)
                        col = h * width + n0
                        o = PS[:, 2 * c + col // HALF, col % HALF:col % HALF + n1 - n0]
                        for j in range(n_src):
                            t = mm(o, et[:, j, c * P:(c + 1) * P], values(j)[:, col:col + n1 - n0],
                                   j == 0, j == n_src - 1, *copied[h])
                et_free[h] = t

            turn(0)
            for h in range(nh):
                if h + 1 < nh:
                    turn(h + 1)
                weigh(h)
            pr.phase()

        def attention(qT, kT, v, yT, Pm, PT, causal):
            scale = 1.0 / math.sqrt(HD)
            mx = stat[:, 8:8 + HEADS * TC].rearrange("p (h c) -> p h c", h=HEADS)
            sm = stat[:, 32:32 + HEADS * TC].rearrange("p (h c) -> p h c", h=HEADS)
            pr.phase()
            free = {}
            for h in range(HEADS):
                f, p0 = h // 2, HD * (h % 2)
                b = h % 4
                for c in range(TC):
                    t = mm(PS[:, b, c * T:(c + 1) * T], qT[p0:p0 + HD, f, c * P:(c + 1) * P],
                           kT[p0:p0 + HD, f, :], True, True, free.get(h - 4))
                s3 = PS[:, b, :].rearrange("p (c t) -> p c t", c=TC)
                if causal is not None:
                    stt(Pm[:, h, :, :], s3, scale, causal, ALU.mult, ALU.add, t)
                    src, sc = Pm[:, h, :, :], 1.0
                else:
                    src, sc = s3, scale
                vred(mx[:, h, :], src, ALU.max, t)
                t = vts(mx[:, h, :], mx[:, h, :], -sc, None, ALU.mult)
                for c in range(TC):
                    free[h] = act(Pm[:, h, c, :], src[:, c, :], ACT.Exp, t, bias=mx[:, h, c:c + 1], scale=sc,
                                  accum=sm[:, h, c:c + 1])
            pr.phase()
            inv = vrec(sm, sm)
            free, yfree, pt_free, turned = {}, {}, {}, {}
            scaled = [vtt(Pm[:, h, :, :], Pm[:, h, :, :], bc(sm[:, h, :].unsqueeze(2), [P, TC, T]), ALU.mult, inv,
                          link=False, eng="pool" if h % 3 == 2 else "dve") for h in range(HEADS)]

            def turn(h):
                b = h % 4
                for k in range(TC):
                    for c in range(TC):
                        t = tr(PS[:, b, k * T + c * P:k * T + c * P + P], Pm[:, h, c, k * P:(k + 1) * P],
                               scaled[h], free.get(h - 4))
                free[h] = turned[h] = acopy(PT[:, h % 3, :], PS[:, b, :], t, pt_free.get(h - 3))

            def weigh(h):
                f, p0 = h // 2, HD * (h % 2)
                for k in range(TC):
                    t = mm(PS[p0:p0 + HD, 4 + f % 4, 0:T], v[:, k, h * HD:(h + 1) * HD],
                           PT[:, h % 3, k * T:(k + 1) * T], k == 0, k == TC - 1, turned[h], yfree.get(f - 4))
                pt_free[h] = t
                if h % 2:
                    yfree[f] = acopy(yT[:, f, :], PS[:, 4 + f % 4, 0:T], t)

            for h in range(HEADS + 2):
                if h < HEADS:
                    turn(h)
                if h >= 2:
                    weigh(h - 2)
            pr.phase()

        def dispatched_experts(rows_tok, S, probs, run_experts, xdT, S2, cbT, o2):
            pr.phase()
            NS = NEXP * SLOT
            for f in range(DC):
                b = f % 4
                for c in range(TC):
                    t = mm(PS[:, b, :], rows_tok[:, c, f * P:(f + 1) * P], S[:, c, :], c == 0, c == TC - 1,
                           fr[f - 4] if f >= 4 else None)
                cp = (acopy if f % 2 else vcopy)(xdT[:, f, :], PS[:, b, :], t)
                if f == 0:
                    fr = {}
                fr[f] = cp
            for c in range(TC):
                for e in range(NEXP):
                    for z in range(2):
                        vts(S2[:, c, e, z, :], S[:, c, e * SLOT:(e + 1) * SLOT], probs[:, c, e:e + 1], None,
                            ALU.mult, link=False, eng="pool" if z else "dve")
            pr.phase()
            copied = {}
            for e in range(NEXP):
                b = 4 + (e // 2) % 4
                for c in range(TC):
                    t = tr(PS[:, b, (e % 2) * T + c * P:(e % 2) * T + c * P + P],
                           S2[:, c, e, :, :].rearrange("p z s -> p (z s)"))
                if e % 2:
                    (acopy if e % 4 == 3 else vcopy)(cbT[:, e - 1:e + 1, :].rearrange("p a t -> p (a t)"),
                                                     PS[:, b, :], t)
            pr.phase()
            run_experts(lambda e: xdT[:, :, e * SLOT:(e + 1) * SLOT], o2)
            pr.phase()
            for e in range(NEXP):
                for c in range(TC):
                    for h in range(2):
                        z = slice(SLOT * h, SLOT * (h + 1))
                        mm(PS[:, 2 * c + h, 0:HALF], cbT[z, e, c * P:(c + 1) * P], o2[z, e, :],
                           e == 0, e == NEXP - 1)
            pr.phase()

        def drain_expert(o2_, e, bank, t):
            vcopy(o2_[0:SLOT, e, :], PS[0:SLOT, bank, 0:HALF], t, link=False)
            return vcopy(o2_[SLOT:P, e, :], PS[SLOT:P, bank + 1, 0:HALF], link=False)

        def build_graph(side_work=()):
            spare = xT[:].rearrange("p k t -> p (k t)")
            ohs = xn_tok[:].rearrange("p c n -> p (c n)").bitcast(BF16)[:, 0:3 * NREL * T] \
                .rearrange("p (b n) -> p b n", b=3)
            iota, at = spare[:, 0:NREL * T], NREL * T
            ohd = spare[:, at:at + 3 * T // 2].bitcast(BF16).rearrange("p (b n) -> p b n", b=3)
            at += 3 * T // 2
            idx = spare[:, at:at + 3 * EC].bitcast(I32).rearrange("p (i k) -> p i k", i=3)
            at += 3 * EC
            idf = spare[:, at:at + 3 * EC].rearrange("p (i k) -> p i k", i=3)
            at += 3 * EC
            rs = spare[:, at:at + EC]
            load_small(iota, dram["c_iota"], "edges")
            for i, n in enumerate(("src", "dst", "edge_type_3")):
                t = load_small(idx[:, i, :], dram[n], "edges")
            yield
            vcopy(idf, idx, t)
            stt(rs, idf[:, 2, :], float(T), idf[:, 0, :], ALU.mult, ALU.add)
            done = {}
            for k in range(EC):
                b = k % 3
                v1 = vts(ohs[:, b, :], iota, rs[:, k:k + 1], None, ALU.is_equal, None,
                         done.get(k - 3), link=(k == 0))
                v2 = vts(ohd[:, b, :], iota[:, 0:T], idf[:, 1, k:k + 1], None, ALU.is_equal, None,
                         link=False)
                for c in range(TC):
                    for h in range(2):
                        t = mm(PS[:, 2 * c + h, 0:HALF], ohd[:, b, c * P:(c + 1) * P],
                               ohs[:, b, h * HALF:(h + 1) * HALF], k == 0, k == EC - 1, v1, v2)
                done[k] = t
                if k % 4 == 3 and side_work:
                    side_work.pop(0)()
            vcopy(A_ds[:].rearrange("p c r s -> p (c r s)").rearrange("p (b n) -> p b n", n=HALF),
                  acc_tok, t)
            pr.phase()
            yield

        def stage_graph():
            for _ in build_graph():
                pass

        def residual_add():
            pr.phase()
            vtt(as_tok(x_tok[:]), acc_tok, as_tok(x_tok[:]), ALU.add)
            pr.phase()

        def stage_L0_gnn():
            with ExitStack() as st:
                A_sd = sb("A_sd", [P, NREL, TC, T], F32, st)
                hT = xT
                qiT = sb("gate_qiT", [P, DC, T], F32, st)
                G = sb("gate_rows", [96, 3, QB, D], BF16, st)
                selg = sb("gate_sel", [96, QN * QL], BF16, st)
                qT = sb("gate_qT", [P, DC, QB * QL], F32, st)
                brow = sb("gate_bg_row", [1, D], F32, st)
                bcol = sb("gate_bias_cols", [P, 3, DC], F32, st)
                work = sb("gate_work", [P, 2, QN * QL], F32, st)
                flat = work[:].rearrange("p a n -> p (a n)")
                aggT = flat[:, 0:DC * T].rearrange("p (k t) -> p k t", k=DC)
                part = [w_.bitcast(BF16).rearrange("p (c n) -> p c n", n=D) for w_ in
                        (flat[:, 0:2 * D], flat[:, 2 * D:4 * D], qiT[:].rearrange("p k t -> p (k t)"))]
                rest = flat[:, 4 * D:5 * D].rearrange("p (b n) -> p b n", b=2)
                side = []
                graph = build_graph(side)
                next(graph)
                wgq_slot, wgq_tok, (wgq,) = load(dram["L0_gnn_Wg"][1])
                wq3 = w3(wgq, DC, D)
                t_q = load_small(qT[:], dram["L0_gnn_query_T"], "gate")
                for i, n in enumerate(("L0_gnn_b1", "L0_gnn_b2", "L0_gnn_bq")):
                    load_small(bcol[:, i, :], dram[n], "gate")
                t_q = load_small(brow[:], dram["L0_gnn_bg"], "gate")

                sel_f = A_sd[0:96, :, :, :].rearrange("p r k t -> p (r k t)")
                for h in range(2):
                    n = QN * QL // 2
                    t = load_small(sel_f[:, 0:n], dram["c_selg"][:, h * n:(h + 1) * n], "selg",
                                   pr.last["dve"] if h else None)
                    vcopy(selg[:, h * n:(h + 1) * n], sel_f[:, 0:n], t)

                rest_free, splits = {}, [0]

                def split_bank(bank, c, h, *waits):
                    n = splits[0]
                    splits[0] += 1
                    col = slice(h * HALF, (h + 1) * HALF)
                    r_ = rest[:, n % 2, :]
                    a = acopy(part[0][:, c, col], PS[:, bank, 0:HALF], *waits)
                    v = vtt(r_, PS[:, bank, 0:HALF], part[0][:, c, col], ALU.subtract, a,
                            rest_free.get(n - 2), link=False)
                    a = acopy(part[1][:, c, col], r_, v)
                    rest_free[n] = vtt(part[2][:, c, col], r_, part[1][:, c, col], ALU.subtract, a, link=False)
                    return v, rest_free[n]

                n_groups = 2 * QB * QL // P
                q_free, q_split, product_done = {}, [], {}

                def query_rows(n):
                    c, h = n // 2, n % 2
                    b = 4 + n % 4
                    o = PS[:, b, 0:HALF]
                    mm(o, ones[0:1, :], brow[0:1, h * HALF:(h + 1) * HALF], True, False, t_q, q_free.get(n - 4))
                    for k in range(DC):
                        t = mm(o, qT[:, k, c * P:(c + 1) * P], wq3[:, k, h * HALF:(h + 1) * HALF], False,
                               k == DC - 1, wgq_tok)
                    if n == 7:
                        release(wgq_slot, t)
                    product_done[n] = t

                def query_split(n):
                    q_free[n], last = split_bank(4 + n % 4, n // 2, n % 2, product_done[n])
                    q_split.append(last)

                def query_step(n):
                    if n < n_groups:
                        query_rows(n)
                    if n >= 1:
                        query_split(n - 1)

                side += [lambda n=n: query_step(n) for n in range(n_groups + 1)]
                next(graph)
                while side:
                    side.pop(0)()
                for i in range(3):
                    for z in range(2):
                        dst = G[QN:QN + QL, i, :, :].rearrange("p (c z) n -> p z c n", z=2)[:, z, :, :]
                        moved = load_small(dst, part[i][QL * z:QL * (z + 1), :, :], "grow", q_split[-1],
                                           eng="act")
                pr.phase()
                turned = []
                for r in range(NREL):
                    for k in range(TC):
                        for c in range(TC):
                            t = tr(PS[:, r, k * T + c * P:k * T + c * P + P], A_ds[:, c, r, k * P:(k + 1) * P])
                    turned.append(vcopy(A_sd[:, r, :, :].rearrange("p k t -> p (k t)"), PS[:, r, :], t))
                for r in range(NREL):
                    for k in range(TC):
                        t = mm(PS[:, 3 + r, 0:T], ones[:], A_sd[:, r, k, :], k == 0, k == TC - 1, turned[r])
                    cnt = rest[:].rearrange("p b n -> p (b n)")[:, r * T:(r + 1) * T]
                    vts(cnt, PS[:, 3 + r, 0:T], 1.0, None, ALU.max, None, t)
                    vrec(cnt, cnt)
                    vtt(A_sd[:, r, :, :], PS[:, r, :].rearrange("p (k t) -> p k t", k=TC),
                        bc(cnt.unsqueeze(1), [P, TC, T]), ALU.mult)
                pr.phase()

                def gate():
                    nonlocal moved
                    pr.phase()
                    t = project_tok([load(dram["L0_gnn_Wg"][0])], [hT])
                    for c in range(TC):
                        for h in range(2):
                            _, v = split_bank(2 * c + h, c, h, t)
                    for i in range(3):
                        for z in range(4):
                            dst = G[0:QN, i, :, :].rearrange("p (c z) n -> p z c n", z=4)[:, z, :, :]
                            moved = load_small(dst, part[i][QN * z:QN * (z + 1), 0:TC, :], "grow", v,
                                               eng="act")
                    pr.phase()
                    nodes = xn_tok[:].rearrange("p c n -> p (c n)").rearrange("p (k t) -> p k t", k=DC)
                    wqh_slot, wqh_tok, (wqh,) = load(dram["L0_gnn_Wq"][0])
                    wqh = w3(wqh, DC, D)
                    slot_free, work_free, side_free = {}, {}, {}
                    step = 0
                    for b in range(QB):
                        for f in range(DC):
                            it = b * DC + f
                            w = work[:, it % 2, :]
                            for q in range(2):
                                pb = 2 * (step % 3)
                                for i in range(3):
                                    for k in range(2):
                                        col = (2 * q + k) * 512
                                        t = mm(PS[:, pb + k, :], G[0:96, i, b, f * P:(f + 1) * P],
                                               selg[:, col:col + 512], i == 0, i == 2, moved,
                                               slot_free.get(step - 3))
                                a = act(PS[:, pb:pb + 2, :], PS[:, pb:pb + 2, :], ACT.Sigmoid, t)
                                n16 = QN // 2
                                s4 = PS[:, pb:pb + 2, :].rearrange("p a (n l) -> p (a n) l", l=QL)
                                q4 = bc(qT[:, f, b * QL:(b + 1) * QL].unsqueeze(1), [P, n16, QL])
                                w4 = w[:, q * 1024:(q + 1) * 1024].rearrange("p (n l) -> p n l", l=QL)
                                slot_free[step] = vtt(w4, s4, q4, ALU.mult, a, work_free.get(it - 2),
                                                      link=False)
                                step += 1
                            w3_ = w.rearrange("p (n l) -> p n l", l=QL)
                            width = QL // 2
                            folded = vtt(w3_[:, :, 0:width], w3_[:, :, 0:width], w3_[:, :, width:QL],
                                         ALU.add, slot_free[step - 1], eng="pool", link=False)
                            if it % 2:
                                width //= 2
                                folded = vtt(w3_[:, :, 0:width], w3_[:, :, 0:width],
                                             w3_[:, :, width:2 * width], ALU.add, folded, eng="pool",
                                             link=False)
                            waiting.append((it, b, f, w3_[:, :, 0:width], folded))
                            if it > 0:
                                finish_sum(waiting.pop(0), work_free)
                            if it % 7 == 3 and it // 7 < DC:
                                o = it // 7
                                for k in range(DC):
                                    t = mm(PS[:, 6 + o % 2, 0:T], wqh[:, k, o * P:(o + 1) * P], hT[:, k, :],
                                           k == 0, k == DC - 1, wqh_tok, side_free.get(o - 2))
                                side_free[o] = acopy(nodes[:, o, :], PS[:, 6 + o % 2, 0:T], t)
                    release(wqh_slot, t)
                    finish_sum(waiting.pop(0), work_free)
                    pr.phase()
                    t = project_T([load(dram["L0_gnn_Wq"][1])], [qiT])
                    alpha = work[:, 0, 0:DC * T].rearrange("p (k t) -> p k t", k=DC)
                    th = work[:, 1, 0:DC * T].rearrange("p (k t) -> p k t", k=DC)
                    a = act(th, qiT[:], ACT.Tanh)
                    vtt(th, th, hT[:], ALU.subtract, a)
                    v = vtt(nodes, acc_T, nodes, ALU.add, t)
                    for o in range(DC):
                        a = act(alpha[:, o, :], nodes[:, o, :], ACT.Sigmoid, v, bias=bcol[:, 2, o:o + 1])
                    vtt(th, th, alpha, ALU.mult, a)
                    vtt(hT[:], hT[:], th, ALU.add)
                    pr.phase()

                waiting = []

                def finish_sum(item, work_free):
                    it, b, f, w3_, folded = item
                    work_free[it] = vred(qiT[:, f, b * QN:(b + 1) * QN], w3_, ALU.add, folded,
                                         link=False)

                def rgcn(h_tok, h_T, layer, root, b):
                    pr.phase()
                    units, movers = [load(dram[root])], [h_T]
                    s, tok, (w,) = units[0]
                    w = w3(w, DC, D)
                    for o in range(DC):
                        for k in range(DC):
                            t = mm(PS[:, o, 0:T], w[:, k, o * P:(o + 1) * P], h_T[:, k, :], k == 0, False, tok)
                    release(s, t)
                    agg_free, bank_free = None, {}
                    step = 0
                    for r in range(NREL):
                        s, tok, (w,) = load(dram[layer][r])
                        w = w3(w, DC, D)
                        for f in range(DC):
                            bk = 6 + step % 2
                            for k in range(TC):
                                t = mm(PS[:, bk, 0:T], h_tok[:, k, f * P:(f + 1) * P], A_sd[:, r, k, :], k == 0,
                                       k == TC - 1, bank_free.get(step - 2))
                            bank_free[step] = cp = vcopy(aggT[:, f, :], PS[:, bk, 0:T], t, agg_free, link=False)
                            step += 1
                        for o in range(DC):
                            for k in range(DC):
                                t = mm(PS[:, o, 0:T], w[:, k, o * P:(o + 1) * P], aggT[:, k, :], False,
                                       r == NREL - 1 and k == DC - 1, tok, cp)
                        release(s, t)
                        agg_free = t
                    for o in range(DC):
                        act(hT[:, o, :], PS[:, o, 0:T], ACT.Relu, t, bias=bcol[:, b, o:o + 1])
                    pr.phase()

                pr.phase()
                pr.pending["act"].append(moved)
                pr.pending["dve"].append(moved)
                norm(xn_tok, x_tok, 1e-5)
                tok_to_T(xT, xn_tok)
                rgcn(xn_tok, xT, "L0_gnn_W_rel1", "L0_gnn_W_root1", 0)
                gate()
                T_to_tok(xn_tok, hT)
                rgcn(xn_tok, xT, "L0_gnn_W_rel2", "L0_gnn_W_root2", 1)
                gate()
                T_to_tok(xn_tok, hT)
                vtt(x_tok[:], x_tok[:], xn_tok[:], ALU.add)
                pr.phase()

        def stage_L0_ffn():
            with ExitStack() as st:
                rw = sb("router_w", [P, DC, NEXP + 1], F32, st)
                sgb = sb("sg_b", [P, 1], F32, st)
                gt = sb("gates_tok", [P, TC, 16], F32, st)
                sc = [sb(f"route{i}", [P, TC, NEXP], F32, st) for i in range(5)]
                slot = sb("slots", [P, TC, NEXP], F32, st)
                B = routed_buffers(st, "r0")
                alphas = sb("alpha_all", [P, 1, T], F32, st)
                grow = sb("gates_row", [16, T], F32, st)
                hT = [sb("shared_h", [P, DC // 2, T], F32, st)]
                tmp = sb("silu", [P, 4, T], F32, st)
                load_small(rw[:], dram["L0_ffn_router_sg_w"], "l0f", *pr.here())
                t = load_small(sgb[:], dram["L0_ffn_sg_b"], "l0f")
                norm(xn_tok, x_tok, 1e-5)
                tok_to_T(xT, xn_tok)
                pr.pending["pe"].append(t)
                pr.pending["act"].append(t)
                lg = small_logits(4, xT, rw, NEXP + 1)
                pr.phase()
                alpha = gt[:, :, NEXP:NEXP + 1]
                for c in range(TC):
                    act(gt[:, c, NEXP:NEXP + 1], PS[:, 4, c * 16 + NEXP:c * 16 + NEXP + 1], ACT.Sigmoid,
                        bias=sgb[:, 0:1])
                pr.phase()
                probs, oh1, oh2, tm, s2 = (s[:] for s in sc)
                softmax8(probs, lg[:, :, 0:NEXP])
                v1, v2, z = stat[:, 44:46], stat[:, 46:48], stat[:, 48:50]
                top2(oh1, oh2, probs, v1, v2, tm, s2)
                vtt(z, v1, v2, ALU.add)
                vrec(z, z)
                vts(s2[:, :, 0:1], alpha, -1.0, 1.0, ALU.mult, ALU.add)
                vtt(z.unsqueeze(2), z.unsqueeze(2), s2[:, :, 0:1], ALU.mult)
                vtt(oh1, oh1, oh2, ALU.add)
                vtt(tm, oh1, probs, ALU.mult)
                gate = gt[:, :, 0:NEXP]
                vtt(gate, tm, bc(z.unsqueeze(2), [P, TC, NEXP]), ALU.mult)
                slots_of(slot[:], oh1)
                rows_to_all(alphas, gt[:, :, NEXP:NEXP + 1], 1, grow)

                def up(e):
                    a, b = load(dram["L0_ffn_w_gate"][e]), load(dram["L0_ffn_w_up"][e])
                    return (a[0], a[1], a[2][0]), (b[0], b[1], b[2][0])

                def shared_up():
                    s, t_, (g, u) = load(dram["L0_ffn_ws_gate"], dram["L0_ffn_ws_up"])
                    return (s, t_, g), (s, t_, u)
                routed_experts(xn_tok, oh1, gate, slot, up, lambda e: load(dram["L0_ffn_w_down"][e]), DC, B)
                glu_experts(xT, alphas, [(shared_up, lambda: load(dram["L0_ffn_ws_down"]), DC // 2, 0)], hT, tmp,
                            opens=False)
                residual_add()
                overflow_branch(xT, oh1, gate, slot, dram["L0_ffn_w_gate"], dram["L0_ffn_w_up"],
                                dram["L0_ffn_w_down"], DC, B, "over_l0")

        def stage_L1_gnn():
            with ExitStack() as st:
                bd = sb("gat_blockdiag", [P, 2 * P], F32, st)
                ab = sb("gat_attn", [P, 2, D], F32, st)
                ft = sb("gat_ft", [P, TC, D], F32, st)
                res = sb("gat_res", [P, TC, D], F32, st)
                a12 = sb("gat_a", [P, TC, 2, HEADS], F32, st)
                arow = sb("gat_arow", [HEADS, T], F32, st)
                cnt = sb("gat_counts", [P, TC, T], F32, st)
                maskb = sb("gat_mask", [P, TC, T], F32, st)
                rcp = sb("gat_rcp", [P, TC, HEADS], F32, st)
                E = sb("gat_E", [P, TC, HEADS * T], F32, st)
                ET = sb("gat_ET", [P, 2, TC, T], F32, st)
                z = pr.op("dve", lambda e: e.memset(bd[:], 0.0), link=True)
                for i, n in enumerate(("L1_gnn_W_fc", "L1_gnn_W_res")):
                    for k in range(2):
                        load_small(bd[HD * k:HD * (k + 1), P * i + HD * k:P * i + HD * (k + 1)], dram[n],
                                   "gat", z)
                for i, n in enumerate(("L1_gnn_attn_l", "L1_gnn_attn_r")):
                    t = load_small(ab[:, i, :], dram[n].partition_broadcast(P), "gat", z)
                norm(xn_tok, x_tok, 1e-5)
                tok_to_T(xT, xn_tok)
                pr.pending["pe"].append(t)
                pr.pending["dve"].append(t)
                for c in range(TC):
                    for f in range(DC):
                        t = mm(PS[:, 3 * c + f // 2, (f % 2) * T:(f % 2 + 1) * T],
                               xT[:, f, c * P:(c + 1) * P], bd[:], True, True)
                pr.phase()
                for c in range(TC):
                    o4 = PS[:, 3 * c:3 * c + 3, :].rearrange("p b (f w) -> p (b f) w", f=2)
                    cp = acopy if c else vcopy
                    cp(ft[:, c, :].rearrange("p (f n) -> p f n", f=DC), o4[:, :, 0:P])
                    cp(res[:, c, :].rearrange("p (f n) -> p f n", f=DC), o4[:, :, P:2 * P])
                pr.phase()
                for c in range(TC):
                    for i in range(2):
                        pv = E[:, c, 0:D]
                        vtt(pv, ft[:, c, :], ab[:, i, :], ALU.mult)
                        vred(a12[:, c, i, :], pv.rearrange("p (h e) -> p h e", h=HEADS), ALU.add)
                vtt(cnt[:], A_ds[:, :, 0, :], A_ds[:, :, 1, :], ALU.add)
                vtt(cnt[:], cnt[:], A_ds[:, :, 2, :], ALU.add)
                pr.phase()
                for c in range(TC):
                    t = tr(PS[0:HEADS, 6, c * P:(c + 1) * P], a12[:, c, 0, :])
                vcopy(arow[:], PS[0:HEADS, 6, 0:T], t)
                edge_attention(HEADS, 1, cnt[:], arow[:], lambda c, h, r: a12[:, c, 1, h:h + 1],
                               lambda j: ft[:, j, :], HD, E[:], ET[:], maskb[:], rcp[:], 0.0)
                for c in range(TC):
                    for g in range(2):
                        o3 = PS[:, 2 * c + g, 0:HALF].rearrange("p (h e) -> p h e", e=HD)
                        f3 = ft[:, c, g * HALF:(g + 1) * HALF].rearrange("p (h e) -> p h e", e=HD)
                        vtt(f3, o3, bc(rcp[:, c, 6 * g:6 * g + 6].unsqueeze(2), [P, 6, HD]), ALU.mult)
                vtt(ft[:], ft[:], res[:], ALU.add)
                stt(x_tok[:], ft[:], 0.0, x_tok[:], ALU.max, ALU.add)
                pr.phase()

        def store_slots(S, mask, slot):
            for c in range(TC):
                for e in range(NEXP):
                    vts(S[:, c, e * SLOT:(e + 1) * SLOT], iota_slot[:, 0:SLOT],
                        slot[:, c, e:e + 1],
                        mask[:, c, e:e + 1], ALU.is_equal, ALU.mult, link=(c == 0 and e == 0))

        def stage_L1_ffn():
            with ExitStack() as st0:
                wln = sb("ln_w", [P, 2, D], F32, st0)
                y_tok = sb("y_tok", [P, TC, D], F32, st0)
                load_small(wln[:, 0, :], dram["L1_ffn_ln1_w"].partition_broadcast(P), "l1f", *pr.here())
                t = load_small(wln[:, 1, :], dram["L1_ffn_ln2_w"].partition_broadcast(P), "l1f")
                with ExitStack() as st:
                    causal = sb("causal", [P, TC, T], F32, st)
                    qT = sb("att_qT", [P, DC, T], F32, st)
                    kT = sb("att_kT", [P, DC, T], F32, st)
                    v = sb("att_v", [P, TC, D], F32, st)
                    Pm = sb("att_P", [P, HEADS, TC, T], F32, st)
                    PT = sb("att_PT", [P, 3, 2 * T], F32, st)
                    t = load_small(causal[:], dram["c_causal"], "l1f", *pr.here())
                    norm(y_tok, x_tok, 1e-5)
                    pr.pending["dve"].append(t)
                    norm(xn_tok, y_tok, 1e-5, weight=wln[:, 0, :])
                    tok_to_T(xT, xn_tok)
                    qkv(qT, kT, v, [dram["L1_ffn_c_attn_w"][i] for i in range(3)])
                    attention(qT, kT, v, xT, Pm, PT, causal[:])
                    project_tok([load(dram["L1_ffn_c_proj_w"])], [xT])
                    pr.phase()
                    vtt(as_tok(y_tok[:]), acc_tok, as_tok(y_tok[:]), ALU.add)
                    pr.phase()
                with ExitStack() as st:
                    wg = sb("moe_wg", [P, DC, NEXP], F32, st)
                    sc = [sb(f"moe_r{i}", [P, TC, NEXP], F32, st) for i in range(6)]
                    S = sb("moe_S", [P, TC, NEXP * SLOT], F32, st)
                    xdT = sb("moe_xdT", [P, DC, NEXP * SLOT], F32, st)
                    S2 = sb("moe_S2", [P, TC, NEXP, 2, SLOT], F32, st)
                    cbT = sb("moe_cbT", [P, NEXP, T], F32, st)
                    o2 = sb("moe_out", [P, NEXP, HALF], F32, st)
                    hT = sb("moe_h", [P, 8, DC * SLOT], F32, st)
                    t = load_small(wg[:], dram["L1_ffn_w_g"], "l1f", *pr.here())
                    norm(xn_tok, y_tok, 1e-5, weight=wln[:, 1, :])
                    tok_to_T(xT, xn_tok)
                    pr.pending["pe"].append(t)
                    lg = small_logits(4, xT, wg, NEXP)
                    pr.phase()
                    logits, oh1, oh2, tm, s2, probs = (s[:] for s in sc)
                    vcopy(logits, lg)
                    v1, v2, z = stat[:, 44:46], stat[:, 46:48], stat[:, 48:50]
                    top2(oh1, oh2, logits, v1, v2, tm, s2)
                    vtt(oh1, oh1, oh2, ALU.add)
                    vtt(probs, logits, bc(v1.unsqueeze(2), [P, TC, NEXP]), ALU.subtract)
                    pr.phase()
                    act(probs, probs, ACT.Exp)
                    pr.phase()
                    vtt(probs, probs, oh1, ALU.mult)
                    vred(z, probs, ALU.add)
                    vrec(z, z)
                    vtt(probs, probs, bc(z.unsqueeze(2), [P, TC, NEXP]), ALU.mult)
                    for c in range(TC):
                        for k in range(TC):
                            mm(PS[:, 5, c * 16:c * 16 + NEXP], before[:, k, c * P:(c + 1) * P], oh1[:, k, :],
                               k == 0, k == TC - 1, pr.last["dve"])
                    pr.phase()
                    vcopy(s2, PS[:, 5, 0:32].rearrange("p (c n) -> p c n", c=TC)[:, :, 0:NEXP])
                    store_slots(S, oh1, s2)

                    hid = 4
                    buffers = 2 * hid
                    gelu, used, drained = {}, {}, {}

                    def up_unit(e, u, xd):
                        s, tok, (w,) = load(dram["L1_ffn_c_fc"][e, u])
                        w = w3(w, DC, D)
                        n = hid * e + u
                        b = 4 + n % 4
                        for o in range(DC):
                            for k in range(DC):
                                t = mm(PS[:, b, o * SLOT:(o + 1) * SLOT], w[:, k, o * P:(o + 1) * P],
                                       xd[:, k, :], k == 0, k == DC - 1, tok, gelu.get(n - 4))
                        release(s, t)
                        gelu[n] = act(hT[:, n % buffers, :], PS[:, b, 0:DC * SLOT], ACT.Gelu, t,
                                      used.get(n - buffers))

                    def down_unit(e, u, o2_):
                        s, tok, (w,) = load(dram["L1_ffn_c_proj_e"][e, u])
                        w = w3(w, DC, D)
                        n = hid * e + u
                        pair = 2 * (e % 2)
                        for k in range(DC):
                            for h in range(2):
                                t = mm(PS[SLOT * h:SLOT * (h + 1), pair + h, 0:HALF],
                                       hT[:, n % buffers, k * SLOT:(k + 1) * SLOT],
                                       w[:, k, h * HALF:(h + 1) * HALF], u == 0 and k == 0,
                                       u == hid - 1 and k == DC - 1, tok, gelu[n], drained.get(e - 2))
                        release(s, t)
                        used[n] = t
                        if u == hid - 1:
                            drained[e] = drain_expert(o2_, e, pair, t)

                    def run_experts(xd, o2_):
                        for e in range(NEXP + 1):
                            for u in range(hid):
                                if e < NEXP:
                                    up_unit(e, u, xd(e))
                                if e > 0:
                                    down_unit(e - 1, u, o2_)

                    dispatched_experts(xn_tok, S, probs, run_experts, xdT, S2, cbT, o2)
                    vtt(as_tok(x_tok[:]), acc_tok, as_tok(x_tok[:]), ALU.add)
                    vtt(x_tok[:], x_tok[:], y_tok[:], ALU.add)
                    pr.phase()

        def qkv(qT, kT, v, units):
            for dst, u in ((qT, units[0]), (kT, units[1])):
                pr.phase()
                project_T([load(u)], [xT])
                pr.phase()
                vcopy(dst[:, 0:3, :], acc_T[:, 0:3, :])
                acopy(dst[:, 3:6, :], acc_T[:, 3:6, :])
            pr.phase()
            project_tok([load(units[2])], [xT])
            pr.phase()
            vcopy(as_tok(v[:])[:, 0:2, :], acc_tok[:, 0:2, :])
            acopy(as_tok(v[:])[:, 2:4, :], acc_tok[:, 2:4, :])
            pr.phase()

        def stage_L2_gnn():
            with ExitStack() as st:
                xr = sb("rgat_xr", [P, NREL, TC, D], F32, st)
                qk = sb("rgat_qk", [P, DC, 2 * RH], F32, st)
                qk2 = sb("rgat_qk2", [P, DC, 2], F32, st)
                bias = sb("rgat_bias", [P, 2, D], F32, st)
                kj = sb("rgat_kj", [RH, NREL * T], F32, st)
                qi = sb("rgat_qi", [P, NREL, TC, RH], F32, st)
                rcp = sb("rgat_rcp", [P, TC, RH], F32, st)
                maskb = sb("rgat_mask", [P, TC, NREL * T], F32, st)
                E = sb("rgat_E", [P, TC, RH * NREL * T], F32, st)
                ET = sb("rgat_ET", [P, 2, NREL * TC, T], F32, st)
                w = pr.here()
                load_small(qk[:], dram["L2_gnn_qk1"], "rgat", *w)
                load_small(qk2[:], dram["L2_gnn_qk2"], "rgat")
                load_small(bias[:, 0, :], dram["L2_gnn_b1"].partition_broadcast(P), "rgat")
                t = load_small(bias[:, 1, :], dram["L2_gnn_b2"].partition_broadcast(P), "rgat")
                norm(xn_tok, x_tok, 1e-5)
                pr.pending["pe"].append(t)
                pr.pending["dve"].append(t)

                def layer(weights, qkw, nh, brow, finish):
                    tok_to_T(xT, xn_tok)
                    xrT = E[:, 0, 0:DC * T].rearrange("p (k t) -> p k t", k=DC)
                    copied, turned, small = {}, {}, {}

                    def product(r):
                        pr.pending["pe"] += copied.get(r - 1, [])
                        t = project_tok([load(dram[weights][r])], [xT])
                        o, d = acc_tok, as_tok(xr[:, r, :, :])
                        copied[r] = [vcopy(d[:, 0:2, :], o[:, 0:2, :], t, link=False),
                                     acopy(d[:, 2:4, :], o[:, 2:4, :], t)]

                    def turn(r):
                        cps = []
                        for g in range(DC // 2):
                            for f in range(2):
                                for c in range(TC):
                                    t = tr(PS[:, 5 + g, f * T + c * P:f * T + c * P + P],
                                           xr[:, r, c, (2 * g + f) * P:(2 * g + f + 1) * P],
                                           *copied[r], small.get(r - 1))
                            d = xrT[:, 2 * g:2 * g + 2, :].rearrange("p a t -> p (a t)")
                            cps.append(acopy(d, PS[:, 5 + g, :], t) if g == 1 else
                                       vcopy(d, PS[:, 5 + g, :], t, link=False))
                        turned[r] = cps

                    def scores(r):
                        for k in range(DC):
                            t = mm(PS[0:nh, 4, 0:T], qkw[:, k, nh:2 * nh], xrT[:, k, :], k == 0, k == DC - 1,
                                   *turned[r])
                        vcopy(kj[0:nh, r * T:(r + 1) * T], PS[0:nh, 4, 0:T], t, link=False)
                        for c in range(TC):
                            for k in range(DC):
                                t = mm(PS[:, 5, c * 16:c * 16 + nh], xrT[:, k, c * P:(c + 1) * P],
                                       qkw[:, k, 0:nh], k == 0, k == DC - 1)
                        small[r] = vcopy(qi[:, r, :, 0:nh],
                                         PS[:, 5, 0:32].rearrange("p (c n) -> p c n", c=TC)[:, :, 0:nh], t,
                                         link=False)

                    product(0)
                    for r in range(NREL):
                        if r + 1 < NREL:
                            product(r + 1)
                        turn(r)
                        scores(r)
                    pr.phase()
                    edge_attention(nh, NREL, A_ds[:].rearrange("p c r s -> p c (r s)"), kj[:],
                                   lambda c, h, r: qi[:, r, c, h:h + 1],
                                   lambda j: xr[:, j // TC, j % TC, :], D // nh, E[:], ET[:], maskb[:],
                                   rcp[:, :, 0:nh], 1e-16)
                    for c in range(TC):
                        for g in range(2):
                            w_ = min(HALF, D // nh)
                            hn = HALF // w_
                            o3 = PS[:, 2 * c + g, 0:HALF].rearrange("p (h e) -> p h e", e=w_)
                            d3 = xn_tok[:, c, g * HALF:(g + 1) * HALF].rearrange("p (h e) -> p h e", e=w_)
                            rc = rcp[:, c, hn * g:hn * (g + 1)] if nh > 1 else rcp[:, c, 0:1]
                            vtt(d3, o3, bc(rc.unsqueeze(2), [P, hn, w_]), ALU.mult)
                    vtt(xn_tok[:], xn_tok[:], bc(brow.unsqueeze(1), [P, TC, D]), ALU.add)
                    finish()

                def elu():
                    ev = E[:, 0, 0:TC * D].rearrange("p (c n) -> p c n", c=TC)
                    t = vts(ev, xn_tok[:], 0.0, None, ALU.min)
                    t = act(ev, ev, ACT.Exp, t)
                    vts(ev, ev, -1.0, None, ALU.add, None, t)
                    stt(xn_tok[:], xn_tok[:], 0.0, ev, ALU.max, ALU.add)
                    pr.phase()

                def add_residual():
                    vtt(x_tok[:], x_tok[:], xn_tok[:], ALU.add)
                    pr.phase()

                layer("L2_gnn_W1", qk, RH, bias[:, 0, :], elu)
                layer("L2_gnn_W2", qk2, 1, bias[:, 1, :], add_residual)

        def stage_L2_ffn():
            with ExitStack() as st:
                sw = sb("sw_w", [P, DC, NEXP], F32, st)
                swb = sb("sw_b", [P, NEXP], F32, st)
                sc = [sb(f"sw_r{i}", [P, TC, NEXP], F32, st) for i in range(4)]
                pr2 = sb("sw_pair", [P, TC, 2], F32, st)
                prow = sb("sw_prow", [2, T], F32, st)
                pall = sb("sw_pall", [P, 2, T], F32, st)
                cmpb = sb("sw_cmp", [P, 3, T], F32, st)
                S = sb("sw_S", [P, TC, NEXP * SLOT], F32, st)
                xdT = sb("sw_xdT", [P, DC, NEXP * SLOT], F32, st)
                S2 = sb("sw_S2", [P, TC, NEXP, 2, SLOT], F32, st)
                cbT = sb("sw_cbT", [P, NEXP, T], F32, st)
                o2 = sb("sw_out", [P, NEXP, HALF], F32, st)
                hT = sb("sw_h", [P, 2, 3 * SLOT], F32, st)
                b1 = sb("sw_b1", [NEXP, HALF], F32, st)
                b2 = sb("sw_b2", [NEXP, D], F32, st)
                earlier = sb("earlier", [P, TC, T], F32, st)
                w = pr.here()
                load_small(sw[:], dram["L2_ffn_switch_w"], "sw", *w)
                load_small(swb[:], dram["L2_ffn_switch_b"].partition_broadcast(P), "sw")
                load_small(earlier[:], dram["c_earlier"], "sw")
                load_small(b1[:], dram["L2_ffn_b1"], "sw")
                t = load_small(b2[:], dram["L2_ffn_b2"], "sw")
                norm(xn_tok, x_tok, 1e-5)
                tok_to_T(xT, xn_tok)
                pr.pending["pe"].append(t)
                pr.pending["dve"].append(t)
                lg = small_logits(4, xT, sw, NEXP)
                pr.phase()
                probs, oh, tm, slot = (s[:] for s in sc)
                vtt(slot, lg, bc(swb[:].unsqueeze(1), [P, TC, NEXP]), ALU.add)
                softmax8(probs, slot)
                pmax = stat[:, 44:46]
                first_max(oh, probs, pmax, tm)
                vcopy(pr2[:, :, 0], pmax)
                vtt(tm, oh, bc(desc[:].unsqueeze(1), [P, TC, NEXP]), ALU.mult)
                vred(pr2[:, :, 1], tm, ALU.max)
                rows_to_all(pall, pr2, 2, prow)
                rank, keep = stat[:, 46:48], stat[:, 48:50]
                for c in range(TC):
                    p1, r1 = pr2[:, c, 0:1], pr2[:, c, 1:2]
                    vts(cmpb[:, 0, :], pall[:, 0, :], p1, None, ALU.is_gt)
                    vts(cmpb[:, 1, :], pall[:, 0, :], p1, None, ALU.is_equal)
                    vtt(cmpb[:, 1, :], cmpb[:, 1, :], earlier[:, c, :], ALU.mult)
                    vtt(cmpb[:, 0, :], cmpb[:, 0, :], cmpb[:, 1, :], ALU.add)
                    vts(cmpb[:, 1, :], pall[:, 1, :], r1, None, ALU.is_equal)
                    vtt(cmpb[:, 0, :], cmpb[:, 0, :], cmpb[:, 1, :], ALU.mult)
                    vred(rank[:, c:c + 1], cmpb[:, 0, :], ALU.add)
                vts(keep, rank, float(CAP2), None, ALU.is_lt)
                vtt(oh, oh, bc(keep.unsqueeze(2), [P, TC, NEXP]), ALU.mult)
                vcopy(slot, bc(rank.unsqueeze(2), [P, TC, NEXP]))
                store_slots(S, oh, slot)

                free = {}

                def expert(e, xd, o2_):
                    s, tok, (wa, wb) = load(dram["L2_ffn_w1"][e], dram["L2_ffn_w2"][e])
                    wa, wb = w3(wa, DC, HALF), w3(wb, 3, D)
                    b = 4 + e % 4
                    for o in range(3):
                        d = PS[:, b, o * SLOT:(o + 1) * SLOT]
                        mm(d, b1[:, o * P:(o + 1) * P], selrow[0:NEXP, e, 0:SLOT], True, False,
                           free.get(("ps", e - 4)))
                        for k in range(DC):
                            t = mm(d, wa[:, k, o * P:(o + 1) * P], xd[:, k, :], False, k == DC - 1, tok)
                    a = act(hT[:, e % 2, :], PS[:, b, 0:3 * SLOT], ACT.Gelu, t, free.get(("h", e - 2)))
                    free["ps", e] = a
                    pair = 2 * (e % 2)
                    for h in range(2):
                        mm(PS[SLOT * h:SLOT * (h + 1), pair + h, 0:HALF], selrow[0:NEXP, e, 0:SLOT],
                           b2[:, h * HALF:(h + 1) * HALF], True, False, free.get(("o", e - 2)))
                    for k in range(3):
                        for h in range(2):
                            t = mm(PS[SLOT * h:SLOT * (h + 1), pair + h, 0:HALF],
                                   hT[:, e % 2, k * SLOT:(k + 1) * SLOT], wb[:, k, h * HALF:(h + 1) * HALF],
                                   False, k == 2, a)
                    release(s, t)
                    free["h", e] = t
                    free["o", e] = drain_expert(o2_, e, pair, t)

                def run_experts(xd, o2_):
                    for e in range(NEXP):
                        expert(e, xd(e), o2_)

                dispatched_experts(xn_tok, S, probs, run_experts, xdT, S2, cbT, o2)
                vtt(as_tok(x_tok[:]), acc_tok, as_tok(x_tok[:]), ALU.add)
                drop = stat[:, 50:52]
                vts(drop, keep, -1.0, 1.0, ALU.mult, ALU.add)
                vtt(drop, drop, pmax, ALU.mult)
                for c in range(TC):
                    stt(x_tok[:, c, :], xn_tok[:, c, :], drop[:, c:c + 1], x_tok[:, c, :], ALU.mult, ALU.add)
                pr.phase()

        def stage_L3_gnn():
            with ExitStack() as st:
                A3 = sb("gcn_A_ds", [P, TC, T], F32, st)
                A3s = sb("gcn_A_sd", [P, TC, T], F32, st)
                eye = sb("gcn_eye", [P, TC, T], F32, st)
                b = sb("gcn_b", [P, D], F32, st)
                xs = sb("gcn_xs", [P, TC, D], F32, st)
                aggT = sb("gcn_aggT", [P, DC, T], F32, st)
                w = pr.here()
                load_small(eye[:], dram["c_eye"], "gcn", *w)
                t = load_small(b[:], dram["L3_gnn_b"].partition_broadcast(P), "gcn")
                deg, dinv = stat[:, 30:32], stat[:, 32:34]
                norm(xn_tok, x_tok, 1e-5)
                pr.pending["dve"].append(t)
                vtt(A3[:], A_ds[:, :, 0, :], A_ds[:, :, 1, :], ALU.add)
                vtt(A3[:], A3[:], A_ds[:, :, 2, :], ALU.add)
                vtt(A3[:], A3[:], eye[:], ALU.add)
                vred(deg, A3[:], ALU.add)
                pr.phase()
                t = pr.op("pool", lambda e: e.tensor_tensor(dinv, deg, stat[:, 62:64], ALU.pow))
                pr.pending["dve"].append(t)
                for c in range(TC):
                    vts(xs[:, c, :], xn_tok[:, c, :], dinv[:, c:c + 1], None, ALU.mult)
                for k in range(TC):
                    for c in range(TC):
                        t = tr(PS[:, 6, k * T + c * P:k * T + c * P + P], A3[:, c, k * P:(k + 1) * P])
                vcopy(A3s[:].rearrange("p k t -> p (k t)"), PS[:, 6, :], t)
                pr.phase()
                for f in range(DC):
                    for k in range(TC):
                        mm(PS[:, f, 0:T], xs[:, k, f * P:(f + 1) * P], A3s[:, k, :], k == 0, k == TC - 1)
                pr.phase()
                vcopy(aggT[:, 0:3, :], acc_T[:, 0:3, :])
                acopy(aggT[:, 3:6, :], acc_T[:, 3:6, :])
                pr.phase()
                project_tok([load(dram["L3_gnn_W"])], [aggT])
                pr.phase()
                for c in range(TC):
                    for h in range(2):
                        x2 = x_tok[:, c, h * HALF:(h + 1) * HALF]
                        stt(x2, PS[:, 2 * c + h, 0:HALF], dinv[:, c:c + 1], x2, ALU.mult, ALU.add)
                    vtt(x_tok[:, c, :], x_tok[:, c, :], b[:], ALU.add)
                pr.phase()

        def stage_L3_ffn():
            with ExitStack() as st0:
                nw = sb("rms_w", [P, 2, D], F32, st0)
                y_tok = sb("y3_tok", [P, TC, D], F32, st0)
                w = pr.here()
                load_small(nw[:, 0, :], dram["L3_ffn_norm1_w"].partition_broadcast(P), "l3f", *w)
                t = load_small(nw[:, 1, :], dram["L3_ffn_norm2_w"].partition_broadcast(P), "l3f")
                with ExitStack() as st:
                    qT = sb("at3_qT", [P, DC, T], F32, st)
                    kT = sb("at3_kT", [P, DC, T], F32, st)
                    v = sb("at3_v", [P, TC, D], F32, st)
                    Pm = sb("at3_P", [P, HEADS, TC, T], F32, st)
                    PT = sb("at3_PT", [P, 3, 2 * T], F32, st)
                    norm(y_tok, x_tok, 1e-5)
                    pr.pending["dve"].append(t)
                    norm(xn_tok, y_tok, 1e-6, center=False, weight=nw[:, 0, :])
                    tok_to_T(xT, xn_tok)
                    qkv(qT, kT, v, [dram["L3_ffn_Wq"], dram["L3_ffn_Wk"], dram["L3_ffn_Wv"]])
                    attention(qT, kT, v, xT, Pm, PT, None)
                    project_tok([load(dram["L3_ffn_Wo"])], [xT])
                    pr.phase()
                    vtt(as_tok(y_tok[:]), acc_tok, as_tok(y_tok[:]), ALU.add)
                    pr.phase()
                with ExitStack() as st:
                    gw = sb("g3_w", [P, DC, NEXP], F32, st)
                    gt = sb("g3_tok", [P, TC, 16], F32, st)
                    sc = [sb(f"g3_r{i}", [P, TC, NEXP], F32, st) for i in range(5)]
                    slot = sb("slots3", [P, TC, NEXP], F32, st)
                    B = routed_buffers(st, "r3")
                    hT = [sb("shared3_h", [P, DC, T], F32, st)]
                    tmp = sb("silu3", [P, 4, T], F32, st)
                    t = load_small(gw[:], dram["L3_ffn_gate_w"], "l3f", *pr.here())
                    norm(xn_tok, y_tok, 1e-6, center=False, weight=nw[:, 1, :])
                    tok_to_T(xT, xn_tok)
                    pr.pending["pe"].append(t)
                    lg = small_logits(4, xT, gw, NEXP)
                    pr.phase()
                    probs, oh1, oh2, tm, s2 = (s[:] for s in sc)
                    softmax8(probs, lg)
                    v1, v2, z = stat[:, 44:46], stat[:, 46:48], stat[:, 48:50]
                    top2(oh1, oh2, probs, v1, v2, tm, s2)
                    vtt(z, v1, v2, ALU.add)
                    vts(z, z, 1e-20, None, ALU.add)
                    vrec(z, z)
                    vtt(oh1, oh1, oh2, ALU.add)
                    vtt(tm, oh1, probs, ALU.mult)
                    gate = gt[:, :, 0:NEXP]
                    vtt(gate, tm, bc(z.unsqueeze(2), [P, TC, NEXP]), ALU.mult)
                    slots_of(slot[:], oh1)
                    vtt(x_tok[:], x_tok[:], y_tok[:], ALU.add)

                    def up(e):
                        s, t_, (g, u) = load(dram["L3_ffn_Weg"][e], dram["L3_ffn_Weu"][e])
                        return (s, t_, g), (s, t_, u)

                    def shared_up():
                        a, b = load(dram["L3_ffn_Wsg"]), load(dram["L3_ffn_Wsu"])
                        return (a[0], a[1], a[2][0]), (b[0], b[1], b[2][0])
                    routed_experts(xn_tok, oh1, gate, slot, up, lambda e: load(dram["L3_ffn_Wed"][e]), DC // 2, B)
                    glu_experts(xT, None, [(shared_up, lambda: load(dram["L3_ffn_Wsd"]), DC, None)], hT, tmp,
                                opens=False)
                    residual_add()
                    overflow_branch(xT, oh1, gate, slot, dram["L3_ffn_Weg"], dram["L3_ffn_Weu"],
                                    dram["L3_ffn_Wed"], DC // 2, B, "over_l3")

        table = {"graph": stage_graph, "L0_gnn": stage_L0_gnn, "L0_ffn": stage_L0_ffn, "L1_gnn": stage_L1_gnn,
                 "L1_ffn": stage_L1_ffn, "L2_gnn": stage_L2_gnn, "L2_ffn": stage_L2_ffn,
                 "L3_gnn": stage_L3_gnn, "L3_ffn": stage_L3_ffn}
        for s in stages:
            table[s]()

        stored = sem("stored")
        pr.dma(lambda e: e.dma_start(out_dram, x_tok[:]), stored, 16, *pr.here())
        pr.number(eng_sem)
        for n, sub in enumerate(subs):
            sub.number({e: sem(f"over{n}_done_{e}") for e in Prog.ENGINES})

        block = ctx.enter_context(nc.Block())

        @block.sync
        def _(e):
            pr.emit("sp", e)
            e.wait_ge(stored, 16)

        @block.tensor
        def _(e):
            pr.emit("pe", e)

        @block.scalar
        def _(e):
            pr.emit("act", e)

        @block.vector
        def _(e):
            pr.emit("dve", e)

        @block.gpsimd
        def _(e):
            pr.emit("pool", e)


STAGES = ["L0_gnn", "L0_ffn", "L1_gnn", "L1_ffn", "L2_gnn", "L2_ffn", "L3_gnn", "L3_ffn"]


def _constants():
    t = np.arange(T)
    part = t.reshape(TC, P).T
    sel = np.zeros((96, QN, QL), np.float32)
    for n in range(QN):
        sel[n, n, :] = 1.0
        sel[QN + np.arange(QL), n, np.arange(QL)] = 1.0
    selrow = np.zeros((HEADS, HEADS, P), np.float32)
    selrow[np.arange(HEADS), np.arange(HEADS), :] = 1.0
    return {
        "c_ident": np.eye(P, dtype=np.float32),
        "c_selrow": selrow,
        "c_desc": np.tile(np.arange(NEXP, 0, -1, dtype=np.float32), (P, 1)),
        "c_iota_slot": np.tile(np.arange(WIDE, dtype=np.float32), (P, 1)),
        "c_iota": np.tile(np.arange(NREL * T, dtype=np.float32), (P, 1)),
        "c_before": (part[:, :, None] < t).astype(np.float32),
        "c_earlier": (t < part[:, :, None]).astype(np.float32),
        "c_eye": (part[:, :, None] == t).astype(np.float32),
        "c_causal": np.where(t <= part[:, :, None], 0.0, NEG).astype(np.float32),
        "c_selg": sel.reshape(96, QN * QL),
    }


def _rows(w):
    w = np.asarray(w)
    *lead, k, n = w.shape
    w = w.reshape(*lead, k // P, P, n)
    w = np.moveaxis(w, -3, -2)
    return np.ascontiguousarray(w).reshape(*lead, P, k // P * n)


def _flip(w):
    return np.swapaxes(np.asarray(w), -1, -2)


def _cols(v):
    return np.ascontiguousarray(np.asarray(v).reshape(-1, P).T)


def _layout(i):
    a = {}
    a["x"] = np.ascontiguousarray(np.asarray(i["x"]).reshape(TC, P, D).transpose(1, 0, 2))
    for n in ("src", "dst", "edge_type_3"):
        a[n] = np.ascontiguousarray(np.asarray(i[n]).reshape(EC, P).T)
    q = np.asarray(i["L0_gnn_query_embs"]).reshape(QB * QL, D).T
    a["L0_gnn_query_T"] = _rows(q).reshape(P, DC, QB * QL)
    for n in ("L0_gnn_W_rel1", "L0_gnn_W_root1", "L0_gnn_W_rel2", "L0_gnn_W_root2", "L0_ffn_w_gate",
              "L0_ffn_w_up", "L0_ffn_w_down", "L0_ffn_ws_gate", "L0_ffn_ws_up", "L0_ffn_ws_down",
              "L2_gnn_W1", "L2_gnn_W2", "L2_ffn_w1", "L2_ffn_w2", "L3_gnn_W"):
        a[n] = _rows(i[n])
    for n in ("L0_gnn_Wg", "L0_gnn_Wq"):
        a[n] = _rows(_flip(i[n]).reshape(2, D, D))
    for n in ("L0_gnn_b1", "L0_gnn_b2", "L0_gnn_bq"):
        a[n] = _cols(i[n])
    a["L0_gnn_bg"] = np.asarray(i["L0_gnn_bg"]).reshape(1, D)
    a["L2_ffn_switch_w"] = _rows(i["L2_ffn_switch_w"]).reshape(P, DC, NEXP)
    for n, (u, v) in (("L0_ffn_router_sg_w", ("L0_ffn_router_w", "L0_ffn_sg_w")),
                      ("L2_gnn_qk1", ("L2_gnn_q1", "L2_gnn_k1")), ("L2_gnn_qk2", ("L2_gnn_q2", "L2_gnn_k2"))):
        side = np.concatenate([np.asarray(i[u]), np.asarray(i[v])], axis=1)
        a[n] = _rows(side).reshape(P, DC, side.shape[1])
    a["L0_ffn_sg_b"] = np.ascontiguousarray(np.broadcast_to(np.asarray(i["L0_ffn_sg_b"]).reshape(1, 1), (P, 1)))
    for n in ("L1_gnn_W_fc", "L1_gnn_W_res"):
        a[n] = np.ascontiguousarray(_flip(i[n]))
    for n in ("L1_gnn_attn_l", "L1_gnn_attn_r", "L1_ffn_ln1_w", "L1_ffn_ln2_w", "L2_gnn_b1", "L2_gnn_b2",
              "L2_ffn_switch_b", "L3_gnn_b", "L3_ffn_norm1_w", "L3_ffn_norm2_w"):
        a[n] = np.asarray(i[n]).reshape(-1)
    a["L1_ffn_c_attn_w"] = _rows(np.ascontiguousarray(
        _flip(i["L1_ffn_c_attn_w"]).reshape(D, 3, D).transpose(1, 0, 2)))
    a["L1_ffn_c_fc"] = _rows(np.ascontiguousarray(
        np.asarray(i["L1_ffn_c_fc"]).reshape(NEXP, D, 4, D).transpose(0, 2, 1, 3)))
    a["L1_ffn_c_proj_e"] = _rows(np.asarray(i["L1_ffn_c_proj_e"]).reshape(NEXP, 4, D, D))
    for n in ("L1_ffn_w_g", "L3_ffn_gate_w"):
        a[n] = _rows(_flip(i[n])).reshape(P, DC, NEXP)
    for n in ("L1_ffn_c_proj_w", "L3_ffn_Wq", "L3_ffn_Wk", "L3_ffn_Wv", "L3_ffn_Wo", "L3_ffn_Weg", "L3_ffn_Weu",
              "L3_ffn_Wed", "L3_ffn_Wsg", "L3_ffn_Wsu", "L3_ffn_Wsd"):
        a[n] = _rows(_flip(i[n]))
    for n in ("L2_ffn_b1", "L2_ffn_b2"):
        a[n] = np.asarray(i[n])
    return a


def kernel(**inputs):
    import concourse.bacc as bacc
    from concourse.bass_utils import run_bass_kernel_spmd

    nc = bacc.Bacc("TRN2", target_bir_lowering=False, num_devices=1)
    arrays = {f"in_{k}_dram": v for k, v in {**_layout(inputs), **_constants()}.items()}
    dram = {k[3:-5]: nc.dram_tensor(k, v.shape, mybir.dt.from_np(v.dtype), kind="ExternalInput").ap()
            for k, v in arrays.items()}
    out = nc.dram_tensor("out_dram", (P, TC, D), F32, kind="ExternalOutput").ap()
    build(nc, dram, out, STAGES)
    r = run_bass_kernel_spmd(nc, [arrays], core_ids=[0])
    got = r.results[0]["out_dram"]
    return np.ascontiguousarray(got.transpose(1, 0, 2)).reshape(T, D)
```
